# Optimizing a Trainium2 kernel written in Bass

```python
import numpy as np
import jax
import jax.numpy as jnp

def _softmax(x, axis=-1):
    return jax.nn.softmax(x, axis=axis)

def _gelu(x):
    return jax.nn.gelu(x, approximate=True)

def _silu(x):
    return jax.nn.silu(x)

def _sigmoid(x):
    return jax.nn.sigmoid(x)

def _layernorm(x, axis=-1, eps=1e-05):
    m = jnp.mean(x, axis=axis, keepdims=True)
    v = jnp.var(x, axis=axis, keepdims=True)
    return (x - m) / jnp.sqrt(v + eps)

def _scatter_add(tgt, idx, src, axis=0):
    return tgt.at[idx].add(src)

def _segment_sum(src, seg, n):
    return jax.ops.segment_sum(src, seg, n)
kernel_name = 'mk_decoder_preln_d2_seqx_r4_b4a387'

def setup_inputs(seed: int=0):
    np.random.seed(seed)
    _w = jnp.asarray

    def _rec_inputs():
        import jax
        import jax.numpy as jnp
        _rk = jax.random.key(seed)
        x = 4.136e-05 + 0.9999 * jax.random.normal(jax.random.fold_in(_rk, 1), (2, 1024, 256), jnp.float32)
        _lenS = 1024 - jax.random.randint(jax.random.fold_in(_rk, 7), (2,), 0, max(1, 1024 // 4) + 1, jnp.int32)
        _lenS2 = 77 - jax.random.randint(jax.random.fold_in(_rk, 8), (2,), 0, max(1, 77 // 4) + 1, jnp.int32)
        _ctx_1024P = jax.random.normal(jax.random.fold_in(_rk, 11), (2, 16, 256), jnp.float32)
        _ctx_1024c = jax.random.dirichlet(jax.random.fold_in(_rk, 511), 0.3 * jnp.ones((16,), jnp.float32), (2, 77))
        _ctx_1024t = jnp.einsum('bsk,bkd->bsd', _ctx_1024c, _ctx_1024P)
        _ctx_1024t = _ctx_1024t * jax.lax.rsqrt(jnp.mean(jnp.square(_ctx_1024t)) + 1e-12) * 0.953939
        ctx_1024 = -0.000392918 + 0.999932 * (_ctx_1024t + 0.3 * jax.random.normal(jax.random.fold_in(_rk, 611), (2, 77, 256), jnp.float32))
        return (x, ctx_1024)
    x, ctx_1024 = _rec_inputs()

    def _L0_attn_setup():
        import jax, jax.numpy as jnp
        import numpy as np
        D_MODEL = 256
        N_HEADS = 16
        KV_HEADS = 4
        D_HEAD = D_MODEL // N_HEADS
        EPS = 1.1920929e-07

        def _rope_factor(n, d_head):
            i = jnp.arange(d_head)
            theta = jnp.power(10000.0, -2.0 * (i // 2).astype(jnp.float32) / d_head)
            pos = jnp.arange(n, dtype=jnp.float32)
            ang = pos[:, None] * theta[None, :]
            cos = jnp.cos(ang)
            sin = jnp.sin(ang) * jnp.where(jnp.arange(n) % 2 == 0, -1.0, 1.0)[:, None]
            return cos + sin
        key = jax.random.key(seed)
        ks = jax.random.split(key, 6)
        b, n = (2, 512)
        s = 1.0 / np.sqrt(D_MODEL)
        return {'x': jax.random.normal(ks[0], (b, n, D_MODEL), dtype=jnp.float32), 'w_q': jax.random.normal(ks[1], (D_MODEL, D_MODEL), dtype=jnp.float32) * s, 'w_k': jax.random.normal(ks[2], (D_MODEL, KV_HEADS * D_HEAD), dtype=jnp.float32) * s, 'w_v': jax.random.normal(ks[3], (D_MODEL, KV_HEADS * D_HEAD), dtype=jnp.float32) * s, 'w_o': jax.random.normal(ks[4], (D_MODEL, D_MODEL), dtype=jnp.float32) * s, 'norm_w': jnp.ones((D_MODEL,), dtype=jnp.float32)}
    _L0_attn_all = _L0_attn_setup()
    _L0_attn_in = {k: v for k, v in _L0_attn_all.items() if k in ('w_q', 'w_k', 'w_v', 'w_o', 'norm_w')}
    del _L0_attn_all

    def _L0_xattn_setup():
        import jax, jax.numpy as jnp
        import numpy as np
        P_SIZE = 100
        WINDOW_LENGTH = 2
        STAN_DEV = WINDOW_LENGTH / 2.0
        B, S, T = (4, 1024, 512)
        Q_SIZE = C_SIZE = 256
        key = jax.random.key(seed)
        k1, k2, k3, k4, k5 = jax.random.split(key, 5)
        q = jax.random.normal(k1, (B, S, Q_SIZE), dtype=jnp.float32)
        c_t = jax.random.normal(k2, (B, T, C_SIZE), dtype=jnp.float32)
        W_a = jax.random.normal(k3, (C_SIZE, Q_SIZE), dtype=jnp.float32) * 0.02
        W_p = jax.random.normal(k4, (P_SIZE, C_SIZE), dtype=jnp.float32) * 0.02
        V_p = jax.random.normal(k5, (1, P_SIZE), dtype=jnp.float32) * 0.02
        return {'q': q, 'c_t': c_t, 'W_a': W_a, 'W_p': W_p, 'V_p': V_p}
    _L0_xattn_all = _L0_xattn_setup()
    _L0_xattn_in = {k: v for k, v in _L0_xattn_all.items() if k in ('W_a', 'W_p', 'V_p')}
    del _L0_xattn_all

    def _L0_ffn_setup():
        import jax, jax.numpy as jnp
        import numpy as np
        B, S, H, F, E, K = (4, 512, 256, 896, 8, 2)
        CAP_FACTOR = 1.25

        def _moe_forward(hidden_states, gate_w, w1, w2, w3):
            b, s, h = hidden_states.shape
            dtype = hidden_states.dtype
            x = hidden_states.reshape(-1, h)
            router_logits = x @ gate_w.T
            expert_weights = jax.nn.softmax(router_logits.astype(jnp.float32), axis=1)
            _, selected_experts = jax.lax.top_k(expert_weights, K)
            top_k_idx = selected_experts.reshape(b, s, K)
            probs = expert_weights.reshape(b, s, E)
            capacity = int(s * K / E * CAP_FACTOR)
            expert_mask = jax.nn.one_hot(top_k_idx, E, dtype=jnp.int32)
            mask_fused = expert_mask.reshape(b, s * K, E)
            count_fused = jnp.cumsum(mask_fused, axis=1)
            count = count_fused.reshape(b, s, K, E)
            trunc_mask = expert_mask * (count <= capacity).astype(jnp.int32)
            combined_mask = trunc_mask.sum(axis=2)
            masked_probs = probs * combined_mask
            pos_fused = mask_fused * count_fused
            pos = pos_fused.reshape(b, s, K, E)
            combined_pos = pos.sum(axis=2) * combined_mask
            pos_in_cap = jax.nn.one_hot(combined_pos, capacity + 1, dtype=jnp.int32)
            combine_mask = masked_probs[..., None] * pos_in_cap
            combine_mask = combine_mask[..., 1:].astype(dtype)
            dispatch_mask = (combine_mask != 0).astype(dtype)
            dispatch = jnp.einsum('bsm,bsec->ebcm', hidden_states, dispatch_mask)
            h1 = jnp.einsum('ebcm,emh->ebch', dispatch, w1)
            h3 = jnp.einsum('ebcm,emh->ebch', dispatch, w3)
            expert_out = jnp.einsum('ebch,ehm->ebcm', jax.nn.silu(h1) * h3, w2)
            final = jnp.einsum('ebcm,bsec->bsm', expert_out, combine_mask)
            return final
        key = jax.random.key(seed)
        k1, k2, k3, k4, k5 = jax.random.split(key, 5)
        s_h = 1.0 / np.sqrt(H)
        s_f = 1.0 / np.sqrt(F)
        return {'hidden_states': jax.random.normal(k1, (B, S, H), dtype=jnp.float32), 'gate_w': jax.random.normal(k2, (E, H), dtype=jnp.float32) * s_h, 'w1': jax.random.normal(k3, (E, H, F), dtype=jnp.float32) * s_h, 'w2': jax.random.normal(k4, (E, F, H), dtype=jnp.float32) * s_f, 'w3': jax.random.normal(k5, (E, H, F), dtype=jnp.float32) * s_h}
    _L0_ffn_all = _L0_ffn_setup()
    _L0_ffn_in = {k: v for k, v in _L0_ffn_all.items() if k in ('gate_w', 'w1', 'w2', 'w3')}
    del _L0_ffn_all

    def _L1_attn_setup():
        import jax, jax.numpy as jnp
        import numpy as np
        B, S, D, H, R = (2, 512, 256, 16, 64)
        HD = D // H
        VOCAB = 2 * R + 1
        key = jax.random.key(seed)
        ks = jax.random.split(key, 7)
        s = 0.02
        return {'x': jax.random.normal(ks[0], (B, S, D), jnp.float32), 'W_qkv': jax.random.normal(ks[1], (D, 3 * D), jnp.float32) * s, 'b_qkv': jnp.zeros((3 * D,), jnp.float32), 'W_out': jax.random.normal(ks[2], (D, D), jnp.float32) * s, 'b_out': jnp.zeros((D,), jnp.float32), 'rel_emb_k': jax.random.normal(ks[3], (VOCAB, HD), jnp.float32) * s, 'rel_emb_v': jax.random.normal(ks[4], (VOCAB, HD), jnp.float32) * s}
    _L1_attn_all = _L1_attn_setup()
    _L1_attn_in = {k: v for k, v in _L1_attn_all.items() if k in ('W_qkv', 'b_qkv', 'W_out', 'b_out', 'rel_emb_k', 'rel_emb_v')}
    del _L1_attn_all

    def _L1_xattn_setup():
        import jax, jax.numpy as jnp
        import numpy as np
        DIM = 256
        key = jax.random.key(seed)
        k1, k2, k3, k4 = jax.random.split(key, 4)
        B, Nq, Nkv = (4, 512, 512)
        x = jax.random.normal(k1, (B, Nq, DIM), dtype=jnp.float32)
        y = jax.random.normal(k2, (B, Nkv, DIM), dtype=jnp.float32)
        Wq = jax.random.normal(k3, (DIM, DIM), dtype=jnp.float32) / np.sqrt(DIM)
        Wkv = jax.random.normal(k4, (DIM, 2 * DIM), dtype=jnp.float32) / np.sqrt(DIM)
        return {'x': x, 'y': y, 'Wq': Wq, 'Wkv': Wkv}
    _L1_xattn_all = _L1_xattn_setup()
    _L1_xattn_in = {k: v for k, v in _L1_xattn_all.items() if k in ('Wq', 'Wkv')}
    del _L1_xattn_all

    def _L1_ffn_setup():
        import jax, jax.numpy as jnp
        import numpy as np
        NUM_EXPERTS = 8
        HIDDEN = 256
        INTER = 256
        BATCH = 2
        SEQ = 256
        TOP_K = 2
        SWIGLU_ALPHA = 1.702
        LIMIT = 7.0

        def _grouped_mm(x, w, expert_ids):
            onehot = jax.nn.one_hot(expert_ids, w.shape[0], dtype=x.dtype)
            y_all = jnp.einsum('tk,ekn->etn', x, w)
            return jnp.einsum('te,etn->tn', onehot, y_all)

        def _gpt_oss_swiglu(x):
            gate = jnp.minimum(x[..., ::2], LIMIT)
            up = jnp.clip(x[..., 1::2], -LIMIT, LIMIT)
            glu = gate * jax.nn.sigmoid(gate * SWIGLU_ALPHA)
            return (up + 1.0) * glu
        key = jax.random.key(seed)
        ks = jax.random.split(key, 7)
        hidden_states = jax.random.normal(ks[0], (BATCH, SEQ, HIDDEN), jnp.float32)
        router_indices = jax.random.randint(ks[1], (BATCH * SEQ, TOP_K), 0, NUM_EXPERTS)
        routing_weights = jax.nn.softmax(jax.random.normal(ks[2], (BATCH * SEQ, NUM_EXPERTS), jnp.float32), axis=-1)
        scale = 0.02
        gate_up_proj = jax.random.normal(ks[3], (NUM_EXPERTS, HIDDEN, 2 * INTER), jnp.float32) * scale
        gate_up_proj_bias = jax.random.normal(ks[4], (NUM_EXPERTS, 2 * INTER), jnp.float32) * scale
        down_proj = jax.random.normal(ks[5], (NUM_EXPERTS, INTER, HIDDEN), jnp.float32) * scale
        down_proj_bias = jax.random.normal(ks[6], (NUM_EXPERTS, HIDDEN), jnp.float32) * scale
        return {'hidden_states': hidden_states, 'router_indices': router_indices, 'routing_weights': routing_weights, 'gate_up_proj': gate_up_proj, 'gate_up_proj_bias': gate_up_proj_bias, 'down_proj': down_proj, 'down_proj_bias': down_proj_bias}
    _L1_ffn_all = _L1_ffn_setup()
    _L1_ffn_in = {k: v for k, v in _L1_ffn_all.items() if k in ('router_indices', 'routing_weights', 'gate_up_proj', 'gate_up_proj_bias', 'down_proj', 'down_proj_bias')}
    del _L1_ffn_all
    return {'x': x, 'ctx_1024': ctx_1024, 'L0_attn_w_q': _L0_attn_in['w_q'], 'L0_attn_w_k': _L0_attn_in['w_k'], 'L0_attn_w_v': _L0_attn_in['w_v'], 'L0_attn_w_o': _L0_attn_in['w_o'], 'L0_attn_norm_w': _L0_attn_in['norm_w'], 'L0_xattn_W_a': _L0_xattn_in['W_a'], 'L0_xattn_W_p': _L0_xattn_in['W_p'], 'L0_xattn_V_p': _L0_xattn_in['V_p'], 'L0_ffn_gate_w': _L0_ffn_in['gate_w'], 'L0_ffn_w1': _L0_ffn_in['w1'], 'L0_ffn_w2': _L0_ffn_in['w2'], 'L0_ffn_w3': _L0_ffn_in['w3'], 'L1_attn_W_qkv': _L1_attn_in['W_qkv'], 'L1_attn_b_qkv': _L1_attn_in['b_qkv'], 'L1_attn_W_out': _L1_attn_in['W_out'], 'L1_attn_b_out': _L1_attn_in['b_out'], 'L1_attn_rel_emb_k': _L1_attn_in['rel_emb_k'], 'L1_attn_rel_emb_v': _L1_attn_in['rel_emb_v'], 'L1_xattn_Wq': _L1_xattn_in['Wq'], 'L1_xattn_Wkv': _L1_xattn_in['Wkv'], 'L1_ffn_router_indices': _L1_ffn_in['router_indices'], 'L1_ffn_routing_weights': _L1_ffn_in['routing_weights'], 'L1_ffn_gate_up_proj': _L1_ffn_in['gate_up_proj'], 'L1_ffn_gate_up_proj_bias': _L1_ffn_in['gate_up_proj_bias'], 'L1_ffn_down_proj': _L1_ffn_in['down_proj'], 'L1_ffn_down_proj_bias': _L1_ffn_in['down_proj_bias']}

def reference(x, ctx_1024, L0_attn_w_q, L0_attn_w_k, L0_attn_w_v, L0_attn_w_o, L0_attn_norm_w, L0_xattn_W_a, L0_xattn_W_p, L0_xattn_V_p, L0_ffn_gate_w, L0_ffn_w1, L0_ffn_w2, L0_ffn_w3, L1_attn_W_qkv, L1_attn_b_qkv, L1_attn_W_out, L1_attn_b_out, L1_attn_rel_emb_k, L1_attn_rel_emb_v, L1_xattn_Wq, L1_xattn_Wkv, L1_ffn_router_indices, L1_ffn_routing_weights, L1_ffn_gate_up_proj, L1_ffn_gate_up_proj_bias, L1_ffn_down_proj, L1_ffn_down_proj_bias):
    import jax
    import jax.numpy as jnp

    def _L0_attn_ref(x, w_q, w_k, w_v, w_o, norm_w):
        import jax, jax.numpy as jnp
        import numpy as np
        D_MODEL = 256
        N_HEADS = 16
        KV_HEADS = 4
        D_HEAD = D_MODEL // N_HEADS
        EPS = 1.1920929e-07

        def _rope_factor(n, d_head):
            i = jnp.arange(d_head)
            theta = jnp.power(10000.0, -2.0 * (i // 2).astype(jnp.float32) / d_head)
            pos = jnp.arange(n, dtype=jnp.float32)
            ang = pos[:, None] * theta[None, :]
            cos = jnp.cos(ang)
            sin = jnp.sin(ang) * jnp.where(jnp.arange(n) % 2 == 0, -1.0, 1.0)[:, None]
            return cos + sin
        b, n, d = x.shape
        reps = N_HEADS // KV_HEADS
        scale = jnp.float32(np.sqrt(D_HEAD))
        xn = x * jax.lax.rsqrt(jnp.mean(x * x, axis=-1, keepdims=True) + EPS) * norm_w
        q = (xn @ w_q).reshape(b, n, N_HEADS, D_HEAD).transpose(0, 2, 1, 3)
        k = (xn @ w_k).reshape(b, n, KV_HEADS, D_HEAD).transpose(0, 2, 1, 3)
        v = (xn @ w_v).reshape(b, n, KV_HEADS, D_HEAD).transpose(0, 2, 1, 3)
        rf = _rope_factor(n, D_HEAD)
        q = q * rf
        k = k * rf
        q5 = q.reshape(b, reps, KV_HEADS, n, D_HEAD)
        scores = jnp.einsum('brknd,bkmd->brknm', q5, k) / scale
        causal = jnp.tril(jnp.ones((n, n), dtype=bool))
        scores = jnp.where(causal, scores, jnp.float32(-jnp.inf))
        p = jax.nn.softmax(scores, axis=-1)
        s = jnp.einsum('brknm,bkmd->brknd', p, v)
        s = s.reshape(b, N_HEADS, n, D_HEAD).transpose(0, 2, 1, 3).reshape(b, n, d)
        return x + s @ w_o

    def _L0_xattn_ref(q, c_t, W_a, W_p, V_p):
        import jax, jax.numpy as jnp
        import numpy as np
        P_SIZE = 100
        WINDOW_LENGTH = 2
        STAN_DEV = WINDOW_LENGTH / 2.0
        B, S, T = (4, 1024, 512)
        Q_SIZE = C_SIZE = 256
        Bq, Sq, _ = q.shape
        hid = jnp.tanh(jnp.einsum('btc,pc->btp', c_t, W_p))
        p_t = Sq * jax.nn.sigmoid(jnp.einsum('btp,op->bto', hid, V_p))
        win_low = p_t.astype(jnp.int32) - WINDOW_LENGTH
        window = win_low + jnp.arange(2 * WINDOW_LENGTH, dtype=jnp.int32)
        window = jnp.clip(window, 0, Sq - 1)
        qw = jnp.take_along_axis(q[:, None, :, :], window[:, :, :, None], axis=2)
        scores = jnp.einsum('btwq,cq,btc->btw', qw, W_a, c_t)
        s_pos = window.astype(jnp.float32)
        gauss = jnp.exp(-jnp.square(s_pos - p_t) / (2.0 * STAN_DEV ** 2))
        a_t = jax.nn.softmax(scores, axis=-1) * gauss
        s_t = jnp.einsum('btw,btwq->btq', a_t, qw)
        return s_t

    def _L0_ffn_ref(hidden_states, gate_w, w1, w2, w3):
        import jax, jax.numpy as jnp
        import numpy as np
        B, S, H, F, E, K = (4, 512, 256, 896, 8, 2)
        CAP_FACTOR = 1.25

        def _moe_forward(hidden_states, gate_w, w1, w2, w3):
            b, s, h = hidden_states.shape
            dtype = hidden_states.dtype
            x = hidden_states.reshape(-1, h)
            router_logits = x @ gate_w.T
            expert_weights = jax.nn.softmax(router_logits.astype(jnp.float32), axis=1)
            _, selected_experts = jax.lax.top_k(expert_weights, K)
            top_k_idx = selected_experts.reshape(b, s, K)
            probs = expert_weights.reshape(b, s, E)
            capacity = int(s * K / E * CAP_FACTOR)
            expert_mask = jax.nn.one_hot(top_k_idx, E, dtype=jnp.int32)
            mask_fused = expert_mask.reshape(b, s * K, E)
            count_fused = jnp.cumsum(mask_fused, axis=1)
            count = count_fused.reshape(b, s, K, E)
            trunc_mask = expert_mask * (count <= capacity).astype(jnp.int32)
            combined_mask = trunc_mask.sum(axis=2)
            masked_probs = probs * combined_mask
            pos_fused = mask_fused * count_fused
            pos = pos_fused.reshape(b, s, K, E)
            combined_pos = pos.sum(axis=2) * combined_mask
            pos_in_cap = jax.nn.one_hot(combined_pos, capacity + 1, dtype=jnp.int32)
            combine_mask = masked_probs[..., None] * pos_in_cap
            combine_mask = combine_mask[..., 1:].astype(dtype)
            dispatch_mask = (combine_mask != 0).astype(dtype)
            dispatch = jnp.einsum('bsm,bsec->ebcm', hidden_states, dispatch_mask)
            h1 = jnp.einsum('ebcm,emh->ebch', dispatch, w1)
            h3 = jnp.einsum('ebcm,emh->ebch', dispatch, w3)
            expert_out = jnp.einsum('ebch,ehm->ebcm', jax.nn.silu(h1) * h3, w2)
            final = jnp.einsum('ebcm,bsec->bsm', expert_out, combine_mask)
            return final
        return _moe_forward(hidden_states, gate_w, w1, w2, w3)

    def _L1_attn_ref(x, W_qkv, b_qkv, W_out, b_out, rel_emb_k, rel_emb_v):
        import jax, jax.numpy as jnp
        import numpy as np
        B, S, D, H, R = (2, 512, 256, 16, 64)
        HD = D // H
        VOCAB = 2 * R + 1
        b, s, d = x.shape
        hd = d // H
        idx = jnp.arange(s)
        dist = jnp.clip(idx[None, :] - idx[:, None], -R, R) + R
        pe_k = rel_emb_k[dist]
        pe_v = rel_emb_v[dist]
        qkv = (x @ W_qkv + b_qkv).reshape(b, s, 3, H, hd)
        qkv = jnp.transpose(qkv, (2, 0, 3, 1, 4))
        q, k, v = (qkv[0], qkv[1], qkv[2])
        q = q / jnp.sqrt(jnp.asarray(hd, x.dtype))
        score = jnp.einsum('bhqd,bhkd->bhqk', q, k) + jnp.einsum('bhqd,qkd->bhqk', q, pe_k)
        attn = jax.nn.softmax(score, axis=-1)
        ctx = jnp.einsum('bhqk,bhkd->bhqd', attn, v) + jnp.einsum('bhqk,qkd->bhqd', attn, pe_v)
        ctx = jnp.transpose(ctx, (0, 2, 1, 3)).reshape(b, s, d)
        return ctx @ W_out + b_out

    def _L1_xattn_ref(x, y, Wq, Wkv):
        import jax, jax.numpy as jnp
        import numpy as np
        DIM = 256
        q = jnp.einsum('bnd,de->bne', x, Wq)
        kv = jnp.einsum('bnd,de->bne', y, Wkv)
        B, Nkv, _ = kv.shape
        kv = kv.reshape(B, Nkv, 2, DIM).transpose(2, 0, 1, 3)
        k, v = (kv[0], kv[1])
        scale = DIM ** (-0.5)
        attn = jnp.einsum('bqd,bkd->bqk', q * scale, k)
        attn = jax.nn.softmax(attn, axis=-1)
        out = jnp.einsum('bqk,bkd->bqd', attn, v)
        return out

    def _L1_ffn_ref(hidden_states, router_indices, routing_weights, gate_up_proj, gate_up_proj_bias, down_proj, down_proj_bias):
        import jax, jax.numpy as jnp
        import numpy as np
        NUM_EXPERTS = 8
        HIDDEN = 256
        INTER = 256
        BATCH = 2
        SEQ = 256
        TOP_K = 2
        SWIGLU_ALPHA = 1.702
        LIMIT = 7.0

        def _grouped_mm(x, w, expert_ids):
            onehot = jax.nn.one_hot(expert_ids, w.shape[0], dtype=x.dtype)
            y_all = jnp.einsum('tk,ekn->etn', x, w)
            return jnp.einsum('te,etn->tn', onehot, y_all)

        def _gpt_oss_swiglu(x):
            gate = jnp.minimum(x[..., ::2], LIMIT)
            up = jnp.clip(x[..., 1::2], -LIMIT, LIMIT)
            glu = gate * jax.nn.sigmoid(gate * SWIGLU_ALPHA)
            return (up + 1.0) * glu
        B = hidden_states.shape[0]
        H = hidden_states.shape[-1]
        x = hidden_states.reshape(-1, H)
        M = x.shape[0]
        top_k = router_indices.shape[1]
        num_experts = gate_up_proj.shape[0]
        topk_weights = jnp.take_along_axis(routing_weights, router_indices, axis=1)
        flat_experts = router_indices.reshape(-1)
        sort_idx = jnp.argsort(flat_experts)
        sorted_pos = sort_idx // top_k
        expert_sorted = flat_experts[sort_idx]
        grouped = x[sorted_pos]
        gate_up = _grouped_mm(grouped, gate_up_proj, expert_sorted)
        gate_up = gate_up + gate_up_proj_bias[expert_sorted]
        inter = _gpt_oss_swiglu(gate_up)
        down = _grouped_mm(inter, down_proj, expert_sorted)
        down = down + down_proj_bias[expert_sorted]
        down = down * topk_weights.reshape(-1)[sort_idx][:, None]
        out = jnp.zeros((M, H), x.dtype).at[sorted_pos].add(down)
        return out.reshape(B, -1, H)
    x = x + _L0_attn_ref(_layernorm(x, axis=-1), L0_attn_w_q, L0_attn_w_k, L0_attn_w_v, L0_attn_w_o, L0_attn_norm_w)
    x = x + _L0_xattn_ref(ctx_1024, _layernorm(x, axis=-1), L0_xattn_W_a, L0_xattn_W_p, L0_xattn_V_p)
    x = x + _L0_ffn_ref(_layernorm(x, axis=-1), L0_ffn_gate_w, L0_ffn_w1, L0_ffn_w2, L0_ffn_w3)
    x = x + _L1_attn_ref(_layernorm(x, axis=-1), L1_attn_W_qkv, L1_attn_b_qkv, L1_attn_W_out, L1_attn_b_out, L1_attn_rel_emb_k, L1_attn_rel_emb_v)
    x = x + _L1_xattn_ref(_layernorm(x, axis=-1), ctx_1024, L1_xattn_Wq, L1_xattn_Wkv)
    x = x + _L1_ffn_ref(_layernorm(x, axis=-1), L1_ffn_router_indices, L1_ffn_routing_weights, L1_ffn_gate_up_proj, L1_ffn_gate_up_proj_bias, L1_ffn_down_proj, L1_ffn_down_proj_bias)
    return x

_drawn_inputs = setup_inputs


def setup_inputs(seed=0):
    import zlib

    import numpy as np

    out = dict(_drawn_inputs(seed))
    spreads = {'L0_attn_norm_w': (1.0, 0.2), 'L1_attn_b_qkv': (0.0, 0.55), 'L1_attn_b_out': (0.0, 0.1)}
    factors = {'L1_attn_W_qkv': 7.64,
     'L1_attn_W_out': 3.603,
     'L1_attn_rel_emb_k': 8.0,
     'L1_attn_rel_emb_v': 8.0,
     'L1_ffn_routing_weights': 8.0,
     'L1_ffn_gate_up_proj': 8.0,
     'L1_ffn_gate_up_proj_bias': 8.0,
     'L1_ffn_down_proj': 8.0,
     'L1_ffn_down_proj_bias': 35.531}
    for name, (base, spread) in spreads.items():
        noise = np.random.default_rng([zlib.crc32(name.encode()), seed]).standard_normal(out[name].shape)
        drawn = base * np.exp(spread * noise) if base else spread * noise
        out[name] = jnp.asarray(drawn.astype(out[name].dtype))
    for name, factor in factors.items():
        out[name] = (out[name] * factor).astype(out[name].dtype)
    return out
```

```python
from contextlib import ExitStack

import concourse.bass as bass
from concourse import mybir

F32 = mybir.dt.float32
BF16 = mybir.dt.bfloat16
I32 = mybir.dt.int32
U32 = mybir.dt.uint32
ALU = mybir.AluOpType
ACT = mybir.ActivationFunctionType
AX = mybir.AxisListType

P = 128
B, S, D = 2, 1024, 256
N = B * S
NT = N // P
DC = D // P
H, HD = 16, 16
KVH = 4
REP = H // KVH
KB = S // P
Q0 = P // H
HG = 8
Q1 = P // HG
R = 64
NR = 2 * R + 1
SC = 77
PH = 100
WIN = 2
E = 8
F0 = 896
FC0 = F0 // P
CAP = int(S * 2 / E * 1.25)
F1 = 256
NF1 = 512
EXT = 520
LN_EPS = 1e-5
RMS_EPS = 1.1920929e-07
NEG = -1e30


class Consts:
    WIDTHS = dict(ident=P, causal=256, head0=D, sum0=Q0, hmask=HG, cmask=2 * Q1, head1=P,
                  diag1=Q1, sum1=Q1, tri=P, ones=P, iota8=E, iota77=SC, cap0=E, spare=1, rope=S)

    @classmethod
    def at(cls, name):
        c = 0
        for k, w in cls.WIDTHS.items():
            if k == name:
                return c, c + w
            c += w
        return c, c


CW = Consts.at("")[0]


class Chain:

    def __init__(self, eng, sem):
        self.eng, self.sem, self.n, self.off = eng, sem, 0, 0

    def __call__(self, ins):
        self.n += 1
        ins.then_inc(self.sem, 1)
        self.eng.wait_ge(self.sem, self.off + self.n)

    def enter(self, i, per, start=0):
        self.off = (i - start) * per
        self.n0, self.per = self.n, per

    def leave(self, count):
        assert self.n - self.n0 == self.per, (self.n - self.n0, self.per)
        self.off = 0
        self.n = self.n0 + self.per * count


class Prog:

    def __init__(self, nc, ctx, dram):
        self.nc, self.ctx, self.d = nc, ctx, dram
        self.x = self.sb("x", [P, NT, D])
        self.xT = self.sb("xT", [P, DC, N])
        self.cst = self.sb("cst", [P, CW])
        self.mean_var = self.sb("mean_var", [P, NT, 2])
        self.rstd = self.sb("rstd", [P, NT])
        self.rms = self.sb("rms", [P, NT])
        self.ps = ctx.enter_context(nc.psum_tensor("ps", [P, 8, 512], F32))
        self.ctxn = self.sb("ctxn", [SC, B, D])
        self.ctxT = self.sb("ctxT", [P, B, DC, SC])
        self.gT = self.sb("gT", [P, B, DC, SC])
        self.wpT = self.sb("wpT", [P, DC, PH])
        self.vp = self.sb("vp", [PH, 1])
        self.sems = []

    def sb(self, name, shape, dt=F32, ctx=None):
        return (ctx or self.ctx).enter_context(self.nc.sbuf_tensor(name, shape, dt))

    def sem(self, name):
        self.sems.append(self.nc.alloc_semaphore(name=name))
        return self.sems[-1]

    def end_stage(self):
        self.nc.clear_and_free_semaphores(self.sems)
        self.nc.all_engine_barrier()
        self.sems = []

    def c(self, name, rows=P):
        a, b = Consts.at(name)
        return self.cst[0:rows, a:b]


def load_inputs(k):
    nc = k.nc
    s_in = k.sem("s_in")
    with nc.Block() as block:
        @block.sync
        def _(sp):
            sp.dma_start(k.x[:, :, :], k.d["x"].rearrange("b (t p) d -> p (b t) d", p=P)).then_inc(s_in, 16)
            sp.dma_start(k.cst[:, :], k.d["consts"]).then_inc(s_in, 16)
            sp.wait_ge(s_in, 32)


def norm_transpose(k, tag, tiles=NT, attn0=False, natural=None):
    nc = k.nc
    x, xT, mv, ps = k.x, k.xT, k.mean_var, k.ps
    with ExitStack() as ctx:
        stats = k.sb(f"stats{tag}", [P, NT, 6], ctx=ctx)
        xs = k.sb(f"xs{tag}", [P, 2, D], ctx=ctx)
        xn = k.sb(f"xn{tag}", [P, 2, D], ctx=ctx)
        nw = k.sb(f"nw{tag}", [P, DC], ctx=ctx)
        s_chain = k.sem(f"s_nchain{tag}")
        s_w = k.sem(f"s_nw{tag}")
        s_var = k.sem(f"s_var{tag}")
        s_sd = k.sem(f"s_sd{tag}")
        s_xs = k.sem(f"s_xs{tag}")
        s_tr = k.sem(f"s_tr{tag}")
        s_xt = k.sem(f"s_xt{tag}")
        with nc.Block() as block:
            if attn0:
                @block.sync
                def _(sp):
                    sp.dma_start(nw[:, :], k.d["L0_attn_norm_w"].rearrange("(c p) -> p c", p=P),
                                 allow_slow_non_contiguous=True).then_inc(s_w, 16)

            @block.vector
            def _(dve):
                link = Chain(dve, s_chain)
                with dve.Fori(0, tiles) as t:
                    last = nc.vector.bn_stats(stats[:, bass.ds(t, 1), :], x[:, bass.ds(t, 1), :])
                    last.then_inc(s_chain, 1)
                link.n += tiles
                dve.wait_ge(s_chain, link.n)
                for t in range(tiles):
                    nc.vector.bn_aggr(mv[:, t, :], stats[:, t, :]).then_inc(s_chain, 1)
                link.n += tiles
                dve.wait_ge(s_chain, link.n)
                nc.vector.tensor_scalar(k.rstd[:, 0:tiles], mv[:, 0:tiles, 1], LN_EPS, None, ALU.add).then_inc(s_var, 1)
                dve.wait_ge(s_sd, 1)
                link(nc.vector.reciprocal(k.rstd[:, 0:tiles], k.rstd[:, 0:tiles]))
                if attn0:
                    link(nc.vector.tensor_tensor(k.rms[:, :], k.rstd[:, :], k.rstd[:, :], ALU.mult))
                    link(nc.vector.tensor_tensor(k.rms[:, :], k.rms[:, :], mv[:, :, 1], ALU.mult))
                    nc.vector.tensor_scalar(k.rms[:, :], k.rms[:, :], RMS_EPS, None, ALU.add).then_inc(s_var, 1)
                    dve.wait_ge(s_sd, 2)
                    link(nc.vector.reciprocal(k.rms[:, :], k.rms[:, :]))
                    link(nc.vector.tensor_tensor(k.rms[:, :], k.rms[:, :], k.rstd[:, :], ALU.mult))
                with dve.Fori(0, tiles // 2) as i:
                    if attn0:
                        link.enter(i, 4)
                    for j in range(2):
                        t = 2 * i + j
                        xt = x[:, bass.ds(t, 1), :].rearrange("p a d -> p (a d)")
                        mean = mv[:, bass.ds(t, 1), 0:1].rearrange("p a b -> p (a b)")
                        rstd = k.rstd[:, bass.ds(t, 1)]
                        dve.wait_ge(s_tr, t + 1)
                        if attn0:
                            rms = k.rms[:, bass.ds(t, 1)]
                            link(nc.vector.tensor_scalar(xn[:, j, :], xt, mean, rstd, ALU.subtract, ALU.mult))
                            nc.vector.tensor_scalar(xs[:, j, :], xt, mean, rms, ALU.subtract, ALU.mult).then_inc(s_xs, 1)
                            dve.wait_ge(s_xs, t + 1)
                            link(nc.vector.tensor_tensor(xt, xt, xn[:, j, :], ALU.add))
                        else:
                            nc.vector.tensor_scalar(xs[:, j, :], xt, mean, rstd, ALU.subtract, ALU.mult).then_inc(s_xs, 1)
                if attn0:
                    link.leave(tiles // 2)

            @block.tensor
            def _(pe):
                pe.sem_inc(s_tr, 2)
                with pe.Fori(0, tiles // 2) as i:
                    for j in range(2):
                        t = 2 * i + j
                        pe.wait_ge(s_xs, t + 1)
                        pe.wait_ge(s_xt, t + 1)
                        for c in range(DC):
                            last = nc.tensor.transpose(ps[:, j, c * P:(c + 1) * P], xs[:, j, c * P:(c + 1) * P], k.c("ident"))
                        last.then_inc(s_tr, 1)

            @block.scalar
            def _(act):
                act.wait_ge(s_var, 1)
                nc.scalar.activation(k.rstd[:, 0:tiles], k.rstd[:, 0:tiles], ACT.Sqrt).then_inc(s_sd, 1)
                if attn0:
                    act.wait_ge(s_var, 2)
                    nc.scalar.activation(k.rms[:, :], k.rms[:, :], ACT.Sqrt).then_inc(s_sd, 1)
                    act.wait_ge(s_w, 16)
                act.sem_inc(s_xt, 2)
                with act.Fori(0, tiles // 2) as i:
                    for j in range(2):
                        t = 2 * i + j
                        act.wait_ge(s_tr, t + 3)
                        if attn0:
                            nc.scalar.activation(xT[:, 0, bass.ds(t * P, P)], ps[:, j, 0:P], ACT.Copy, scale=nw[:, 0:1])
                            nc.scalar.activation(xT[:, 1, bass.ds(t * P, P)], ps[:, j, P:2 * P], ACT.Copy, scale=nw[:, 1:2]).then_inc(s_xt, 1)
                        else:
                            nc.scalar.activation(xT[:, :, bass.ds(t * P, P)],
                                                 ps[:, j, 0:D].rearrange("p (c q) -> p c q", c=DC), ACT.Copy).then_inc(s_xt, 1)

            if natural is not None:
                @block.gpsimd
                def _(pool):
                    pool.wait_ge(s_xs, 1)
                    for t in range(tiles):
                        nc.gpsimd.tensor_scalar(natural[:, t, :], x[:, t, :], mv[:, t, 0:1], k.rstd[:, t:t + 1],
                                                ALU.subtract, ALU.mult)


def attention0(k):
    nc, ps, xT = k.nc, k.ps, k.xT
    with ExitStack() as ctx:
        qT = k.sb("qT0", [P, DC, N], ctx=ctx)
        kT = k.sb("kT0", [P, N], ctx=ctx)
        v = k.sb("v0", [P, NT, 64], ctx=ctx)
        with ExitStack() as wctx:
            wq = k.sb("wq0", [P, DC, D], ctx=wctx)
            wk = k.sb("wk0", [P, DC, P], ctx=wctx)
            wv = k.sb("wv0", [P, DC, 64], ctx=wctx)
            rq = k.sb("rq0", [P, S], ctx=wctx)
            s_w = k.sem("s_w0")
            s_rq = k.sem("s_rq0")
            s_mm = k.sem("s_proj0")
            s_ev = k.sem("s_projev0")
            s_mmv = k.sem("s_projv0")
            with nc.Block() as block:
                @block.sync
                def _(sp):
                    sp.dma_start(wq[:, :, :], k.d["L0_attn_w_q"].rearrange("(c p) n -> p c n", p=P)).then_inc(s_w, 16)
                    for z in range(2):
                        sp.dma_start(wk[:, :, z * 64:(z + 1) * 64], k.d["L0_attn_w_k"].rearrange("(c p) n -> p c n", p=P)).then_inc(s_w, 16)
                    sp.dma_start(wv[:, :, :], k.d["L0_attn_w_v"].rearrange("(c p) n -> p c n", p=P)).then_inc(s_w, 16)

                @block.tensor
                def _(pe):
                    pe.wait_ge(s_w, 64)
                    with pe.Fori(0, N // 512) as n:
                        pe.wait_ge(s_ev, (n + 1) * (DC + 1))
                        for r in range(DC + 1):
                            for c in range(DC):
                                w = wq[:, c, r * P:(r + 1) * P] if r < DC else wk[:, c, :]
                                last = nc.tensor.matmul(ps[:, r, :], w, xT[:, c, bass.ds(n * 512, 512)],
                                                        start=(c == 0), stop=(c == DC - 1))
                            last.then_inc(s_mm, 1)
                    for t in range(NT):
                        for c in range(DC):
                            last = nc.tensor.matmul(ps[:, 6 + t // 8, (t % 8) * 64:(t % 8) * 64 + 64],
                                                    xT[:, c, t * P:(t + 1) * P], wv[:, c, :],
                                                    start=(c == 0), stop=(c == DC - 1))
                        last.then_inc(s_mmv, 1)

                @block.vector
                def _(dve):
                    nc.vector.tensor_scalar(rq[:, :], k.c("rope"), float(HD) ** -0.5, None, ALU.mult).then_inc(s_rq, 1)
                    dve.wait_ge(s_rq, 1)
                    dve.sem_inc(s_ev, DC + 1)
                    for n in range(N // 512):
                        for r in range(DC + 1):
                            dve.wait_ge(s_mm, n * (DC + 1) + r + 1)
                            o = (n * 512) % S
                            if r < DC:
                                nc.vector.tensor_tensor(qT[:, r, n * 512:(n + 1) * 512], ps[:, r, :], rq[:, o:o + 512],
                                                        ALU.mult).then_inc(s_ev, 1)
                            else:
                                nc.vector.tensor_tensor(kT[:, n * 512:(n + 1) * 512], ps[:, r, :],
                                                        k.c("rope")[:, o:o + 512], ALU.mult).then_inc(s_ev, 1)

                @block.scalar
                def _(act):
                    for g in range(2):
                        act.wait_ge(s_mmv, 8 * (g + 1))
                        nc.scalar.activation(v[:, 8 * g:8 * g + 8, :], ps[:, 6 + g, :].rearrange("p (t n) -> p t n", t=8), ACT.Copy)

        TPG = P // Q0
        TPB = KB * TPG
        with ExitStack() as actx:
            qbd = k.sb("qbd0", [P, 2, P], ctx=actx)
            causal = k.sb("causal0", [P, 256], BF16, ctx=actx)
            identb = k.sb("identb0", [P, P], BF16, ctx=actx)
            prob = k.sb("prob0", [P, 2, S], ctx=actx)
            probT = k.sb("probT0", [P, 2, S], ctx=actx)
            nmax = k.sb("nmax0", [P, 2], ctx=actx)
            rsum = k.sb("rsum0", [P, 2], ctx=actx)
            rinv = k.sb("rinv0", [P, 2], ctx=actx)
            om = k.sb("om0", [P, 2, D], ctx=actx)
            sm = {n: k.sem("s_a0_" + n) for n in ("const", "q", "s", "max", "exp", "tr", "evA", "evD", "o", "inv", "om", "c", "ctx")}

            def steps(eng, body, lags):
                with eng.Fori(0, B) as b:
                    def static(s):
                        def tile(lag):
                            u = s - lag
                            if u < 0 or u >= TPB:
                                return None
                            return b, u // TPG, u % TPG, u % 2, b * TPB + u
                        return tile
                    for a in range(KB):
                        for m in range(4):
                            body(static(a * TPG + m))
                        with eng.Fori(2, TPG // 2) as i:
                            for j in range(2):
                                def tile(lag, i=i, j=j):
                                    m = 2 * i + j - lag
                                    return b, a, m, (j - lag) % 2, b * TPB + a * TPG + m
                                body(tile)
                    for s in range(TPB, TPB + lags):
                        body(static(s))

            with nc.Block() as block:
                @block.gpsimd
                def _(pool):
                    nc.gpsimd.tensor_copy(causal[:, :], k.c("causal")).then_inc(sm["const"], 1)
                    nc.gpsimd.tensor_copy(identb[:, :], k.c("ident")).then_inc(sm["const"], 1)

                    def body(tile):
                        if tile(0) is None:
                            return
                        b, a, m, j, t = tile(0)
                        pool.wait_ge(sm["s"], t + 1)
                        tok = b * S + a * P + m * Q0
                        nc.gpsimd.tensor_tensor(
                            qbd[:, j, :].rearrange("p (c h i) -> p c h i", c=DC, h=HG),
                            qT[:, :, bass.ds(tok, Q0)].unsqueeze(2).to_broadcast([P, DC, HG, Q0]),
                            k.c("hmask").unsqueeze(1).unsqueeze(3).to_broadcast([P, DC, HG, Q0]),
                            ALU.mult).then_inc(sm["q"], 1)
                    steps(pool, body, 0)

                @block.tensor
                def _(pe):
                    pe.sem_inc(sm["s"], 2)
                    pe.wait_ge(sm["const"], 2)

                    def body(tile):
                        if tile(0):
                            b, a, m, j, t = tile(0)
                            L = (a + 1) * P
                            pe.wait_ge(sm["q"], t + 1)
                            pe.wait_ge(sm["exp"], t + 1)
                            for h in range(0, L, 512):
                                w = min(512, L - h)
                                last = nc.tensor.matmul(ps[:, 2 * j + h // 512, 0:w], qbd[:, j, :],
                                                        kT[:, bass.ds(b * S + h, w)], start=True, stop=(h + w < L))
                            last = nc.tensor.matmul(ps[:, 2 * j + (L - 1) // 512, (L - P) % 512:(L - P) % 512 + P], identb[:, :],
                                                    causal[:, bass.ds(120 - m * Q0, P)], start=False, stop=True)
                            last.then_inc(sm["s"], 1)
                        if tile(1):
                            b, a, m, j, t = tile(1)
                            pe.wait_ge(sm["exp"], t + 3)
                            pe.wait_ge(sm["evA"], t + 1)
                            for kb in range(a + 1):
                                if kb == 4:
                                    pe.wait_ge(sm["evD"], t + 1)
                                last = nc.tensor.transpose(ps[:, 4 + kb // 4, (kb % 4) * P:(kb % 4) * P + P],
                                                           prob[:, j, kb * P:(kb + 1) * P], k.c("ident"))
                            last.then_inc(sm["tr"], 1)
                        if tile(2):
                            b, a, m, j, t = tile(2)
                            pe.wait_ge(sm["evA"], t + 2)
                            pe.wait_ge(sm["evD"], t + 2)
                            pe.wait_ge(sm["om"], t + 2)
                            for kb in range(a + 1):
                                last = nc.tensor.matmul(ps[:, 6, 0:64], probT[:, j, kb * P:(kb + 1) * P],
                                                        v[:, bass.ds(b * KB + kb, 1), :].rearrange("p a n -> p (a n)"),
                                                        start=(kb == 0), stop=(kb == a))
                            last.then_inc(sm["o"], 1)
                        if tile(3):
                            b, a, m, j, t = tile(3)
                            pe.wait_ge(sm["om"], t + 3)
                            pe.wait_ge(sm["ctx"], t + 1)
                            for c in range(DC):
                                last = nc.tensor.matmul(ps[:, 7, c * Q0:(c + 1) * Q0], om[:, j, c * P:(c + 1) * P],
                                                        k.c("sum0"), start=True, stop=True)
                            last.then_inc(sm["c"], 1)
                    steps(pe, body, 3)

                @block.vector
                def _(dve):
                    dve.sem_inc(sm["evD"], 1)
                    dve.sem_inc(sm["om"], 2)
                    dve.sem_inc(sm["inv"], 2)
                    dve.sem_inc(sm["ctx"], 1)

                    def body(tile):
                        if tile(0):
                            b, a, m, j, t = tile(0)
                            L = (a + 1) * P
                            dve.wait_ge(sm["s"], t + 3)
                            src = ps[:, 2 * j, 0:L] if L <= 512 else ps[:, 2 * j:2 * j + 2, :].rearrange("p a n -> p (a n)")[:, 0:L]
                            nc.vector.tensor_reduce(nmax[:, j:j + 1], src, AX.X, ALU.max, negate=True).then_inc(sm["max"], 1)
                        if tile(1):
                            b, a, m, j, t = tile(1)
                            dve.wait_ge(sm["tr"], t + 1)
                            if a >= 4:
                                w = (a - 3) * P
                                nc.vector.tensor_copy(probT[:, j, 512:512 + w], ps[:, 5, 0:w]).then_inc(sm["evD"], 1)
                            else:
                                dve.sem_inc(sm["evD"], 1)
                            dve.wait_ge(sm["om"], t + 1)
                            nc.vector.reciprocal(rinv[:, j:j + 1], rsum[:, j:j + 1]).then_inc(sm["inv"], 1)
                        if tile(2):
                            b, a, m, j, t = tile(2)
                            dve.wait_ge(sm["o"], t + 1)
                            dve.wait_ge(sm["inv"], t + 3)
                            nc.vector.scalar_tensor_tensor(
                                om[:, j, :].rearrange("p (r n) -> p r n", r=REP),
                                ps[:, 6, 0:64].unsqueeze(1).to_broadcast([P, REP, 64]), rinv[:, j:j + 1],
                                k.c("head0").rearrange("p (r n) -> p r n", r=REP), ALU.mult, ALU.mult).then_inc(sm["om"], 1)
                        if tile(3):
                            b, a, m, j, t = tile(3)
                            dve.wait_ge(sm["c"], t + 1)
                            nc.vector.tensor_copy(xT[:, :, bass.ds(b * S + a * P + m * Q0, Q0)],
                                                  ps[:, 7, 0:DC * Q0].rearrange("p (c q) -> p c q", c=DC)).then_inc(sm["ctx"], 1)
                    steps(dve, body, 3)

                @block.scalar
                def _(act):
                    act.sem_inc(sm["exp"], 2)
                    act.sem_inc(sm["evA"], 1)

                    def body(tile):
                        if tile(0):
                            b, a, m, j, t = tile(0)
                            L = (a + 1) * P
                            act.wait_ge(sm["max"], t + 1)
                            act.wait_ge(sm["inv"], t + 1)
                            src = ps[:, 2 * j, 0:L] if L <= 512 else ps[:, 2 * j:2 * j + 2, :].rearrange("p a n -> p (a n)")[:, 0:L]
                            nc.scalar.activation(prob[:, j, 0:L], src, ACT.Exp, bias=nmax[:, j:j + 1],
                                                 accum_out=rsum[:, j:j + 1]).then_inc(sm["exp"], 1)
                        if tile(1):
                            b, a, m, j, t = tile(1)
                            w = min(a + 1, 4) * P
                            act.wait_ge(sm["tr"], t + 1)
                            nc.scalar.activation(probT[:, j, 0:w], ps[:, 4, 0:w], ACT.Copy).then_inc(sm["evA"], 1)
                    steps(act, body, 1)

        project_out(k, "0", "L0_attn_w_o", None)


def project_out(k, tag, w_name, b_name):
    nc, ps, xT = k.nc, k.ps, k.xT
    with ExitStack() as ctx:
        wo = k.sb("wo" + tag, [P, DC, D], ctx=ctx)
        bo = k.sb("bo" + tag, [1, D], ctx=ctx)
        s_w, s_mm, s_add = k.sem("s_wo" + tag), k.sem("s_omm" + tag), k.sem("s_oadd" + tag)
        with nc.Block() as block:
            @block.sync
            def _(sp):
                sp.dma_start(wo[:, :, :], k.d[w_name].rearrange("(c p) n -> p c n", p=P)).then_inc(s_w, 16)
                if b_name:
                    sp.dma_start(bo[:, :], k.d[b_name].rearrange("(a n) -> a n", a=1)).then_inc(s_w, 16)

            @block.tensor
            def _(pe):
                pe.wait_ge(s_w, 32 if b_name else 16)
                for t in range(NT):
                    if t >= 4:
                        pe.wait_ge(s_add, t - 3)
                    for c in range(DC):
                        last = nc.tensor.matmul(ps[:, t % 4, 0:D], xT[:, c, t * P:(t + 1) * P], wo[:, c, :],
                                                start=(c == 0), stop=(c == DC - 1 and not b_name))
                    if b_name:
                        last = nc.tensor.matmul(ps[:, t % 4, 0:D], k.c("ones", 1), bo[:, :], start=False, stop=True)
                    last.then_inc(s_mm, 1)

            @block.vector
            def _(dve):
                for t in range(NT):
                    dve.wait_ge(s_mm, t + 1)
                    nc.vector.tensor_tensor(k.x[:, t, :], k.x[:, t, :], ps[:, t % 4, 0:D], ALU.add).then_inc(s_add, 1)


def context_prep(k):
    nc, ps = k.nc, k.ps
    with ExitStack() as ctx:
        wa = k.sb("wa", [P, DC, D], ctx=ctx)
        waT = k.sb("waT", [P, DC, D], ctx=ctx)
        wp = k.sb("wp", [PH, D], ctx=ctx)
        s_ld, s_t1, s_e1, s_g, s_ge = (k.sem("s_ctx" + n) for n in ("ld", "t1", "e1", "g", "ge"))
        with nc.Block() as block:
            @block.sync
            def _(sp):
                sp.dma_start(wa[:, :, :], k.d["L0_xattn_W_a"].rearrange("(c p) q -> p c q", p=P)).then_inc(s_ld, 16)
                sp.dma_start(k.ctxn[:, :, :], k.d["ctx_1024"].rearrange("b j q -> j b q")).then_inc(s_ld, 16)
                sp.dma_start(wp[:, :], k.d["L0_xattn_W_p"]).then_inc(s_ld, 16)
                sp.dma_start(k.vp[:, :], k.d["L0_xattn_V_p"].rearrange("a p -> p a"),
                             allow_slow_non_contiguous=True).then_inc(s_ld, 16)

            @block.tensor
            def _(pe):
                pe.wait_ge(s_ld, 64)
                for q in range(DC):
                    for c in range(DC):
                        nc.tensor.transpose(ps[:, 0, (q * DC + c) * P:(q * DC + c + 1) * P], wa[:, c, q * P:(q + 1) * P], k.c("ident"))
                for b in range(B):
                    for c in range(DC):
                        nc.tensor.transpose(ps[:, 1, (b * DC + c) * P:(b * DC + c) * P + SC],
                                            k.ctxn[:, b, c * P:(c + 1) * P], k.c("ident", SC)[:, 0:SC])
                for c in range(DC):
                    last = nc.tensor.transpose(ps[:, 2, c * P:c * P + PH], wp[:, c * P:(c + 1) * P], k.c("ident", PH)[:, 0:PH])
                last.then_inc(s_t1, 1)
                pe.wait_ge(s_e1, 1)
                for b in range(B):
                    for c in range(DC):
                        for q in range(DC):
                            last = nc.tensor.matmul(ps[:, 3, (b * DC + c) * P:(b * DC + c) * P + SC],
                                                    waT[:, q, c * P:(c + 1) * P], k.ctxT[:, b, q, :],
                                                    start=(q == 0), stop=(q == DC - 1))
                last.then_inc(s_g, 1)

            @block.vector
            def _(dve):
                dve.wait_ge(s_t1, 1)
                nc.vector.tensor_copy(waT[:, :, :], ps[:, 0, :].rearrange("p (q c) -> p q c", q=DC))
                nc.vector.tensor_copy(k.wpT[:, :, :], ps[:, 2, 0:DC * P].rearrange("p (c n) -> p c n", c=DC)[:, :, 0:PH])
                nc.vector.tensor_copy(k.ctxT[:, :, :, :].rearrange("p b c j -> p (b c) j"),
                                      ps[:, 1, :].rearrange("p (bc n) -> p bc n", n=P)[:, :, 0:SC]).then_inc(s_e1, 1)
                dve.wait_ge(s_g, 1)
                nc.vector.tensor_copy(k.gT[:, :, :, :].rearrange("p b c j -> p (b c) j"),
                                      ps[:, 3, :].rearrange("p (bc n) -> p bc n", n=P)[:, :, 0:SC]).then_inc(s_ge, 1)


def cross_attention0(k):
    nc, ps, xT = k.nc, k.ps, k.xT
    with ExitStack() as ctx:
        hidT = k.sb("hidT", [PH, N], ctx=ctx)
        pt = k.sb("pt", [P, NT], ctx=ctx)
        lo = k.sb("lo", [P, NT], ctx=ctx)
        loi = k.sb("loi", [P, NT], I32, ctx=ctx)
        fl = k.sb("fl", [P, NT], ctx=ctx)
        mx = k.sb("mx", [P, NT], ctx=ctx)
        sc = k.sb("sc", [P, NT, SC], ctx=ctx)
        cnt = k.sb("cnt", [P, NT, SC], ctx=ctx)
        tmp = k.sb("tmp", [P, NT, SC], ctx=ctx)
        gs = k.sb("gs", [P, NT, SC], ctx=ctx)
        aT = k.sb("aT", [SC, NT, P], ctx=ctx)
        s_hid, s_th, s_z, s_tz, s_sc, s_ch, s_gin, s_g, s_ein, s_e, s_a, s_at, s_ate, s_o, s_x = (
            k.sem("s_x0_" + n) for n in ("hid", "th", "z", "tz", "sc", "ch", "gin", "g", "ein", "e", "a", "at", "ate", "o", "x"))

        def rows(v):
            return v.unsqueeze(2).to_broadcast([P, NT, SC])

        with nc.Block() as block:
            @block.tensor
            def _(pe):
                for n in range(4):
                    for c in range(DC):
                        last = nc.tensor.matmul(ps[0:PH, n, :], k.wpT[:, c, :], xT[:, c, n * 512:(n + 1) * 512],
                                                start=(c == 0), stop=(c == DC - 1))
                    last.then_inc(s_hid, 1)
                for t in range(NT):
                    for c in range(DC):
                        last = nc.tensor.matmul(ps[:, 4 + t // 4, (t % 4) * P:(t % 4) * P + SC], xT[:, c, t * P:(t + 1) * P],
                                                k.gT[:, t // KB, c, :], start=(c == 0), stop=(c == DC - 1))
                    if t % 4 == 3:
                        last.then_inc(s_sc, 1)
                pe.wait_ge(s_th, 4)
                for t in range(NT):
                    last = nc.tensor.matmul(ps[:, 0, t:t + 1], hidT[:, t * P:(t + 1) * P], k.vp[:, :], start=True, stop=True)
                last.then_inc(s_z, 1)
                pe.wait_ge(s_a, 1)
                for g in range(4):
                    for t in range(4 * g, 4 * g + 4):
                        last = nc.tensor.transpose(ps[0:SC, 1 + g, (t % 4) * P:(t % 4 + 1) * P], sc[:, t, :], k.c("ident"))
                    last.then_inc(s_at, 1)
                for t in range(NT):
                    if t % 4 == 0:
                        pe.wait_ge(s_ate, t // 4 + 1)
                    if t >= 2:
                        pe.wait_ge(s_x, t - 1)
                    nc.tensor.matmul(ps[:, 5 + t % 2, 0:D], aT[:, t, :], k.ctxn[:, t // KB, :], start=True, stop=True).then_inc(s_o, 1)

            @block.scalar
            def _(act):
                for n in range(4):
                    act.wait_ge(s_hid, n + 1)
                    nc.scalar.activation(hidT[:, n * 512:(n + 1) * 512], ps[0:PH, n, :], ACT.Tanh).then_inc(s_th, 1)
                act.wait_ge(s_z, 1)
                nc.scalar.activation(pt[:, :], ps[:, 0, 0:NT], ACT.Tanh, scale=0.5).then_inc(s_tz, 1)
                act.wait_ge(s_gin, 1)
                nc.scalar.activation(gs[:, :, :], gs[:, :, :], ACT.Exp, scale=-0.5).then_inc(s_g, 1)
                act.wait_ge(s_ein, 1)
                nc.scalar.activation(sc[:, :, :], sc[:, :, :], ACT.Exp).then_inc(s_e, 1)
                for g in range(4):
                    act.wait_ge(s_at, g + 1)
                    nc.scalar.activation(aT[:, 4 * g:4 * g + 4, :], ps[0:SC, 1 + g, :].rearrange("p (t n) -> p t n", t=4),
                                         ACT.Copy).then_inc(s_ate, 1)

            @block.vector
            def _(dve):
                link = Chain(dve, s_ch)
                for g in range(4):
                    dve.wait_ge(s_sc, g + 1)
                    link(nc.vector.tensor_copy(sc[:, 4 * g:4 * g + 4, :],
                                               ps[:, 4 + g, :].rearrange("p (t n) -> p t n", t=4)[:, :, 0:SC]))
                dve.wait_ge(s_tz, 1)
                link(nc.vector.tensor_scalar(pt[:, :], pt[:, :], 1.0, SC / 2.0, ALU.add, ALU.mult))
                iota = k.c("iota77").unsqueeze(1).to_broadcast([P, NT, SC])
                link(nc.vector.tensor_tensor(gs[:, :, :], iota, rows(pt[:, :]), ALU.subtract))
                nc.vector.tensor_tensor(gs[:, :, :], gs[:, :, :], gs[:, :, :], ALU.mult).then_inc(s_gin, 1)
                link(nc.vector.tensor_copy(loi[:, :], pt[:, :]))
                link(nc.vector.tensor_copy(lo[:, :], loi[:, :]))
                link(nc.vector.tensor_tensor(fl[:, :], lo[:, :], pt[:, :], ALU.is_gt))
                link(nc.vector.tensor_tensor(lo[:, :], lo[:, :], fl[:, :], ALU.subtract))
                link(nc.vector.tensor_scalar(lo[:, :], lo[:, :], float(WIN), None, ALU.subtract))
                link(nc.vector.tensor_tensor(tmp[:, :, :], iota, rows(lo[:, :]), ALU.subtract))
                link(nc.vector.tensor_scalar(cnt[:, :, :], tmp[:, :, :], 0.0, None, ALU.is_ge))
                link(nc.vector.tensor_scalar(tmp[:, :, :], tmp[:, :, :], 2.0 * WIN - 1, None, ALU.is_le))
                link(nc.vector.tensor_tensor(cnt[:, :, :], cnt[:, :, :], tmp[:, :, :], ALU.mult))
                link(nc.vector.tensor_scalar(fl[:, :], lo[:, :], -1.0, 1.0, ALU.mult, ALU.add))
                link(nc.vector.tensor_scalar(cnt[:, :, 0], fl[:, :], 0.0, 2.0 * WIN, ALU.max, ALU.min))
                link(nc.vector.tensor_scalar(fl[:, :], lo[:, :], float(SC - 1 - 2 * WIN), None, ALU.subtract))
                link(nc.vector.tensor_scalar(cnt[:, :, SC - 1], fl[:, :], 0.0, 2.0 * WIN, ALU.max, ALU.min))
                link(nc.vector.tensor_scalar(tmp[:, :, :], cnt[:, :, :], 0.0, None, ALU.is_gt))
                link(nc.vector.tensor_tensor(sc[:, :, :], sc[:, :, :], tmp[:, :, :], ALU.mult))
                link(nc.vector.tensor_scalar(tmp[:, :, :], tmp[:, :, :], 1.0, -NEG, ALU.subtract, ALU.mult))
                link(nc.vector.tensor_tensor(sc[:, :, :], sc[:, :, :], tmp[:, :, :], ALU.add))
                link(nc.vector.tensor_reduce(mx[:, :], sc[:, :, :], AX.X, ALU.max))
                nc.vector.tensor_tensor(sc[:, :, :], sc[:, :, :], rows(mx[:, :]), ALU.subtract).then_inc(s_ein, 1)
                dve.wait_ge(s_e, 1)
                link(nc.vector.tensor_tensor(sc[:, :, :], sc[:, :, :], cnt[:, :, :], ALU.mult))
                link(nc.vector.tensor_reduce(mx[:, :], sc[:, :, :], AX.X, ALU.add))
                link(nc.vector.reciprocal(mx[:, :], mx[:, :]))
                dve.wait_ge(s_g, 1)
                link(nc.vector.tensor_tensor(sc[:, :, :], sc[:, :, :], gs[:, :, :], ALU.mult))
                nc.vector.tensor_tensor(sc[:, :, :], sc[:, :, :], rows(mx[:, :]), ALU.mult).then_inc(s_a, 1)
                for t in range(NT):
                    dve.wait_ge(s_o, t + 1)
                    nc.vector.tensor_tensor(k.x[:, t, :], k.x[:, t, :], ps[:, 5 + t % 2, 0:D], ALU.add).then_inc(s_x, 1)


def moe0(k):
    nc, ps, xT = k.nc, k.ps, k.xT
    ROWS = 2 * CAP
    ST = ROWS // P
    G8 = [P, NT, E]
    disp = nc.dram_tensor("disp", ((E + 1) * ROWS, D), F32, kind="Internal").ap()
    ybuf = nc.dram_tensor("ybuf", (E * ROWS, D), F32, kind="Internal").ap()
    with ExitStack() as ctx:
        wgt = k.sb("wgt", [P, 2, NT], ctx=ctx)
        idx_s = k.sb("idx_s", [P, 2, NT], U32, ctx=ctx)
        idx_g = k.sb("idx_g", [P, 2, NT], U32, ctx=ctx)
        with ExitStack() as rctx:
            xn = k.sb("xn_nat", [P, NT, D], ctx=rctx)
            zero = k.sb("zero", [P, ST * D], ctx=rctx)
            s_zero, s_zf = k.sem("s_zero"), k.sem("s_zf")
            norm_transpose(k, "0c", natural=xn)
            gT = k.sb("gateT", [P, DC, E], ctx=rctx)
            lg, ex, oh1, oh2, cand, pos, base, keep, cw = (k.sb("r_" + n, G8, ctx=rctx) for n in (
                "lg", "ex", "oh1", "oh2", "cand", "pos", "base", "keep", "cw"))
            m1, m2, sl, va = (k.sb("r_" + n, [P, NT], ctx=rctx) for n in ("m1", "m2", "sl", "va"))
            dump = k.sb("r_dump", [P, 1], ctx=rctx)
            s_g, s_lg, s_ch, s_ei, s_ex, s_sel, s_cum, s_idx, s_sc = (
                k.sem("s_r_" + n) for n in ("g", "lg", "ch", "ei", "ex", "sel", "cum", "idx", "sc"))
            with nc.Block() as block:
                @block.sync
                def _(sp):
                    for c in range(DC):
                        sp.dma_start(gT[:, c, :], k.d["L0_ffn_gate_w"][:, c * P:(c + 1) * P].rearrange("e p -> p e"),
                                     allow_slow_non_contiguous=True).then_inc(s_g, 16)
                    sp.wait_ge(s_zero, 1)
                    rows = disp.rearrange("(n p a) d -> n p (a d)", p=P, a=ST)
                    for n in range(rows.shape[0]):
                        sp.dma_start(rows[n], zero[:, :]).then_inc(s_zf, 16)
                    sp.wait_ge(s_zf, 16 * rows.shape[0])

                @block.tensor
                def _(pe):
                    pe.wait_ge(s_g, 16 * DC)
                    for t in range(NT):
                        for c in range(DC):
                            last = nc.tensor.matmul(ps[:, 0, t * E:(t + 1) * E], xT[:, c, t * P:(t + 1) * P], gT[:, c, :],
                                                    start=(c == 0), stop=(c == DC - 1))
                    last.then_inc(s_lg, 1)
                    pe.wait_ge(s_sel, 1)
                    nc.tensor.matmul(ps[:, 1, 0:NT * E], k.c("tri"), cand[:, :, :].rearrange("p t e -> p (t e)"),
                                     start=True, stop=True, skip_group_check=True)
                    for b in range(B):
                        for s in range(1, KB):
                            o = (b * KB + s) * E
                            w = (KB - s) * E
                            last = nc.tensor.matmul(ps[:, 1, o:o + w], k.c("ones"),
                                                    cand[:, b * KB:b * KB + KB - s, :].rearrange("p t e -> p (t e)"),
                                                    start=False, stop=True, skip_group_check=True)
                    last.then_inc(s_cum, 1)

                @block.scalar
                def _(act):
                    act.wait_ge(s_ei, 1)
                    nc.scalar.activation(ex[:, :, :], ex[:, :, :], ACT.Exp).then_inc(s_ex, 1)

                @block.vector
                def _(dve):
                    nc.vector.memset(zero[:, :], 0.0).then_inc(s_zero, 1)
                    link = Chain(dve, s_ch)
                    iota = k.c("iota8").unsqueeze(1).to_broadcast(G8)

                    def row(v):
                        return v.unsqueeze(2).to_broadcast(G8)

                    def first_best(oh, m):
                        link(nc.vector.tensor_reduce(m[:, :], lg[:, :, :], AX.X, ALU.max))
                        link(nc.vector.tensor_tensor(cand[:, :, :], lg[:, :, :], row(m[:, :]), ALU.is_lt))
                        link(nc.vector.tensor_scalar(cand[:, :, :], cand[:, :, :], 100.0, None, ALU.mult))
                        link(nc.vector.tensor_tensor(cand[:, :, :], cand[:, :, :], iota, ALU.add))
                        link(nc.vector.tensor_reduce(m2[:, :], cand[:, :, :], AX.X, ALU.min))
                        link(nc.vector.tensor_tensor(oh[:, :, :], iota, row(m2[:, :]), ALU.is_equal))

                    dve.wait_ge(s_lg, 1)
                    link(nc.vector.tensor_copy(lg[:, :, :], ps[:, 0, 0:NT * E].rearrange("p (t e) -> p t e", e=E)))
                    first_best(oh1, m1)
                    nc.vector.tensor_tensor(ex[:, :, :], lg[:, :, :], row(m1[:, :]), ALU.subtract).then_inc(s_ei, 1)
                    link(nc.vector.tensor_scalar(cand[:, :, :], oh1[:, :, :], NEG, None, ALU.mult))
                    dve.wait_ge(s_ei, 1)
                    link(nc.vector.tensor_tensor(lg[:, :, :], lg[:, :, :], cand[:, :, :], ALU.add))
                    first_best(oh2, m1)
                    nc.vector.tensor_tensor(cand[:, :, :], oh1[:, :, :], oh2[:, :, :], ALU.add).then_inc(s_sel, 1)
                    dve.wait_ge(s_ex, 1)
                    link(nc.vector.tensor_reduce(m1[:, :], ex[:, :, :], AX.X, ALU.add))
                    link(nc.vector.reciprocal(m1[:, :], m1[:, :]))
                    link(nc.vector.tensor_tensor(ex[:, :, :], ex[:, :, :], row(m1[:, :]), ALU.mult))
                    for b in range(B):
                        link(nc.vector.tensor_scalar(base[:, b * KB:(b + 1) * KB, :],
                                                     k.c("cap0").unsqueeze(1).to_broadcast([P, KB, E]),
                                                     float(b * CAP - 1), None, ALU.add))
                    dve.wait_ge(s_cum, 1)
                    link(nc.vector.tensor_copy(pos[:, :, :], ps[:, 1, 0:NT * E].rearrange("p (t e) -> p t e", e=E)))
                    link(nc.vector.tensor_scalar(keep[:, :, :], pos[:, :, :], float(CAP), None, ALU.is_le))
                    link(nc.vector.tensor_tensor(base[:, :, :], base[:, :, :], pos[:, :, :], ALU.add))
                    for c, oh in enumerate((oh1, oh2)):
                        link(nc.vector.tensor_tensor(oh[:, :, :], oh[:, :, :], keep[:, :, :], ALU.mult))
                        link(nc.vector.tensor_tensor(cw[:, :, :], oh[:, :, :], ex[:, :, :], ALU.mult))
                        link(nc.vector.tensor_reduce(wgt[:, c, :], cw[:, :, :], AX.X, ALU.add))
                        link(nc.vector.tensor_tensor(cw[:, :, :], oh[:, :, :], base[:, :, :], ALU.mult))
                        link(nc.vector.tensor_reduce(sl[:, :], cw[:, :, :], AX.X, ALU.add))
                        link(nc.vector.tensor_reduce(va[:, :], oh[:, :, :], AX.X, ALU.add))
                        link(nc.vector.tensor_copy(idx_g[:, c, :], sl[:, :]))
                        link(nc.vector.tensor_scalar(va[:, :], va[:, :], -1.0, 1.0, ALU.mult, ALU.add))
                        link(nc.vector.tensor_tensor(va[:, :], va[:, :], k.c("spare").to_broadcast([P, NT]), ALU.mult))
                        link(nc.vector.tensor_tensor(sl[:, :], sl[:, :], va[:, :], ALU.add))
                        link(nc.vector.tensor_copy(idx_s[:, c, :], sl[:, :]))
            with nc.Block() as block:
                @block.gpsimd
                def _(pool):
                    for t in range(NT):
                        for c in range(2):
                            nc.gpsimd.indirect_dma_start(
                                out=disp, out_offset=bass.IndirectOffsetOnAxis(ap=idx_s[:, c, t:t + 1], axis=0),
                                in_=xn[:, t, :], in_offset=None).then_inc(s_sc, 16)
                    pool.wait_ge(s_sc, 16 * 2 * NT)

        UPE = FC0 + 2
        HR = ROWS // 2
        with ExitStack() as ectx:
            w1 = k.sb("w1", [P, 2, DC, F0], ctx=ectx)
            w3 = k.sb("w3", [P, 2, DC, F0], ctx=ectx)
            w2 = k.sb("w2", [P, 2, FC0, D], ctx=ectx)
            xe = k.sb("xe", [P, 2, ST, D], ctx=ectx)
            xeT = k.sb("xeT", [P, 2, DC, ROWS], ctx=ectx)
            sg = k.sb("sg", [P, 2, ROWS], ctx=ectx)
            hT = k.sb("hT", [P, 2, FC0, ROWS], ctx=ectx)
            ye = k.sb("ye", [P, 2, ST, D], ctx=ectx)
            s_w13 = [k.sem(f"s_w13_{j}") for j in range(2)]
            s_w2 = [k.sem(f"s_w2_{j}") for j in range(2)]
            s_xe = [k.sem(f"s_xe_{j}") for j in range(2)]
            s_use, s_hT, s_xet, s_silu, s_ye, s_yst, s_yfree = (
                k.sem("s_m_" + n) for n in ("use", "hT", "xet", "silu", "ye", "yst", "yfree"))
            with nc.Block() as block:
                @block.sync
                def _(sp):
                    for e in range(E + 1):
                        j = e % 2
                        if e >= 2:
                            sp.wait_ge(s_use, UPE * (e - 3) + FC0 + 2 if e >= 3 else 1)
                        sp.dma_start(xe[:, j, :, :], disp[e * ROWS:(e + 1) * ROWS, :].rearrange("(t p) d -> p t d", p=P)).then_inc(s_xe[j], 16)
                        if e == E:
                            break
                        if e >= 2:
                            sp.wait_ge(s_use, UPE * (e - 2) + FC0 + 1)
                        sp.dma_start(w1[:, j, :, :], k.d["L0_ffn_w1"][e].rearrange("(c p) f -> p c f", p=P)).then_inc(s_w13[j], 16)
                        sp.dma_start(w3[:, j, :, :], k.d["L0_ffn_w3"][e].rearrange("(c p) f -> p c f", p=P)).then_inc(s_w13[j], 16)
                        if e >= 2:
                            sp.wait_ge(s_use, UPE * (e - 1) + 1)
                        sp.dma_start(w2[:, j, :, :], k.d["L0_ffn_w2"][e].rearrange("(c p) d -> p c d", p=P)).then_inc(s_w2[j], 16)

                def banks(n):
                    return 4 * (n % 2)

                @block.tensor
                def _(pe):
                    def transposes(j, n):
                        for tt in range(ST):
                            for c in range(DC):
                                q = tt * DC + c
                                last = nc.tensor.transpose(ps[:, banks(n) + q // 4, (q % 4) * P:(q % 4 + 1) * P],
                                                           xe[:, j, tt, c * P:(c + 1) * P], k.c("ident"))
                        last.then_inc(s_use, 1)

                    pe.wait_ge(s_xe[0], 16)
                    transposes(0, 0)
                    with pe.Fori(0, E // 2) as i:
                        for j in range(2):
                            n0 = UPE * j + 1
                            pe.wait_ge(s_xet, 2 * i + j + 1)
                            pe.wait_ge(s_w13[j], 32 * i + 32)
                            for f in range(FC0):
                                n = n0 + f
                                if f == 1:
                                    pe.wait_ge(s_ye, 2 * i + j + 1)
                                elif f >= 2:
                                    pe.wait_ge(s_hT, 2 * FC0 * i + FC0 * j + f - 1)
                                for w, o in ((w1, 0), (w3, 2)):
                                    for h in range(2):
                                        for c in range(DC):
                                            last = nc.tensor.matmul(ps[:, banks(n) + o + h, 0:HR], w[:, j, c, f * P:(f + 1) * P],
                                                                    xeT[:, j, c, h * HR:(h + 1) * HR],
                                                                    start=(c == 0), stop=(c == DC - 1))
                                last.then_inc(s_use, 1)
                            n = n0 + FC0
                            pe.wait_ge(s_xe[1 - j], 16 * i + 16 * (j + 1))
                            pe.wait_ge(s_hT, 2 * FC0 * i + FC0 * j + FC0 - 1)
                            transposes(1 - j, n)
                            n = n0 + FC0 + 1
                            pe.wait_ge(s_hT, 2 * FC0 * i + FC0 * j + FC0)
                            pe.wait_ge(s_w2[j], 16 * i + 16)
                            for tt in range(ST):
                                for f in range(FC0):
                                    last = nc.tensor.matmul(ps[:, banks(n) + tt // 2, (tt % 2) * D:(tt % 2 + 1) * D],
                                                            hT[:, j, f, tt * P:(tt + 1) * P], w2[:, j, f, :],
                                                            start=(f == 0), stop=(f == FC0 - 1))
                            last.then_inc(s_use, 1)

                @block.scalar
                def _(act):
                    def copy_rows(j, n, use):
                        act.wait_ge(s_use, use)
                        for q in range(3):
                            w = min(2, ST - 2 * q)
                            last = nc.scalar.activation(
                                xeT[:, j, :, 2 * q * P:(2 * q + w) * P].rearrange("p c (t n) -> p t c n", n=P),
                                ps[:, banks(n) + q, 0:w * DC * P].rearrange("p (t c n) -> p t c n", t=w, c=DC), ACT.Copy)
                        last.then_inc(s_xet, 1)

                    copy_rows(0, 0, 1)
                    with act.Fori(0, E // 2) as i:
                        for j in range(2):
                            for f in range(FC0):
                                n = UPE * j + 1 + f
                                act.wait_ge(s_use, 2 * UPE * i + n + 1)
                                nc.scalar.activation(sg[:, n % 2, :].rearrange("p (h m) -> p h m", h=2),
                                                     ps[:, banks(n):banks(n) + 2, 0:HR], ACT.Silu).then_inc(s_silu, 1)
                            n = UPE * j + 1 + FC0
                            copy_rows(1 - j, n, 2 * UPE * i + n + 1)

                @block.vector
                def _(dve):
                    dve.sem_inc(s_ye, 1)
                    with dve.Fori(0, E // 2) as i:
                        for j in range(2):
                            for f in range(FC0):
                                n = UPE * j + 1 + f
                                dve.wait_ge(s_silu, 2 * FC0 * i + FC0 * j + f + 1)
                                nc.vector.tensor_tensor(hT[:, j, f, :].rearrange("p (h m) -> p h m", h=2),
                                                        ps[:, banks(n) + 2:banks(n) + 4, 0:HR],
                                                        sg[:, n % 2, :].rearrange("p (h m) -> p h m", h=2),
                                                        ALU.mult).then_inc(s_hT, 1)
                            n = UPE * j + 2 + FC0
                            dve.wait_ge(s_use, 2 * UPE * i + n + 1)
                            dve.wait_ge(s_yfree, 2 * i + j + 1)
                            nc.vector.tensor_copy(ye[:, j, :, :], ps[:, banks(n):banks(n) + 3, :].rearrange(
                                "p a n -> p (a n)")[:, 0:ST * D].rearrange("p (t d) -> p t d", d=D)).then_inc(s_ye, 1)

                @block.gpsimd
                def _(pool):
                    pool.sem_inc(s_yfree, 2)
                    for e in range(E):
                        pool.wait_ge(s_ye, e + 2)
                        pool.dma_start(ybuf[e * ROWS:(e + 1) * ROWS, :].rearrange("(t p) d -> p t d", p=P),
                                       ye[:, e % 2, :, :]).then_inc(s_yst, 16)
                        pool.wait_ge(s_yst, 16 * (e + 1))
                        pool.sem_inc(s_yfree, 1)

        with ExitStack() as cctx:
            NB = 8
            yg = k.sb("yg", [P, NB, D], ctx=cctx)
            s_yg = [k.sem(f"s_yg{n}") for n in range(NB)]
            s_add = k.sem("s_yadd")
            with nc.Block() as block:
                @block.gpsimd
                def _(pool):
                    for n in range(2 * NT):
                        if n >= NB:
                            pool.wait_ge(s_add, n - NB + 1)
                        nc.gpsimd.indirect_dma_start(
                            out=yg[:, n % NB, :], out_offset=None, in_=ybuf,
                            in_offset=bass.IndirectOffsetOnAxis(ap=idx_g[:, n % 2, n // 2:n // 2 + 1], axis=0)).then_inc(s_yg[n % NB], 16)

                @block.vector
                def _(dve):
                    for n in range(2 * NT):
                        t = n // 2
                        dve.wait_ge(s_yg[n % NB], 16 * (n // NB + 1))
                        if n:
                            dve.wait_ge(s_add, n)
                        nc.vector.scalar_tensor_tensor(k.x[:, t, :], yg[:, n % NB, :], wgt[:, n % 2, t:t + 1], k.x[:, t, :],
                                                       ALU.mult, ALU.add).then_inc(s_add, 1)


def attention1(k):
    nc, ps, xT = k.nc, k.ps, k.xT
    TPB = S // Q1
    HALF = TPB // 2
    W_RT, W_TV = 512, 384
    O_RT, O_TV = 248, 255
    extk = nc.dram_tensor("extk", (EXT, HD), F32, kind="Internal").ap()
    extv = nc.dram_tensor("extv", (EXT, HD), F32, kind="Internal").ap()
    qd = nc.dram_tensor("qd", (D, N), F32, kind="Internal").ap()
    with ExitStack() as ctx:
        qT = k.sb("qT1", [P, DC * N], ctx=ctx)
        kT = k.sb("kT1", [P, DC * N], ctx=ctx)
        v = k.sb("v1", [P, NT, D], ctx=ctx)
        rt = k.sb("rt", [P, W_RT], ctx=ctx)
        tv = k.sb("tv", [P, W_TV, HD], ctx=ctx)
        with ExitStack() as wctx:
            w = k.sb("wqkv", [P, DC, 3 * D], ctx=wctx)
            bc = k.sb("bqkv", [P, 6], ctx=wctx)
            bv = k.sb("bv", [1, D], ctx=wctx)
            ek = k.sb("ek", [P, 4, 8, HD], ctx=wctx)
            s_w, s_ext, s_tab, s_rt, s_bq, s_mm, s_ev, s_mmv, s_evv, s_qd = (
                k.sem("s_p1_" + n) for n in ("w", "ext", "tab", "rt", "bq", "mm", "ev", "mmv", "evv", "qd"))
            s_rte = k.sem("s_p1_rte")
            with nc.Block() as block:
                @block.sync
                def _(sp):
                    sp.dma_start(w[:, :, :], k.d["L1_attn_W_qkv"].rearrange("(c p) n -> p c n", p=P)).then_inc(s_w, 16)
                    sp.dma_start(bc[:, :], k.d["L1_attn_b_qkv"].rearrange("(s p) -> p s", p=P),
                                 allow_slow_non_contiguous=True).then_inc(s_w, 16)
                    sp.dma_start(bv[:, :], k.d["L1_attn_b_qkv"][2 * D:3 * D].rearrange("(a n) -> a n", a=1)).then_inc(s_w, 16)
                    lo = O_TV - R
                    for ext, name in ((extk, "L1_attn_rel_emb_k"), (extv, "L1_attn_rel_emb_v")):
                        rel = k.d[name]
                        sp.dma_start(ext[0:lo, :], rel[0:1, :].to_broadcast([lo, HD])).then_inc(s_ext, 16)
                        sp.dma_start(ext[lo:lo + NR, :], rel).then_inc(s_ext, 16)
                        sp.dma_start(ext[lo + NR:EXT, :], rel[NR - 1:NR, :].to_broadcast([EXT - lo - NR, HD])).then_inc(s_ext, 16)
                    sp.wait_ge(s_ext, 96)
                    for c in range(8):
                        sp.dma_start(ek[:, :, c, :], extk[7 - c:7 - c + W_RT, :].rearrange("(s p) d -> p s d", p=P)).then_inc(s_tab, 16)
                    sp.dma_start(tv[:, :, :].rearrange("p w d -> p (w d)"),
                                 bass.AP(extv.tensor, 0, [[HD, P], [1, W_TV * HD]])).then_inc(s_tab, 16)
                    for c in range(DC):
                        sp.wait_ge(s_ev, (N // 512) * (c + 1))
                        sp.dma_start(qd[c * P:(c + 1) * P, :], qT[:, c * N:(c + 1) * N]).then_inc(s_qd, 16)
                    sp.wait_ge(s_tab, 16 * 9)
                    sp.wait_ge(s_qd, 16 * DC)

                @block.tensor
                def _(pe):
                    pe.wait_ge(s_w, 48)
                    n = 0
                    for r in range(2 * DC):
                        for q in range(N // 512):
                            if n >= 4:
                                pe.wait_ge(s_ev, n - 3)
                            for c in range(DC):
                                last = nc.tensor.matmul(ps[:, n % 4, :], w[:, c, r * P:(r + 1) * P], xT[:, c, q * 512:(q + 1) * 512],
                                                        start=(c == 0), stop=(c == DC - 1))
                            last.then_inc(s_mm, 1)
                            n += 1
                    for t in range(NT):
                        if t >= 3:
                            pe.wait_ge(s_evv, t - 2)
                        for c in range(DC):
                            nc.tensor.matmul(ps[:, 4 + t % 3, 0:D], xT[:, c, t * P:(t + 1) * P], w[:, c, 2 * D:3 * D],
                                             start=(c == 0), stop=False)
                        nc.tensor.matmul(ps[:, 4 + t % 3, 0:D], k.c("ones", 1), bv[:, :], start=False, stop=True).then_inc(s_mmv, 1)
                    pe.wait_ge(s_tab, 16 * 9)
                    for z in range(4):
                        last = nc.tensor.transpose(ps[:, 7, z * P:(z + 1) * P], ek[:, z, :, :].rearrange("p c d -> p (c d)"), k.c("ident"))
                    last.then_inc(s_rt, 1)

                @block.scalar
                def _(act):
                    act.wait_ge(s_bq, 1)
                    n = 0
                    for r in range(2 * DC):
                        for q in range(N // 512):
                            act.wait_ge(s_mm, n + 1)
                            dst = qT if r < DC else kT
                            o = (r % DC) * N + q * 512
                            nc.scalar.activation(dst[:, o:o + 512], ps[:, n % 4, :], ACT.Identity, bias=bc[:, r:r + 1],
                                                 scale=(HD ** -0.5 if r < DC else 1.0)).then_inc(s_ev, 1)
                            n += 1

                @block.vector
                def _(dve):
                    dve.wait_ge(s_w, 48)
                    nc.vector.tensor_scalar(bc[:, 0:DC], bc[:, 0:DC], HD ** -0.5, None, ALU.mult).then_inc(s_bq, 1)
                    for t in range(NT):
                        dve.wait_ge(s_mmv, t + 1)
                        nc.vector.tensor_copy(v[:, t, :], ps[:, 4 + t % 3, 0:D]).then_inc(s_evv, 1)
                    dve.wait_ge(s_rt, 1)
                    nc.vector.tensor_copy(rt[:, :], ps[:, 7, :]).then_inc(s_rte, 1)

        def near(m):
            return max(0, min(KB - 2, (Q1 * m - R + 1) // P))

        groups, m0 = [], 0
        for m in range(1, TPB + 1):
            if m == TPB or near(m) != near(m0) or m == HALF:
                groups.append((m0, m - m0))
                m0 = m
        with ExitStack() as actx:
            qrep = k.sb("qrep", [P, 2, HG, S // 2], ctx=actx)
            kz = k.sb("kz", [P, 2, S], ctx=actx)
            vz = k.sb("vz", [P, 2, KB, P], ctx=actx)
            qbd = k.sb("qbd1", [P, 2, P], ctx=actx)
            qc = k.sb("qc1", [P, 2, 2 * P], ctx=actx)
            prob = k.sb("prob1", [P, 2, S], ctx=actx)
            probT = k.sb("probT1", [P, 2, S], ctx=actx)
            nmax = k.sb("nmax1", [P, 2], ctx=actx)
            rsum = k.sb("rsum1", [P, 2], ctx=actx)
            rinv = k.sb("rinv1", [P, 2], ctx=actx)
            om = k.sb("om1", [P, 2, P], ctx=actx)
            pv = k.sb("pv1", [P, D], ctx=actx)
            pvs = k.sb("pvs1", [P, HD], ctx=actx)
            osum = k.sb("osum1", [P, P], ctx=actx)
            sm = {n: k.sem("s_a1_" + n) for n in ("q", "s", "max", "exp", "tr", "evA", "evD", "o", "inv", "om", "c", "ctx",
                                                  "zone", "pv", "pvs", "os")}
            s_qr = [k.sem(f"s_qrep{n}") for n in range(2)]

            def steps(eng, body, lags, prologue=None):
                with eng.Fori(0, B) as b:
                    with eng.Fori(0, DC) as g:
                        bg = b * DC + g
                        if prologue:
                            prologue(b, g, bg)

                        def static(s):
                            def tile(lag):
                                m = s - lag
                                if m < 0 or m >= TPB:
                                    return None
                                return b, g, m, near(m), m % 2, bg * TPB + m
                            return tile
                        for m0, cnt in groups:
                            for m in range(m0, m0 + 4):
                                body(static(m))
                            if cnt > 4:
                                with eng.Fori(m0 // 2 + 2, (m0 + cnt) // 2) as i:
                                    for j in range(2):
                                        def tile(lag, i=i, j=j, m0=m0):
                                            m = 2 * i + j - lag
                                            return b, g, m, near(m0), (j - lag) % 2, bg * TPB + m
                                        body(tile)
                        for s in range(TPB, TPB + lags):
                            body(static(s))

            with nc.Block() as block:
                @block.sync
                def _(sp):
                    for n in range(4 * B):
                        b, g, h = n // 4, n // 2 % 2, n % 2
                        if n >= 2:
                            sp.wait_ge(sm["q"], HALF * (n - 1))
                        src = qd[g * P:(g + 1) * P, b * S + h * (S // 2):b * S + (h + 1) * (S // 2)].rearrange("(h d) t -> d h t", d=HD)
                        for c in range(8):
                            sp.dma_start(qrep[c * HD:(c + 1) * HD, h, :, :], src).then_inc(s_qr[h], 16)

                @block.gpsimd
                def _(pool):
                    def body(tile):
                        if tile(0) is None:
                            return
                        b, g, m, nb, j, t = tile(0)
                        if isinstance(m, int) and m % HALF == 0:
                            pool.wait_ge(s_qr[m // HALF], 128 * (b * DC + g) + 128)
                        half = (m // HALF) if isinstance(m, int) else halves[0]
                        halves[0] = half
                        pool.wait_ge(sm["s"], t + 1)
                        nc.gpsimd.tensor_tensor(
                            qbd[:, j, :].rearrange("p (h i) -> p h i", h=HG),
                            qT[:, bass.ds(g * N + b * S + m * Q1, Q1)].unsqueeze(1).to_broadcast([P, HG, Q1]),
                            k.c("hmask").unsqueeze(2).to_broadcast([P, HG, Q1]), ALU.mult)
                        nc.gpsimd.tensor_tensor(
                            qc[:, j, :].rearrange("p (e h i) -> p e h i", e=2, h=HG),
                            qrep[:, half, :, bass.ds(m * Q1 - half * (S // 2), Q1)].unsqueeze(1).to_broadcast([P, 2, HG, Q1]),
                            k.c("cmask").rearrange("p (e i) -> p e i", e=2).unsqueeze(2).to_broadcast([P, 2, HG, Q1]),
                            ALU.mult).then_inc(sm["q"], 1)
                    halves = [0]
                    steps(pool, body, 0)

                @block.tensor
                def _(pe):
                    pe.sem_inc(sm["s"], 2)

                    def scores(tile):
                        b, g, m, nb, j, t = tile
                        pe.wait_ge(sm["q"], t + 1)
                        pe.wait_ge(sm["exp"], t + 1)
                        bank = ps[:, 2 * j:2 * j + 2, :].rearrange("p a n -> p (a n)")
                        w0 = nb * P - m * Q1 + O_RT
                        nc.tensor.matmul(bank[:, 0:2 * P], qbd[:, j, :], kT[:, bass.ds(g * N + b * S + nb * P, 2 * P)],
                                         start=True, stop=False, skip_group_check=True)
                        for e in range(2):
                            last = nc.tensor.matmul(bank[:, 0:2 * P], qc[:, j, e * P:(e + 1) * P], rt[:, bass.ds(w0 - 8 * e, 2 * P)],
                                                    start=False, stop=(e == 1), skip_group_check=True)
                        cut = (2 + nb) * P
                        for lo, hi in ((2 * P, 512), (512, S)):
                            first = lo == 512
                            for a, z, zone, shift in ((lo, min(hi, cut), 0, 2 * P), (max(lo, cut), hi, 1, 0)):
                                if a < z:
                                    last = nc.tensor.matmul(bank[:, a:z], qbd[:, j, :], kz[:, zone, a - shift:z - shift],
                                                            start=first, stop=True, skip_group_check=True)
                                    first = False
                        last.then_inc(sm["s"], 1)

                    def body(tile):
                        if tile(0):
                            scores(tile(0))
                        if tile(1):
                            b, g, m, nb, j, t = tile(1)
                            pe.wait_ge(sm["exp"], t + 3)
                            pe.wait_ge(sm["evA"], t + 1)
                            for kb in range(KB):
                                if kb == 4:
                                    pe.wait_ge(sm["evD"], t + 1)
                                last = nc.tensor.transpose(ps[:, 4 + kb // 4, (kb % 4) * P:(kb % 4) * P + P],
                                                           prob[:, j, kb * P:(kb + 1) * P], k.c("ident"))
                            last.then_inc(sm["tr"], 1)
                        if tile(2):
                            b, g, m, nb, j, t = tile(2)
                            pe.wait_ge(sm["evA"], t + 2)
                            pe.wait_ge(sm["evD"], t + 2)
                            pe.wait_ge(sm["os"], t + 1)
                            for p in range(KB):
                                if p < 2:
                                    rhs = v[:, bass.ds(b * KB + nb + p, 1), bass.ds(g * P, P)].rearrange("p a n -> p (a n)")
                                elif p - 2 < nb:
                                    rhs = vz[:, 0, p - 2, :]
                                else:
                                    rhs = vz[:, 1, p, :]
                                nc.tensor.matmul(ps[:, 6, 0:P], probT[:, j, p * P:(p + 1) * P], rhs, start=(p == 0), stop=(p == KB - 1))
                            for p in range(2):
                                w0 = (nb + p) * P - m * Q1 - (Q1 - 1) + O_TV
                                last = nc.tensor.matmul(ps[:, 6, P:P + D], probT[:, j, p * P:(p + 1) * P],
                                                        tv[:, bass.ds(w0, Q1), :].rearrange("p w d -> p (w d)"),
                                                        start=(p == 0), stop=(p == 1))
                            last.then_inc(sm["o"], 1)
                        if tile(3):
                            b, g, m, nb, j, t = tile(3)
                            pe.wait_ge(sm["om"], t + 3)
                            pe.wait_ge(sm["ctx"], t + 1)
                            nc.tensor.matmul(ps[:, 7, 0:Q1], om[:, j, :], k.c("sum1"), start=True, stop=True).then_inc(sm["c"], 1)

                    def prologue(b, g, bg):
                        pe.wait_ge(sm["zone"], 4 * bg + 4)
                    steps(pe, body, 3, prologue)

                @block.vector
                def _(dve):
                    dve.sem_inc(sm["evD"], 1)
                    dve.sem_inc(sm["om"], 2)
                    dve.sem_inc(sm["os"], 1)
                    dve.sem_inc(sm["inv"], 2)
                    dve.sem_inc(sm["ctx"], 1)

                    def prologue(b, g, bg):
                        for z, col in ((0, 0), (1, W_RT - 1)):
                            nc.vector.tensor_scalar(kz[:, z, :], kT[:, bass.ds(g * N + b * S, S)], rt[:, col:col + 1], None,
                                                    ALU.add).then_inc(sm["zone"], 1)
                        for z, col in ((0, 0), (1, W_TV - 1)):
                            nc.vector.tensor_tensor(
                                vz[:, z, :, :].rearrange("p t (h d) -> p t h d", h=HG),
                                v[:, bass.ds(b * KB, KB), bass.ds(g * P, P)].rearrange("p t (h d) -> p t h d", h=HG),
                                tv[:, col, :].unsqueeze(1).unsqueeze(1).to_broadcast([P, KB, HG, HD]), ALU.add).then_inc(sm["zone"], 1)

                    def body(tile):
                        if tile(0):
                            b, g, m, nb, j, t = tile(0)
                            dve.wait_ge(sm["s"], t + 3)
                            nc.vector.tensor_reduce(nmax[:, j:j + 1], ps[:, 2 * j:2 * j + 2, :].rearrange("p a n -> p (a n)"),
                                                    AX.X, ALU.max, negate=True).then_inc(sm["max"], 1)
                        if tile(1):
                            b, g, m, nb, j, t = tile(1)
                            dve.wait_ge(sm["tr"], t + 1)
                            nc.vector.tensor_copy(probT[:, j, 512:S], ps[:, 5, :]).then_inc(sm["evD"], 1)
                            dve.wait_ge(sm["om"], t + 1)
                            nc.vector.reciprocal(rinv[:, j:j + 1], rsum[:, j:j + 1]).then_inc(sm["inv"], 1)
                        if tile(2):
                            b, g, m, nb, j, t = tile(2)
                            dve.wait_ge(sm["o"], t + 1)
                            dve.wait_ge(sm["pvs"], t + 1)
                            nc.vector.tensor_tensor(pv[:, :].rearrange("p (c d) -> p c d", d=HD),
                                                    ps[:, 6, P:P + D].rearrange("p (c d) -> p c d", d=HD),
                                                    k.c("diag1").unsqueeze(2).to_broadcast([P, Q1, HD]), ALU.mult).then_inc(sm["pv"], 1)
                            dve.wait_ge(sm["pv"], t + 1)
                            dve.wait_ge(sm["os"], t + 1)
                            nc.vector.tensor_reduce(pvs[:, :], pv[:, :].rearrange("p (c d) -> p d c", d=HD), AX.X,
                                                    ALU.add).then_inc(sm["pvs"], 1)
                            dve.wait_ge(sm["pvs"], t + 2)
                            dve.wait_ge(sm["om"], t + 2)
                            nc.vector.tensor_tensor(osum[:, :].rearrange("p (h d) -> p h d", h=HG),
                                                    ps[:, 6, 0:P].rearrange("p (h d) -> p h d", h=HG),
                                                    pvs[:, :].unsqueeze(1).to_broadcast([P, HG, HD]), ALU.add).then_inc(sm["os"], 1)
                            dve.wait_ge(sm["os"], t + 2)
                            dve.wait_ge(sm["inv"], t + 3)
                            nc.vector.scalar_tensor_tensor(om[:, j, :], osum[:, :], rinv[:, j:j + 1], k.c("head1"),
                                                           ALU.mult, ALU.mult).then_inc(sm["om"], 1)
                        if tile(3):
                            b, g, m, nb, j, t = tile(3)
                            dve.wait_ge(sm["c"], t + 1)
                            nc.vector.tensor_copy(xTf[:, bass.ds(g * N + b * S + m * Q1, Q1)], ps[:, 7, 0:Q1]).then_inc(sm["ctx"], 1)
                    xTf = xT[:, :, :].rearrange("p c n -> p (c n)")
                    dve.sem_inc(sm["pvs"], 1)
                    steps(dve, body, 3, prologue)

                @block.scalar
                def _(act):
                    act.sem_inc(sm["exp"], 2)
                    act.sem_inc(sm["evA"], 1)

                    def body(tile):
                        if tile(0):
                            b, g, m, nb, j, t = tile(0)
                            act.wait_ge(sm["max"], t + 1)
                            act.wait_ge(sm["inv"], t + 1)
                            nc.scalar.activation(prob[:, j, :], ps[:, 2 * j:2 * j + 2, :].rearrange("p a n -> p (a n)"), ACT.Exp,
                                                 bias=nmax[:, j:j + 1], accum_out=rsum[:, j:j + 1]).then_inc(sm["exp"], 1)
                        if tile(1):
                            b, g, m, nb, j, t = tile(1)
                            act.wait_ge(sm["tr"], t + 1)
                            nc.scalar.activation(probT[:, j, 0:512], ps[:, 4, :], ACT.Copy).then_inc(sm["evA"], 1)
                    steps(act, body, 1)

        project_out(k, "1", "L1_attn_W_out", "L1_attn_b_out")


def cross_attention1(k):
    nc, ps, xT = k.nc, k.ps, k.xT
    with ExitStack() as ctx:
        wq = k.sb("xwq", [P, DC, D], ctx=ctx)
        wkv = k.sb("xwkv", [P, DC, 2 * D], ctx=ctx)
        wqT = k.sb("xwqT", [P, DC, D], ctx=ctx)
        kT = k.sb("xkT", [P, B, DC, SC], ctx=ctx)
        aT1 = k.sb("xaT1", [P, B, DC, SC], ctx=ctx)
        v = k.sb("xv", [SC, B, D], ctx=ctx)
        mx = k.sb("xmx", [P, NT], ctx=ctx)
        sc = k.sb("xsc", [P, NT, SC], ctx=ctx)
        pT = k.sb("xpT", [SC, NT, P], ctx=ctx)
        s_w, s_t, s_te, s_k, s_ke, s_a, s_ae, s_sc, s_ch, s_ein, s_e, s_at, s_ate, s_o, s_x = (
            k.sem("s_x1_" + n) for n in ("w", "t", "te", "k", "ke", "a", "ae", "sc", "ch", "ein", "e", "at", "ate", "o", "x"))

        def rows(r):
            return r.unsqueeze(2).to_broadcast([P, NT, SC])

        with nc.Block() as block:
            @block.sync
            def _(sp):
                sp.dma_start(wq[:, :, :], k.d["L1_xattn_Wq"].rearrange("(c p) n -> p c n", p=P)).then_inc(s_w, 16)
                sp.dma_start(wkv[:, :, :], k.d["L1_xattn_Wkv"].rearrange("(c p) n -> p c n", p=P)).then_inc(s_w, 16)

            @block.tensor
            def _(pe):
                pe.wait_ge(s_w, 32)
                for q in range(DC):
                    for c in range(DC):
                        last = nc.tensor.transpose(ps[:, 0, (q * DC + c) * P:(q * DC + c + 1) * P], wq[:, c, q * P:(q + 1) * P], k.c("ident"))
                last.then_inc(s_t, 1)
                for b in range(B):
                    for e in range(DC):
                        for c in range(DC):
                            nc.tensor.matmul(ps[:, 1, (b * DC + e) * P:(b * DC + e) * P + SC], wkv[:, c, e * P:(e + 1) * P],
                                             k.ctxT[:, b, c, :], start=(c == 0), stop=(c == DC - 1))
                    for c in range(DC):
                        last = nc.tensor.matmul(ps[0:SC, 2, b * D:(b + 1) * D], k.ctxT[:, b, c, :], wkv[:, c, D:2 * D],
                                                start=(c == 0), stop=(c == DC - 1))
                last.then_inc(s_k, 1)
                pe.wait_ge(s_ke, 1)
                for b in range(B):
                    for c in range(DC):
                        for e in range(DC):
                            last = nc.tensor.matmul(ps[:, 3, (b * DC + c) * P:(b * DC + c) * P + SC], wqT[:, e, c * P:(c + 1) * P],
                                                    kT[:, b, e, :], start=(e == 0), stop=(e == DC - 1))
                last.then_inc(s_a, 1)
                pe.wait_ge(s_ae, 1)
                for t in range(NT):
                    for c in range(DC):
                        last = nc.tensor.matmul(ps[:, 4 + t // 4, (t % 4) * P:(t % 4) * P + SC], xT[:, c, t * P:(t + 1) * P],
                                                aT1[:, t // KB, c, :], start=(c == 0), stop=(c == DC - 1))
                    if t % 4 == 3:
                        last.then_inc(s_sc, 1)
                pe.wait_ge(s_e, 1)
                for g in range(4):
                    for t in range(4 * g, 4 * g + 4):
                        last = nc.tensor.transpose(ps[0:SC, g, (t % 4) * P:(t % 4 + 1) * P], sc[:, t, :], k.c("ident"))
                    last.then_inc(s_at, 1)
                for t in range(NT):
                    if t % 4 == 0:
                        pe.wait_ge(s_ate, t // 4 + 1)
                    if t >= 2:
                        pe.wait_ge(s_x, t - 1)
                    nc.tensor.matmul(ps[:, 4 + t % 2, 0:D], pT[:, t, :], v[:, t // KB, :], start=True, stop=True).then_inc(s_o, 1)

            @block.scalar
            def _(act):
                act.wait_ge(s_ein, 1)
                nc.scalar.activation(sc[:, :, :], sc[:, :, :], ACT.Exp).then_inc(s_e, 1)
                for g in range(4):
                    act.wait_ge(s_at, g + 1)
                    nc.scalar.activation(pT[:, 4 * g:4 * g + 4, :], ps[0:SC, g, :].rearrange("p (t n) -> p t n", t=4),
                                         ACT.Copy).then_inc(s_ate, 1)

            @block.vector
            def _(dve):
                link = Chain(dve, s_ch)
                dve.wait_ge(s_t, 1)
                nc.vector.tensor_copy(wqT[:, :, :], ps[:, 0, :].rearrange("p (q c) -> p q c", q=DC))
                dve.wait_ge(s_k, 1)
                nc.vector.tensor_copy(v[:, :, :], ps[0:SC, 2, :].rearrange("p (b d) -> p b d", b=B))
                nc.vector.tensor_copy(kT[:, :, :, :].rearrange("p b c j -> p (b c) j"),
                                      ps[:, 1, :].rearrange("p (bc n) -> p bc n", n=P)[:, :, 0:SC]).then_inc(s_ke, 1)
                dve.wait_ge(s_a, 1)
                nc.vector.tensor_scalar(aT1[:, :, :, :].rearrange("p b c j -> p (b c) j"),
                                        ps[:, 3, :].rearrange("p (bc n) -> p bc n", n=P)[:, :, 0:SC],
                                        float(D) ** -0.5, None, ALU.mult).then_inc(s_ae, 1)
                for g in range(4):
                    dve.wait_ge(s_sc, g + 1)
                    link(nc.vector.tensor_copy(sc[:, 4 * g:4 * g + 4, :],
                                               ps[:, 4 + g, :].rearrange("p (t n) -> p t n", t=4)[:, :, 0:SC]))
                link(nc.vector.tensor_reduce(mx[:, :], sc[:, :, :], AX.X, ALU.max))
                nc.vector.tensor_tensor(sc[:, :, :], sc[:, :, :], rows(mx[:, :]), ALU.subtract).then_inc(s_ein, 1)
                dve.wait_ge(s_e, 1)
                link(nc.vector.tensor_reduce(mx[:, :], sc[:, :, :], AX.X, ALU.add))
                link(nc.vector.reciprocal(mx[:, :], mx[:, :]))
                for t in range(NT):
                    dve.wait_ge(s_o, t + 1)
                    nc.vector.scalar_tensor_tensor(k.x[:, t, :], ps[:, 4 + t % 2, 0:D], mx[:, t:t + 1], k.x[:, t, :],
                                                   ALU.mult, ALU.add).then_inc(s_x, 1)


def moe1(k):
    nc, ps, xT = k.nc, k.ps, k.xT
    T1 = NF1 // P
    FC1 = F1 // P
    LIMIT, ALPHA = 7.0, 1.702
    norm_transpose(k, "1c", tiles=T1)
    with ExitStack() as ctx:
        gu = k.sb("gu", [P, 2, DC, 2 * F1], ctx=ctx)
        dn = k.sb("dn", [P, 2, FC1, D], ctx=ctx)
        gub = k.sb("gub", [E, 2 * F1], ctx=ctx)
        gubT = k.sb("gubT", [P, FC1, 2, E], ctx=ctx)
        dnb = k.sb("dnb", [1, E, D], ctx=ctx)
        idx = k.sb("ridx", [P, T1, 2], I32, ctx=ctx)
        idf = k.sb("ridf", [P, T1, 2], ctx=ctx)
        rw = k.sb("rw", [P, T1, E], ctx=ctx)
        cw = k.sb("rcw", [P, T1, E], ctx=ctx)
        oh = k.sb("roh", [P, T1, E], ctx=ctx)
        g1 = k.sb("g1", [P, NF1], ctx=ctx)
        sg = k.sb("sg1", [P, NF1], ctx=ctx)
        u1 = k.sb("u1", [P, NF1], ctx=ctx)
        hT = k.sb("hT1", [P, 2, FC1, NF1], ctx=ctx)
        s_in, s_bt, s_bte, s_ch, s_gu, s_g1, s_sg, s_hT, s_dn, s_acc = (
            k.sem("s_m1_" + n) for n in ("in", "bt", "bte", "ch", "gu", "g1", "sg", "hT", "dn", "acc"))
        s_wgu = [k.sem(f"s_wgu{j}") for j in range(2)]
        s_wdn = [k.sem(f"s_wdn{j}") for j in range(2)]
        with nc.Block() as block:
            @block.sync
            def _(sp):
                sp.dma_start(gub[:, :], k.d["L1_ffn_gate_up_proj_bias"]).then_inc(s_in, 16)
                sp.dma_start(dnb[:, :, :], k.d["L1_ffn_down_proj_bias"].rearrange("(a e) d -> a e d", a=1)).then_inc(s_in, 16)
                sp.dma_start(idx[:, :, :], k.d["L1_ffn_router_indices"].rearrange("(t p) k -> p t k", p=P)).then_inc(s_in, 16)
                sp.dma_start(rw[:, :, :], k.d["L1_ffn_routing_weights"].rearrange("(t p) e -> p t e", p=P)).then_inc(s_in, 16)
                for e in range(E):
                    if e >= 2:
                        sp.wait_ge(s_gu, FC1 * (e - 1))
                    sp.dma_start(gu[:, e % 2, :, :], k.d["L1_ffn_gate_up_proj"][e].rearrange("(c p) f -> p c f", p=P)).then_inc(s_wgu[e % 2], 16)
                    if e >= 2:
                        sp.wait_ge(s_dn, e - 1)
                    sp.dma_start(dn[:, e % 2, :, :], k.d["L1_ffn_down_proj"][e].rearrange("(c p) d -> p c d", p=P)).then_inc(s_wdn[e % 2], 16)

            @block.tensor
            def _(pe):
                pe.wait_ge(s_in, 64)
                for c in range(FC1):
                    for z in range(2):
                        o = c * 2 * P + z
                        last = nc.tensor.transpose(ps[:, 7, (2 * c + z) * E:(2 * c + z + 1) * E], gub[:, o:o + 2 * P - 1:2],
                                                   k.c("ident", E)[:, 0:E])
                last.then_inc(s_bt, 1)

                def gate_up(j, e, i):
                    pe.wait_ge(s_wgu[j], 16 * i + 16)
                    for c in range(FC1):
                        pe.wait_ge(s_hT, FC1 * e + c + 1)
                        for z in range(2):
                            o = c * 2 * P + z
                            for q in range(DC):
                                last = nc.tensor.matmul(ps[:, 2 * c + z, :], gu[:, j, q, o:o + 2 * P - 1:2], xT[:, q, 0:NF1],
                                                        start=(q == 0), stop=(q == DC - 1))
                        last.then_inc(s_gu, 1)

                def down(j, e, i, bias):
                    pe.wait_ge(s_wdn[j], 16 * i + 16)
                    pe.wait_ge(s_hT, FC1 * e + 4)
                    pe.wait_ge(s_acc, T1 * e + 4)
                    for t in range(T1):
                        for c in range(FC1):
                            nc.tensor.matmul(ps[:, 4 + t // 2, (t % 2) * D:(t % 2 + 1) * D], hT[:, j, c, t * P:(t + 1) * P],
                                             dn[:, j, c, :], start=(c == 0), stop=False)
                        last = nc.tensor.matmul(ps[:, 4 + t // 2, (t % 2) * D:(t % 2 + 1) * D], k.c("ones", 1), bias,
                                                start=False, stop=True)
                    last.then_inc(s_dn, 1)

                gate_up(0, 0, 0)
                with pe.Fori(0, E // 2 - 1) as i:
                    for j in range(2):
                        e = 2 * i + j
                        gate_up(1 - j, e + 1, i + j)
                        down(j, e, i, dnb[:, bass.ds(e, 1), :].rearrange("p a d -> p (a d)"))
                gate_up(1, E - 1, E // 2 - 1)
                down(0, E - 2, E // 2 - 1, dnb[:, E - 2, :])
                down(1, E - 1, E // 2 - 1, dnb[:, E - 1, :])

            @block.scalar
            def _(act):
                with act.Fori(0, FC1 * E) as n:
                    act.wait_ge(s_g1, n + 1)
                    nc.scalar.activation(sg[:, :], g1[:, :], ACT.Sigmoid, scale=ALPHA).then_inc(s_sg, 1)

            @block.vector
            def _(dve):
                link = Chain(dve, s_ch)
                dve.sem_inc(s_hT, 2)
                dve.sem_inc(s_acc, 4)
                dve.wait_ge(s_in, 64)
                iota = k.c("iota8").unsqueeze(1).to_broadcast([P, T1, E])
                link(nc.vector.tensor_copy(idf[:, :, :], idx[:, :, :]))
                link(nc.vector.tensor_tensor(cw[:, :, :], iota, idf[:, :, 0:1].to_broadcast([P, T1, E]), ALU.is_equal))
                link(nc.vector.tensor_tensor(oh[:, :, :], iota, idf[:, :, 1:2].to_broadcast([P, T1, E]), ALU.is_equal))
                link(nc.vector.tensor_tensor(cw[:, :, :], cw[:, :, :], oh[:, :, :], ALU.add))
                link(nc.vector.tensor_tensor(cw[:, :, :], cw[:, :, :], rw[:, :, :], ALU.mult))
                dve.wait_ge(s_bt, 1)
                link(nc.vector.tensor_copy(gubT[:, :, :, :].rearrange("p c z e -> p (c z e)"), ps[:, 7, 0:2 * FC1 * E]))

                for e in range(E + 1):
                    if e < E:
                        for c in range(FC1):
                            dve.wait_ge(s_gu, FC1 * e + c + 1)
                            nc.vector.tensor_scalar(g1[:, :], ps[:, 2 * c, :], gubT[:, c, 0, e:e + 1], LIMIT,
                                                    ALU.add, ALU.min).then_inc(s_g1, 1)
                            link(nc.vector.tensor_scalar(u1[:, :], ps[:, 2 * c + 1, :], gubT[:, c, 1, e:e + 1], LIMIT,
                                                         ALU.add, ALU.min))
                            link(nc.vector.tensor_scalar(u1[:, :], u1[:, :], -LIMIT, 1.0, ALU.max, ALU.add))
                            dve.wait_ge(s_sg, FC1 * e + c + 1)
                            link(nc.vector.tensor_tensor(sg[:, :], g1[:, :], sg[:, :], ALU.mult))
                            nc.vector.tensor_tensor(hT[:, e % 2, c, :], u1[:, :], sg[:, :], ALU.mult).then_inc(s_hT, 1)
                            dve.wait_ge(s_hT, FC1 * e + c + 3)
                    if e:
                        dve.wait_ge(s_dn, e)
                        for t in range(T1):
                            nc.vector.scalar_tensor_tensor(k.x[:, t, :], ps[:, 4 + t // 2, (t % 2) * D:(t % 2 + 1) * D],
                                                           cw[:, t, e - 1:e], k.x[:, t, :], ALU.mult, ALU.add).then_inc(s_acc, 1)


def store(k):
    nc = k.nc
    s_out = k.sem("s_out")
    with nc.Block() as block:
        @block.sync
        def _(sp):
            sp.dma_start(k.d["out"].rearrange("b (t p) d -> p (b t) d", p=P), k.x[:, :, :]).then_inc(s_out, 16)
            sp.wait_ge(s_out, 16)


def decoder(nc, dram):
    with ExitStack() as ctx:
        k = Prog(nc, ctx, dram)
        load_inputs(k)
        norm_transpose(k, "0a", attn0=True)
        attention0(k)
        k.end_stage()
        context_prep(k)
        norm_transpose(k, "0b")
        cross_attention0(k)
        k.end_stage()
        moe0(k)
        k.end_stage()
        norm_transpose(k, "1a")
        attention1(k)
        k.end_stage()
        norm_transpose(k, "1b")
        cross_attention1(k)
        k.end_stage()
        moe1(k)
        store(k)


_INS = ['x', 'ctx_1024', 'L0_attn_w_q', 'L0_attn_w_k', 'L0_attn_w_v', 'L0_attn_w_o', 'L0_attn_norm_w',
        'L0_xattn_W_a', 'L0_xattn_W_p', 'L0_xattn_V_p', 'L0_ffn_gate_w', 'L0_ffn_w1', 'L0_ffn_w2', 'L0_ffn_w3',
        'L1_attn_W_qkv', 'L1_attn_b_qkv', 'L1_attn_W_out', 'L1_attn_b_out', 'L1_attn_rel_emb_k',
        'L1_attn_rel_emb_v', 'L1_xattn_Wq', 'L1_xattn_Wkv', 'L1_ffn_router_indices', 'L1_ffn_routing_weights',
        'L1_ffn_gate_up_proj', 'L1_ffn_gate_up_proj_bias', 'L1_ffn_down_proj', 'L1_ffn_down_proj_bias']


def shape_constants():
    import numpy as np
    c = np.zeros((P, CW), np.float32)

    def put(name, a):
        lo, hi = Consts.at(name)
        c[:a.shape[0], lo:hi] = a
    p = np.arange(P)[:, None]
    put("ident", np.eye(P))
    put("causal", np.where(np.arange(256)[None, :] - 120 <= p % Q0, 0.0, NEG))
    put("head0", (p // Q0 == np.arange(D)[None, :] // HD))
    put("sum0", (p % Q0 == np.arange(Q0)[None, :]))
    put("hmask", (p // HD == np.arange(HG)[None, :]))
    i = np.arange(2 * Q1)[None, :]
    put("cmask", (i % Q1 == 8 * (i // Q1) + p // HD))
    put("head1", (p // Q1 == np.arange(P)[None, :] // HD))
    put("diag1", (Q1 - 1 - np.arange(Q1)[None, :] == p % Q1))
    put("sum1", (p % Q1 == np.arange(Q1)[None, :]))
    put("tri", (p <= np.arange(P)[None, :]))
    put("ones", np.ones((P, P)))
    put("iota8", np.arange(E)[None, :] + 0 * p)
    put("iota77", np.arange(SC)[None, :] + 0 * p)
    put("cap0", np.arange(E)[None, :] * 2 * CAP + 0 * p)
    put("spare", E * 2 * CAP + p)
    f = np.float32
    d = np.arange(HD)
    theta = np.power(f(10000.0), f(-2.0) * (d // 2).astype(f) / f(HD)).astype(f)
    pos = np.arange(S, dtype=f)
    ang = (pos[:, None] * theta[None, :]).astype(f)
    rf = np.cos(ang) + np.sin(ang) * np.where(np.arange(S) % 2 == 0, f(-1.0), f(1.0))[:, None]
    put("rope", np.tile(rf.T.astype(f), (8, 1)))
    return c


def kernel(**inputs):
    import numpy as np
    import concourse.bacc as bacc
    from concourse.bass_utils import run_bass_kernel_spmd

    nc = bacc.Bacc("TRN2", target_bir_lowering=False, num_devices=1)
    arrays, dram = {}, {}
    for name in _INS:
        a = np.ascontiguousarray(inputs[name])
        arrays[f"in_{name}"] = a
        dram[name] = nc.dram_tensor(f"in_{name}", a.shape, mybir.dt.from_np(a.dtype), kind="ExternalInput").ap()
    arrays["in_consts"] = shape_constants()
    dram["consts"] = nc.dram_tensor("in_consts", (P, CW), F32, kind="ExternalInput").ap()
    dram["out"] = nc.dram_tensor("out_0", (B, S, D), F32, kind="ExternalOutput").ap()
    decoder(nc, dram)
    r = run_bass_kernel_spmd(nc, [arrays], core_ids=[0])
    return r.results[0]["out_0"]
```

```python
from contextlib import ExitStack

import concourse.bass as bass
from concourse import mybir

F32 = mybir.dt.float32
BF16 = mybir.dt.bfloat16
I32 = mybir.dt.int32
U32 = mybir.dt.uint32
ALU = mybir.AluOpType
ACT = mybir.ActivationFunctionType
AX = mybir.AxisListType

P = 128
B, S, D = 2, 1024, 256
N = B * S
NT = N // P
DC = D // P
H, HD = 16, 16
KVH = 4
REP = H // KVH
KB = S // P
HG = P // HD
NH = B * H
NTILE = NH * KB
PERIOD = 2 * KB
R = 64
NR = 2 * R + 1
SC = 77
PH = 100
WIN = 2
E = 8
F0 = 896
FC0 = F0 // P
CAP = int(S * 2 / E * 1.25)
F1 = 256
NF1 = 512
Q_PARTS = (0, 0, 0, 1, 1, 2)
K_PARTS = (0, 1, 2, 0, 1, 0)
TERMS = len(Q_PARTS)
KS = TERMS * HD
LN_EPS = 1e-5
RMS_EPS = 1.1920929e-07
NEG = -1e30


class Consts:
    WIDTHS = dict(ident=P, causal=P, late=P, tri=P, ones=P, iota8=E, iota77=SC, cap0=E, spare=1, rope=S)

    @classmethod
    def at(cls, name):
        c = 0
        for k, w in cls.WIDTHS.items():
            if k == name:
                return c, c + w
            c += w
        return c, c


CW = Consts.at("")[0]


class Chain:

    def __init__(self, eng, sem):
        self.eng, self.sem, self.n, self.off = eng, sem, 0, 0

    def __call__(self, ins):
        self.n += 1
        ins.then_inc(self.sem, 1)
        self.eng.wait_ge(self.sem, self.off + self.n)

    def enter(self, i, per, start=0):
        self.off = (i - start) * per
        self.n0, self.per = self.n, per

    def leave(self, count):
        assert self.n - self.n0 == self.per, (self.n - self.n0, self.per)
        self.off = 0
        self.n = self.n0 + self.per * count


class Prog:

    def __init__(self, nc, ctx, dram):
        self.nc, self.ctx, self.d = nc, ctx, dram
        self.x = self.sb("x", [P, NT, D])
        self.xT = self.sb("xT", [P, DC, N])
        self.cst = self.sb("cst", [P, CW])
        self.mean_var = self.sb("mean_var", [P, NT, 2])
        self.rstd = self.sb("rstd", [P, NT])
        self.rms = self.sb("rms", [P, NT])
        self.ps = ctx.enter_context(nc.psum_tensor("ps", [P, 8, 512], F32))
        self.ctxn = self.sb("ctxn", [SC, B, D])
        self.ctxT = self.sb("ctxT", [P, B, DC, SC])
        self.gT = self.sb("gT", [P, B, DC, SC])
        self.wpT = self.sb("wpT", [P, DC, PH])
        self.vp = self.sb("vp", [PH, 1])
        self.sems = []
        self.relk = self.sb("relk", [KS, P + 1], BF16)
        self.relv = self.sb("relv", [P, 2, HD])
        self.skew_u = nc.dram_tensor("skew_u", (KB, P, 2 * P), F32, kind="Internal").ap()
        self.skew_p = nc.dram_tensor("skew_p", (KB, P, 2 * P), F32, kind="Internal").ap()
        self.disp = nc.dram_tensor("disp", ((E + 1) * 2 * CAP, D), F32, kind="Internal").ap()

    def sb(self, name, shape, dt=F32, ctx=None):
        return (ctx or self.ctx).enter_context(self.nc.sbuf_tensor(name, shape, dt))

    def sem(self, name):
        self.sems.append(self.nc.alloc_semaphore(name=name))
        return self.sems[-1]

    def end_stage(self):
        self.nc.clear_and_free_semaphores(self.sems)
        self.nc.all_engine_barrier()
        self.sems = []

    def c(self, name, rows=P):
        a, b = Consts.at(name)
        return self.cst[0:rows, a:b]


def norm_rms_transpose(k, tag):
    nc = k.nc
    tiles = NT
    x, xT, mv, ps = k.x, k.xT, k.mean_var, k.ps
    with ExitStack() as ctx:
        stats = k.sb(f"stats{tag}", [P, NT, 6], ctx=ctx)
        xs = k.sb(f"xs{tag}", [P, 2, D], ctx=ctx)
        xn = k.sb(f"xn{tag}", [P, 2, D], ctx=ctx)
        nw = k.sb(f"nw{tag}", [P, DC], ctx=ctx)
        s_chain = k.sem(f"s_nchain{tag}")
        s_w = k.sem(f"s_nw{tag}")
        s_var = k.sem(f"s_var{tag}")
        s_sd = k.sem(f"s_sd{tag}")
        s_xs = k.sem(f"s_xs{tag}")
        s_tr = k.sem(f"s_tr{tag}")
        s_xt = k.sem(f"s_xt{tag}")
        with nc.Block() as block:
            @block.sync
            def _(sp):
                sp.dma_start(nw[:, :], k.d["L0_attn_norm_w"].rearrange("(c p) -> p c", p=P),
                             allow_slow_non_contiguous=True).then_inc(s_w, 16)

            @block.vector
            def _(dve):
                link = Chain(dve, s_chain)
                with dve.Fori(0, tiles) as t:
                    last = nc.vector.bn_stats(stats[:, bass.ds(t, 1), :], x[:, bass.ds(t, 1), :])
                    last.then_inc(s_chain, 1)
                link.n += tiles
                dve.wait_ge(s_chain, link.n)
                for t in range(tiles):
                    nc.vector.bn_aggr(mv[:, t, :], stats[:, t, :]).then_inc(s_chain, 1)
                link.n += tiles
                dve.wait_ge(s_chain, link.n)
                nc.vector.tensor_scalar(k.rstd[:, 0:tiles], mv[:, 0:tiles, 1], LN_EPS, None, ALU.add).then_inc(s_var, 1)
                dve.wait_ge(s_sd, 1)
                link(nc.vector.reciprocal(k.rstd[:, 0:tiles], k.rstd[:, 0:tiles]))
                link(nc.vector.tensor_tensor(k.rms[:, :], k.rstd[:, :], k.rstd[:, :], ALU.mult))
                link(nc.vector.tensor_tensor(k.rms[:, :], k.rms[:, :], mv[:, :, 1], ALU.mult))
                nc.vector.tensor_scalar(k.rms[:, :], k.rms[:, :], RMS_EPS, None, ALU.add).then_inc(s_var, 1)
                dve.wait_ge(s_sd, 2)
                link(nc.vector.reciprocal(k.rms[:, :], k.rms[:, :]))
                link(nc.vector.tensor_tensor(k.rms[:, :], k.rms[:, :], k.rstd[:, :], ALU.mult))
                with dve.Fori(0, tiles // 2) as i:
                    link.enter(i, 4)
                    for j in range(2):
                        t = 2 * i + j
                        xt = x[:, bass.ds(t, 1), :].rearrange("p a d -> p (a d)")
                        mean = mv[:, bass.ds(t, 1), 0:1].rearrange("p a b -> p (a b)")
                        rstd = k.rstd[:, bass.ds(t, 1)]
                        dve.wait_ge(s_tr, t + 1)
                        rms = k.rms[:, bass.ds(t, 1)]
                        link(nc.vector.tensor_scalar(xn[:, j, :], xt, mean, rstd, ALU.subtract, ALU.mult))
                        nc.vector.tensor_scalar(xs[:, j, :], xt, mean, rms, ALU.subtract, ALU.mult).then_inc(s_xs, 1)
                        dve.wait_ge(s_xs, t + 1)
                        link(nc.vector.tensor_tensor(xt, xt, xn[:, j, :], ALU.add))
                link.leave(tiles // 2)

            @block.tensor
            def _(pe):
                pe.sem_inc(s_tr, 2)
                with pe.Fori(0, tiles // 2) as i:
                    for j in range(2):
                        t = 2 * i + j
                        pe.wait_ge(s_xs, t + 1)
                        pe.wait_ge(s_xt, t + 1)
                        for c in range(DC):
                            last = nc.tensor.transpose(ps[:, j, c * P:(c + 1) * P], xs[:, j, c * P:(c + 1) * P], k.c("ident"))
                        last.then_inc(s_tr, 1)

            @block.scalar
            def _(act):
                act.wait_ge(s_var, 1)
                nc.scalar.activation(k.rstd[:, 0:tiles], k.rstd[:, 0:tiles], ACT.Sqrt).then_inc(s_sd, 1)
                act.wait_ge(s_var, 2)
                nc.scalar.activation(k.rms[:, :], k.rms[:, :], ACT.Sqrt).then_inc(s_sd, 1)
                act.wait_ge(s_w, 16)
                act.sem_inc(s_xt, 2)
                with act.Fori(0, tiles // 2) as i:
                    for j in range(2):
                        t = 2 * i + j
                        act.wait_ge(s_tr, t + 3)
                        nc.scalar.activation(xT[:, 0, bass.ds(t * P, P)], ps[:, j, 0:P], ACT.Copy, scale=nw[:, 0:1])
                        nc.scalar.activation(xT[:, 1, bass.ds(t * P, P)], ps[:, j, P:2 * P], ACT.Copy, scale=nw[:, 1:2]).then_inc(s_xt, 1)


def norm_transpose(k, tag, tiles=NT, natural=None, loads=None):
    nc, x, xT, mv, ps = k.nc, k.x, k.xT, k.mean_var, k.ps
    G = tiles // 4
    with ExitStack() as ctx:
        stats = k.sb(f"stats{tag}", [P, NT, 6], ctx=ctx)
        shift = k.sb(f"shift{tag}", [P, NT], ctx=ctx)
        xs = natural if natural is not None else k.sb(f"xs{tag}", [P, 4, D], ctx=ctx)
        slots = NT if natural is not None else 4
        s_stat, s_aggr, s_var, s_sd, s_rstd, s_shift, s_xs, s_tr, s_xtA, s_xtD = (
            k.sem(f"s_n{tag}" + n) for n in ("stat", "aggr", "var", "sd", "rstd", "shift", "xs", "tr", "xtA", "xtD"))

        def copy_out(t):
            return xT[:, :, t * P:(t + 1) * P], ps[:, t % 4, 0:D].rearrange("p (c q) -> p c q", c=DC)

        with nc.Block() as block:
            if loads is not None:
                @block.sync
                def _(sp):
                    loads(sp)

            @block.vector
            def _(dve):
                for g in range(G + 2):
                    if g < G:
                        group = slice(4 * g, 4 * g + 4)
                        for t in range(4 * g, 4 * g + 4):
                            nc.vector.bn_stats(stats[:, t, :], x[:, t, :]).then_inc(s_stat, 1)
                        for t in range(4 * g, 4 * g + 4):
                            dve.wait_ge(s_stat, t + 1)
                            nc.vector.bn_aggr(mv[:, t, :], stats[:, t, :]).then_inc(s_aggr, 1)
                        dve.wait_ge(s_aggr, 4 * g + 4)
                        nc.vector.tensor_scalar(k.rstd[:, group], mv[:, group, 1], LN_EPS, None, ALU.add).then_inc(s_var, 1)
                    if 1 <= g <= G:
                        group = slice(4 * g - 4, 4 * g)
                        dve.wait_ge(s_sd, g)
                        nc.vector.reciprocal(k.rstd[:, group], k.rstd[:, group]).then_inc(s_rstd, 1)
                        dve.wait_ge(s_rstd, g)
                        nc.vector.scalar_tensor_tensor(shift[:, group], mv[:, group, 0], -1.0, k.rstd[:, group],
                                                       ALU.mult, ALU.mult).then_inc(s_shift, 1)
                    if g >= 2:
                        for t in (4 * g - 7, 4 * g - 5):
                            dve.wait_ge(s_tr, t + 1)
                            nc.vector.tensor_copy(*copy_out(t)).then_inc(s_xtD, 1)

            @block.scalar
            def _(act):
                for g in range(G + 1):
                    if g < G:
                        group = slice(4 * g, 4 * g + 4)
                        act.wait_ge(s_var, g + 1)
                        nc.scalar.activation(k.rstd[:, group], k.rstd[:, group], ACT.Sqrt).then_inc(s_sd, 1)
                        act.wait_ge(s_shift, g + 1)
                        for t in range(4 * g, 4 * g + 4):
                            if t >= slots:
                                act.wait_ge(s_tr, t - 3)
                            nc.scalar.activation(xs[:, t % slots, :], x[:, t, :], ACT.Identity, scale=k.rstd[:, t:t + 1],
                                                 bias=shift[:, t:t + 1]).then_inc(s_xs, 1)
                    if g >= 1:
                        for t in (4 * g - 4, 4 * g - 2):
                            act.wait_ge(s_tr, t + 1)
                            dst, src = copy_out(t)
                            nc.scalar.activation(dst, src, ACT.Copy).then_inc(s_xtA, 1)

            @block.tensor
            def _(pe):
                for t in range(tiles):
                    pe.wait_ge(s_xs, t + 1)
                    if t >= 4:
                        pe.wait_ge(s_xtD if t % 2 else s_xtA, (t - 4) // 2 + 1)
                    for c in range(DC):
                        last = nc.tensor.transpose(ps[:, t % 4, c * P:(c + 1) * P], xs[:, t % slots, c * P:(c + 1) * P], k.c("ident"))
                    last.then_inc(s_tr, 1)


def project_heads(k, tag, rel, vz, cm):
    nc, ps, xT = k.nc, k.ps, k.xT
    NZ = 2 if rel else 1
    kh = H if rel else KVH
    kd = nc.dram_tensor("kd" + tag, (3, B * kh, HD, NZ, S), BF16, kind="Internal").ap()
    qd = nc.dram_tensor(f"qd{tag}", (3, NH, HD, S), BF16, kind="Internal").ap()
    NV = kh * HD
    NW = D + 2 * NV
    NB = 4
    with ExitStack() as ctx:
        w = k.sb("wqkv" + tag, [P, DC, NW], ctx=ctx)
        bc = k.sb("bc" + tag, [P, 6], ctx=ctx)
        rc = k.sb("rc" + tag, [P, 2], ctx=ctx)
        bv = k.sb("bv" + tag, [1, D], ctx=ctx)
        rv = k.sb("rv" + tag, [P, 2, HD], ctx=ctx)
        f32 = k.sb("f32" + tag, [P, NB, 512], ctx=ctx)
        res = k.sb("res" + tag, [P, NB, 512], ctx=ctx)
        parts = k.sb("parts" + tag, [P, NB, 3, 512], BF16, ctx=ctx)
        s_w, s_b, s_be, s_mm, s_f, s_hi, s_res, s_mid, s_lo, s_mmv, s_v, s_zone, s_const = (
            k.sem("s_p" + tag + n) for n in ("w", "b", "be", "mm", "f", "hi", "res", "mid", "lo", "mmv", "v", "zone", "const"))
        s_st = [k.sem(f"s_p{tag}st{n}") for n in range(NB)]
        prods, units = [], []
        for q in range(N // 512):
            b = q // 2
            for c in range(DC):
                units.append((len(prods), P, q, qd, b * H + HG * c, c))
                prods.append((c * P, P, q))
            for c in range(-(-NV // P)):
                rows = min(P, NV)
                for z in range(NZ):
                    units.append((len(prods), rows, q, kd[:, :, :, z, :], b * kh + HG * c, 2 + 2 * z + c))
                prods.append((D + c * P, rows, q))
        last_unit = [max(i for i, u in enumerate(units) if u[0] == n) for n in range(len(prods))]
        def load_weights(sp):
            if rel:
                sp.dma_start(w[:, :, :], k.d["L1_attn_W_qkv"].rearrange("(c p) n -> p c n", p=P)).then_inc(s_w, 16)
                sp.dma_start(bv[:, :], k.d["L1_attn_b_qkv"][2 * D:3 * D].rearrange("(a n) -> a n", a=1)).then_inc(s_w, 16)
                sp.dma_start(bc[:, 0:4], k.d["L1_attn_b_qkv"][0:2 * D].rearrange("(s p) -> p s", p=P),
                             allow_slow_non_contiguous=True).then_inc(s_b, 16)
                for z, row in ((0, 0), (1, NR - 1)):
                    for h in range(HG):
                        sp.dma_start(rc[h * HD:(h + 1) * HD, z:z + 1], k.d["L1_attn_rel_emb_k"][row:row + 1, :].rearrange("a d -> d a"),
                                     allow_slow_non_contiguous=True).then_inc(s_b, 16)
                    sp.dma_start(rv[:, z, :], k.d["L1_attn_rel_emb_v"][row:row + 1, :].to_broadcast([P, HD])).then_inc(s_b, 16)
            else:
                for o, n, name in ((0, D, "q"), (D, NV, "k"), (D + NV, NV, "v")):
                    sp.dma_start(w[:, :, o:o + n], k.d["L0_attn_w_" + name].rearrange("(c p) n -> p c n", p=P)).then_inc(s_w, 16)

        if rel:
            norm_transpose(k, "1a", loads=load_weights)
        with nc.Block() as block:
            @block.sync
            def _(sp):
                if not rel:
                    load_weights(sp)
                for i, (n, rows, q, dst, h0, _) in enumerate(units):
                    sp.wait_ge(s_lo, i + 1)
                    o = (q % 2) * 512
                    for part in range(3):
                        sp.dma_start(dst[part, h0:h0 + rows // HD, :, o:o + 512].rearrange("h d t -> (h d) t"),
                                     parts[0:rows, i % NB, part, :]).then_inc(s_st[i % NB], 16)
                for n in range(NB):
                    sp.wait_ge(s_st[n], 48 * ((len(units) - 1 - n) // NB + 1))

            @block.tensor
            def _(pe):
                pe.wait_ge(s_w, 32 if rel else 48)
                for n, (o, rows, q) in enumerate(prods):
                    if n >= 4:
                        pe.wait_ge(s_f, last_unit[n - 4] + 1)
                    for c in range(DC):
                        last = nc.tensor.matmul(ps[0:rows, n % 4, :], w[:, c, o:o + rows], xT[:, c, q * 512:(q + 1) * 512],
                                                start=(c == 0), stop=(c == DC - 1))
                    last.then_inc(s_mm, 1)
                for t in range(NT):
                    if t >= 4:
                        pe.wait_ge(s_v, t - 3)
                    for c in range(DC):
                        last = nc.tensor.matmul(ps[:, 4 + t % 4, 0:NV], xT[:, c, t * P:(t + 1) * P], w[:, c, NW - NV:NW],
                                                start=(c == 0), stop=(c == DC - 1 and not rel))
                    if rel:
                        last = nc.tensor.matmul(ps[:, 4 + t % 4, 0:NV], k.c("ones", 1), bv[:, :], start=False, stop=True)
                    last.then_inc(s_mmv, 1)

            @block.scalar
            def _(act):
                if rel:
                    act.wait_ge(s_be, 1)
                for i, (n, rows, q, dst, h0, col) in enumerate(units):
                    if rel:
                        act.wait_ge(s_mm, n + 1)
                        if i >= NB:
                            act.wait_ge(s_res, i - NB + 1)
                        nc.scalar.activation(f32[0:rows, i % NB, :], ps[0:rows, n % 4, :], ACT.Identity, bias=bc[0:rows, col:col + 1],
                                             scale=(HD ** -0.5 if col < 2 else 1.0)).then_inc(s_f, 1)
                    act.wait_ge(s_f, i + 1)
                    if i >= NB:
                        act.wait_ge(s_st[i % NB], 48 * (i // NB))
                    nc.scalar.activation(parts[0:rows, i % NB, 0, :], f32[0:rows, i % NB, :], ACT.Copy).then_inc(s_hi, 1)

            @block.gpsimd
            def _(pool):
                if not rel:
                    nc.gpsimd.tensor_copy(cm[:, 0, :], k.c("causal"))
                    nc.gpsimd.tensor_copy(cm[:, 1, :], k.c("ident")).then_inc(s_const, 1)
                for i, (n, rows, *_) in enumerate(units):
                    pool.wait_ge(s_res, i + 1)
                    if i >= NB:
                        pool.wait_ge(s_st[i % NB], 48 * (i // NB))
                    nc.gpsimd.tensor_copy(parts[0:rows, i % NB, 1, :], res[0:rows, i % NB, :]).then_inc(s_mid, 1)

            @block.vector
            def _(dve):
                if rel:
                    dve.wait_ge(s_b, 16 * (1 + 2 * HG + 2))
                    nc.vector.tensor_scalar(bc[:, 0:2], bc[:, 0:2], HD ** -0.5, None, ALU.mult)
                    nc.vector.tensor_scalar(bc[:, 4:6], bc[:, 2:4], rc[:, 1:2], None, ALU.add).then_inc(s_zone, 1)
                    dve.wait_ge(s_zone, 1)
                    nc.vector.tensor_scalar(bc[:, 2:4], bc[:, 2:4], rc[:, 0:1], None, ALU.add).then_inc(s_be, 1)

                def rotate(i):
                    n, rows, q, dst, h0, col = units[i]
                    dve.wait_ge(s_mm, n + 1)
                    if i >= NB:
                        dve.wait_ge(s_hi, i - NB + 1)
                        dve.wait_ge(s_res, i - NB + 1)
                    rope = k.c("rope")[0:rows, (q % 2) * 512:(q % 2 + 1) * 512]
                    if col < 2:
                        nc.vector.scalar_tensor_tensor(f32[0:rows, i % NB, :], ps[0:rows, n % 4, :], HD ** -0.5, rope,
                                                       ALU.mult, ALU.mult).then_inc(s_f, 1)
                    else:
                        nc.vector.tensor_tensor(f32[0:rows, i % NB, :], ps[0:rows, n % 4, :], rope, ALU.mult).then_inc(s_f, 1)

                def residue(i):
                    rows = units[i][1]
                    dve.wait_ge(s_hi, i + 1)
                    if i >= NB:
                        dve.wait_ge(s_mid, i - NB + 1)
                        dve.wait_ge(s_lo, i - NB + 1)
                    dve.wait_ge(s_f, i + 1)
                    nc.vector.tensor_tensor(res[0:rows, i % NB, :], f32[0:rows, i % NB, :], parts[0:rows, i % NB, 0, :],
                                            ALU.subtract).then_inc(s_res, 1)

                def low(i):
                    rows = units[i][1]
                    dve.wait_ge(s_mid, i + 1)
                    dve.wait_ge(s_res, i + 1)
                    if i >= NB:
                        dve.wait_ge(s_st[i % NB], 48 * (i // NB))
                    nc.vector.tensor_tensor(parts[0:rows, i % NB, 2, :], res[0:rows, i % NB, :], parts[0:rows, i % NB, 1, :],
                                            ALU.subtract).then_inc(s_lo, 1)

                for i in range(len(units) + 2):
                    if i < len(units) and not rel:
                        rotate(i)
                    if 0 < i <= len(units):
                        residue(i - 1)
                    if i > 1:
                        low(i - 2)
                for t in range(NT):
                    b, kb = t // KB, t % KB
                    dve.wait_ge(s_mmv, t + 1)
                    src = ps[:, 4 + t % 4, 0:NV]
                    heads = slice(b * H, (b + 1) * H)
                    if rel:
                        for z in range(2):
                            last = nc.vector.tensor_tensor(vz[:, heads, z, kb, :], src.rearrange("p (h d) -> p h d", d=HD),
                                                           rv[:, z, :].unsqueeze(1).to_broadcast([P, H, HD]), ALU.add)
                        last.then_inc(s_zone, 1)
                        dve.wait_ge(s_zone, t + 2)
                        nc.vector.tensor_copy(vz[0:R, heads, 2, kb, :], vz[0:R, heads, 0, kb, :])
                        nc.vector.tensor_copy(vz[R:P, heads, 2, kb, :], vz[R:P, heads, 1, kb, :]).then_inc(s_v, 1)
                    else:
                        nc.vector.tensor_copy(vz[:, heads, 0, kb, :].rearrange("p (r g) d -> p r g d", r=REP),
                                              src.rearrange("p (g d) -> p g d", d=HD).unsqueeze(1).to_broadcast(
                                                  [P, REP, KVH, HD])).then_inc(s_v, 1)
    return qd, kd


def relative_tables(k, dispatch):
    nc, ps = k.nc, k.ps
    relk, relv, skew_u, skew_p = k.relk, k.relv, k.skew_u, k.skew_p
    with ExitStack() as ctx:
        emb = k.sb("emb", [P, 2, HD], ctx=ctx)
        ends = k.sb("ends", [P, 2, 2, HD], ctx=ctx)
        df = k.sb("df", [P, 2, HD], ctx=ctx)
        hi = k.sb("dhi", [P, 2, HD], BF16, ctx=ctx)
        terms = k.sb("terms", [P, 2, TERMS, HD], ctx=ctx)
        zero = k.sb("zeros", [P, KB * 2 * P], ctx=ctx)
        s_ld, s_z, s_fill, s_ch, s_t, s_te = (k.sem("s_rt" + n) for n in ("ld", "z", "fill", "ch", "t", "te"))
        with nc.Block() as block:
            @block.sync
            def _(sp):
                for n, name in enumerate("kv"):
                    sp.dma_start(emb[:, n, :], k.d["L1_attn_rel_emb_" + name][0:P, :]).then_inc(s_ld, 16)
                    for z, row in ((0, 0), (1, NR - 1)):
                        sp.dma_start(ends[:, n, z, :], k.d["L1_attn_rel_emb_" + name][row:row + 1, :].to_broadcast([P, HD])).then_inc(s_ld, 16)
                sp.wait_ge(s_z, 1)
                for buf in (skew_u, skew_p):
                    sp.dma_start(buf.rearrange("a p n -> p a n"), zero[:, :].rearrange("p (a n) -> p a n", a=KB)).then_inc(s_fill, 16)
                sp.wait_ge(s_fill, 32)

            @block.gpsimd
            def _(pool):
                dispatch(pool)

            @block.tensor
            def _(pe):
                pe.wait_ge(s_t, 1)
                for z in range(2):
                    last = nc.tensor.transpose(ps[0:KS, 0, z * P:(z + 1) * P], terms[:, z, :, :].rearrange("p t d -> p (t d)"), k.c("ident"))
                last.then_inc(s_te, 1)

            @block.vector
            def _(dve):
                link = Chain(dve, s_ch)
                nc.vector.memset(zero[:, :], 0.0).then_inc(s_z, 1)
                dve.wait_ge(s_ld, 16 * 6)
                for n, dst in ((0, df), (1, relv)):
                    link(nc.vector.tensor_tensor(dst[:, 0, :], emb[:, n, :], ends[:, n, 0, :], ALU.subtract))
                    link(nc.vector.tensor_tensor(dst[:, 1, :], ends[:, n, 0, :], ends[:, n, 1, :], ALU.subtract))
                for part in range(3):
                    link(nc.vector.tensor_copy(hi[:, :, :], df[:, :, :]))
                    for c in range(TERMS):
                        if K_PARTS[c] == part:
                            link(nc.vector.tensor_copy(terms[:, :, c, :], hi[:, :, :]))
                    link(nc.vector.tensor_tensor(df[:, :, :], df[:, :, :], hi[:, :, :], ALU.subtract))
                dve.sem_inc(s_t, 1)
                dve.wait_ge(s_te, 1)
                nc.vector.tensor_copy(relk[:, :], ps[0:KS, 0, 0:P + 1]).then_inc(s_z, 1)


def past(t, n):
    return not isinstance(t, int) or t >= n


def sweep(eng, body, lead, lag):
    def at(i, s):
        def tile(o):
            u, c = (s + o) % PERIOD, (s + o) // PERIOD
            t = PERIOD * (i + c) + u
            if isinstance(t, int) and not 0 <= t < NTILE:
                return None
            return u, 2 * (i + c) + u // KB, i + c, t, (PERIOD // 4) * (i + c) + u // 4
        return tile
    for s in range(-lead, PERIOD):
        body(at(0, s))
    with eng.Fori(1, NTILE // PERIOD - 1) as i:
        for s in range(PERIOD):
            body(at(i, s))
    for s in range(PERIOD + lag):
        body(at(NTILE // PERIOD - 1, s))


def attention(k, tag, rel):
    nc, ps = k.nc, k.ps
    with ExitStack() as ctx:
        Z = 3 if rel else 1
        vz = k.sb("vz" + tag, [P, NH, Z, KB, HD], ctx=ctx)
        cm = None if rel else k.sb("cm" + tag, [P, 2, P], BF16, ctx=ctx)
        qd, kd = project_heads(k, tag, rel, vz, cm)
        if rel:
            relk, relv, skew_u, skew_p = k.relk, k.relv, k.skew_u, k.skew_p
        k.end_stage()
        NZ = 2 if rel else 1
        LEAD = 6 if rel else 0
        TL = 6 if rel else 3
        BL = TL + 2 if rel else TL + 3
        OB = (6, 6) if rel else (6, 7)
        NPR = 8
        SIDE = 2 * P + 1
        qs = k.sb("qs" + tag, [KS, 2, S], BF16, ctx=ctx)
        ks = k.sb("ks" + tag, [KS, 2, NZ, S], BF16, ctx=ctx)
        vh = k.sb("vh" + tag, [P, 2, Z * KB * HD], ctx=ctx)
        oT = k.sb("oT" + tag, [HD, 2, S], ctx=ctx)
        out = k.sb("out" + tag, [P, KB, NH, HD], ctx=ctx)
        prob = k.sb("prob" + tag, [P, NPR, S], ctx=ctx)
        probT = k.sb("probT" + tag, [P, 2, S], ctx=ctx)
        nmax = k.sb("nmax" + tag, [P, 2], ctx=ctx)
        rsum = k.sb("rsum" + tag, [P, 4], ctx=ctx)
        rinv = k.sb("rinv" + tag, [P, PERIOD], ctx=ctx)
        if rel:
            side = k.sb("side", [P, 4, SIDE], ctx=ctx)
            band = k.sb("band", [P, 4, P], ctx=ctx)
            dev = k.sb("dev", [P, 4, 2 * P], ctx=ctx)
            wr = k.sb("wr", [P, 4, P], ctx=ctx)
            wm = k.sb("wm", [P, 2, P], ctx=ctx)
            gsum = k.sb("gsum", [P, PERIOD], ctx=ctx)
            ge = k.sb("ge", [P, KB, HD], ctx=ctx)
        s_score, s_add, s_max, s_exp, s_tr, s_evA, s_evD, s_inv, s_o, s_oE, s_bt, s_out, s_side, s_sideE, s_band, s_wm, s_gsum, s_ge = (
            k.sem(f"s_t{tag}_{n}") for n in ("score", "add", "max", "exp", "tr", "evA", "evD", "inv", "o", "oE", "bt", "out",
                                             "side", "sideE", "band", "wm", "gsum", "ge"))
        s_lq = [k.sem(f"s_lq{tag}{j}") for j in range(2)]
        s_lk = [k.sem(f"s_lk{tag}{j}") for j in range(2)]
        s_vh = [k.sem(f"s_vh{tag}{j}") for j in range(2)]
        s_bo, s_bb, s_po, s_pb = ([k.sem(f"s_{n}{tag}{j}") for j in range(4)] for n in ("bo", "bb", "po", "pb"))
        if not rel:
            zero = k.sb("zero", [P, 2 * CAP // P * D], ctx=ctx)
            s_zero, s_fill = k.sem("s_zero"), k.sem("s_fill")
        LD = 16 * TERMS

        def width(a):
            return S if rel else (a + 1) * P

        def act_blocks(a):
            return -(-width(a) // P // 2)

        def side_step(tile):
            return tile(LEAD)[3] + 1 if tile(LEAD) else tile(-TL)[3] + TL + LEAD + 1

        def band_keys(a):
            lo, hi = max(0, a * P - R), min(S, a * P + P + R)
            return lo, hi, lo - (a * P - R)

        def wide(bank, lo, hi):
            return ps[:, bank:bank + 2, :].rearrange("p a n -> p (a n)")[:, lo:hi]

        def skewed(buf, a):
            return bass.AP(buf.tensor, a * P * 2 * P, [[2 * P + 1, P], [1, P]])

        with nc.Block() as block:
            @block.sync
            def _(sp):
                def load_queries(j, n):
                    for c in range(TERMS):
                        sp.dma_start(qs[c * HD:(c + 1) * HD, j, :],
                                     qd[Q_PARTS[c], bass.ds(n, 1), :, :].rearrange("a d t -> (a d) t")).then_inc(s_lq[j], 16)

                def load_keys(j, n, terms=range(TERMS)):
                    kn = n if rel else (n // H) * KVH + n % KVH
                    for c in terms:
                        sp.dma_start(ks[c * HD:(c + 1) * HD, j, :, :].rearrange("d z t -> d (z t)"),
                                     kd[K_PARTS[c], bass.ds(kn, 1), :, :, :].rearrange("a d z t -> (a d) (z t)")).then_inc(s_lk[j], 16)

                def load_values(j, n):
                    sp.dma_start(vh[:, j, :], vz[:, bass.ds(n, 1), :, :, :].rearrange("p a z k d -> p (a z k d)")).then_inc(s_vh[j], 16)

                def body(tile):
                    if tile(-TL - 2):
                        u, n, m, t, t4 = tile(-TL - 2)
                        if u % KB == KB - 1 and not (isinstance(n, int) and n + 2 >= NH):
                            sp.wait_ge(s_o, t + 1)
                            load_values(u // KB, n + 2)
                    for behind in (1, 2, 3):
                        if tile(-behind):
                            u, n, m, t, t4 = tile(-behind)
                            if u % KB == KB - 1 and not (isinstance(n, int) and n + 2 >= NH):
                                if behind == 1:
                                    sp.wait_ge(s_score, t + 1)
                                    load_queries(u // KB, n + 2)
                                else:
                                    load_keys(u // KB, n + 2, range(3 * behind - 6, 3 * behind - 3))
                    if rel and tile(-3):
                        u, n, m, t, t4 = tile(-3)
                        sp.wait_ge(s_po[u % 4], 16 * t4 + 16)
                        if isinstance(t, int) and t + 3 + LEAD > NTILE:
                            sp.wait_ge(s_tr, t - 3)
                            sp.wait_ge(s_gsum, t - 3)
                        sp.dma_start(wr[:, u % 4, :], skewed(skew_p, u % KB)).then_inc(s_pb[u % 4], 16)
                    if rel and tile(LEAD):
                        u, n, m, t, t4 = tile(LEAD)
                        sp.wait_ge(s_band, t + 1)
                        sp.dma_start(skewed(skew_u, u % KB), band[:, u % 4, :]).then_inc(s_bo[u % 4], 16)
                    if rel and tile(-1):
                        u, n, m, t, t4 = tile(-1)
                        lo, hi, o = band_keys(u % KB)
                        sp.wait_ge(s_exp, t + 1)
                        sp.dma_start(skew_p[u % KB, :, o:o + hi - lo], prob[:, u % NPR, lo:hi]).then_inc(s_po[u % 4], 16)
                    if rel and tile(3):
                        u, n, m, t, t4 = tile(3)
                        sp.wait_ge(s_bo[u % 4], 16 * t4 + 16)
                        sp.dma_start(dev[:, u % 4, :], skew_u[u % KB]).then_inc(s_bb[u % 4], 16)
                for n in range(2):
                    load_queries(n, n)
                    load_keys(n, n)
                load_values(0, 0)
                load_values(1, 1)
                if not rel:
                    sp.wait_ge(s_zero, 1)
                    rows = k.disp.rearrange("(n p a) d -> n p (a d)", p=P, a=2 * CAP // P)
                    for n in range(E + 1):
                        sp.dma_start(rows[n], zero[:, :]).then_inc(s_fill, 16)
                sweep(sp, body, LEAD, BL)
                if not rel:
                    sp.wait_ge(s_fill, 16 * (E + 1))

            @block.tensor
            def _(pe):
                def body(tile):
                    if rel and (tile(LEAD) or tile(-TL)):
                        if past(side_step(tile), 2):
                            pe.wait_ge(s_sideE, side_step(tile) - 1)
                        if tile(LEAD):
                            u, n, m, t, t4 = tile(LEAD)
                            a, j = u % KB, u // KB
                            if a == 0:
                                pe.wait_ge(s_lq[j], LD * m + LD)
                            last = nc.tensor.matmul(ps[:, 7, 0:P + 1], qs[:, j, a * P:(a + 1) * P], relk[:, :], start=True, stop=True)
                        if tile(-TL):
                            u, n, m, t, t4 = tile(-TL)
                            pe.wait_ge(s_pb[u % 4], 16 * t4 + 16)
                            last = nc.tensor.transpose(ps[:, 7, P + 1:SIDE], wr[:, u % 4, :], k.c("ident"))
                        last.then_inc(s_side, 1)
                    back = tile(-BL) and tile(-BL)[0] % KB == KB - 1
                    if tile(-TL):
                        u, n, m, t, t4 = tile(-TL)
                        pe.wait_ge(s_exp, t + 1)
                        if past(t, 1):
                            pe.wait_ge(s_evD, t)
                            pe.wait_ge(s_evA, t)
                        for kb in range(width(u % KB) // P):
                            if back and kb == width(u % KB) // P - 1:
                                pe.wait_ge(s_oE, tile(-BL)[4] + 1)
                            bank, col = divmod(kb, act_blocks(u % KB))
                            last = nc.tensor.transpose(ps[:, 4 + bank, col * P:(col + 1) * P],
                                                       prob[:, u % NPR, kb * P:(kb + 1) * P], k.c("ident"))
                        last.then_inc(s_tr, 1)
                    if back:
                        u, n, m, t, t4 = tile(-BL)
                        if not tile(-TL):
                            pe.wait_ge(s_oE, t4 + 1)
                        for p in range(KB):
                            last = nc.tensor.transpose(ps[:, OB[1], p * HD:(p + 1) * HD], oT[:, u // KB, p * P:(p + 1) * P], k.c("ident", HD)[:, 0:HD])
                        last.then_inc(s_bt, 1)
                    if tile(0):
                        u, n, m, t, t4 = tile(0)
                        a, j = u % KB, u // KB
                        bank = 2 * (u % 2)
                        if u % KB == 0:
                            pe.wait_ge(s_lq[j], LD * m + LD)
                            pe.wait_ge(s_lk[j], LD * m + LD)
                        if past(t, 2):
                            pe.wait_ge(s_exp, t - 1)
                        query = qs[:, j, a * P:(a + 1) * P]
                        edges = sorted({0, 512, a * P + R, S} if rel else {0, min(512, a * P), a * P, a * P + P})
                        for lo, hi in zip(edges, edges[1:]):
                            last = nc.tensor.matmul(wide(bank, lo, hi), query, ks[:, j, int(rel and lo >= a * P + R), lo:hi],
                                                    start=True, stop=(rel or lo < a * P))
                        if not rel:
                            last = nc.tensor.matmul(wide(bank, a * P, a * P + P), cm[:, 1, :], cm[:, 0, :], start=False, stop=True)
                        last.then_inc(s_score, 1)
                    if tile(-TL - 1):
                        u, n, m, t, t4 = tile(-TL - 1)
                        a, j = u % KB, u // KB
                        pe.wait_ge(s_evA, t + 1)
                        pe.wait_ge(s_evD, t + 1)
                        if rel:
                            pe.wait_ge(s_sideE, t + TL + LEAD + 1)
                        if u % KB == 0:
                            pe.wait_ge(s_vh[j], 16 * m + 16)
                            if not rel and past(t, KB):
                                pe.wait_ge(s_oE, t4 - 1)
                        if u % KB == (0 if rel else 4) and past(t, KB):
                            pe.wait_ge(s_out, n)
                        if rel and u % KB == 4:
                            pe.wait_ge(s_oE, t4)
                        o = ps[0:HD, OB[u % KB // 4], (u % 4) * P:(u % 4 + 1) * P]
                        blocks = width(a) // P
                        for kb in range(blocks):
                            zone = (0 if kb < a else 2 if kb == a else 1) if rel else 0
                            col = (zone * KB + kb) * HD
                            last = nc.tensor.matmul(o, vh[:, j, col:col + HD], probT[:, u % 2, kb * P:(kb + 1) * P],
                                                    start=(kb == 0), stop=(kb == blocks - 1 and not rel))
                        if rel:
                            last = nc.tensor.matmul(o, relv[:, 0, :], side[:, (u + TL + LEAD) % 4, P + 1:SIDE], start=False, stop=True)
                        last.then_inc(s_o, 1)
                sweep(pe, body, LEAD, BL)

            @block.scalar
            def _(act):
                def body(tile):
                    if tile(-TL - 2):
                        u, n, m, t, t4 = tile(-TL - 2)
                        if u % 4 == 3:
                            act.wait_ge(s_o, t + 1)
                            o = (u % KB - 3) * P
                            nc.scalar.activation(oT[:, u // KB, o:o + 4 * P], ps[0:HD, OB[u % KB // 4], :], ACT.Copy).then_inc(s_oE, 1)
                    if rel and (tile(LEAD) or tile(-TL)):
                        slot = (tile(LEAD) or [tile(-TL) and tile(-TL)[0] + TL + LEAD])[0] % 4
                        act.wait_ge(s_side, side_step(tile))
                        if past(side_step(tile), 5):
                            act.wait_ge(s_band, min(side_step(tile) - 4, NTILE) if isinstance(side_step(tile), int) else side_step(tile) - 4)
                        lo, hi = 0 if tile(LEAD) else P + 1, SIDE if tile(-TL) else P + 1
                        nc.scalar.activation(side[:, slot, lo:hi], ps[:, 7, lo:hi], ACT.Copy).then_inc(s_sideE, 1)
                    if tile(-TL):
                        u, n, m, t, t4 = tile(-TL)
                        act.wait_ge(s_tr, t + 1)
                        e = act_blocks(u % KB) * P
                        nc.scalar.activation(probT[:, u % 2, 0:e], ps[:, 4, 0:e], ACT.Copy).then_inc(s_evA, 1)
                    if tile(-1):
                        u, n, m, t, t4 = tile(-1)
                        w = width(u % KB)
                        act.wait_ge(s_max, t + 1)
                        if past(t, NPR):
                            act.wait_ge(s_tr, t + 1 - NPR)
                        if past(t, 4):
                            act.wait_ge(s_inv, t - 3)
                        nc.scalar.activation(prob[:, u % NPR, 0:w], wide(2 * (u % 2), 0, w), ACT.Exp, bias=nmax[:, u % 2:u % 2 + 1],
                                             accum_out=rsum[:, u % 4:u % 4 + 1]).then_inc(s_exp, 1)
                sweep(act, body, LEAD, BL)

            if rel:
                @block.gpsimd
                def _(pool):
                    def body(tile):
                        if tile(-5):
                            u, n, m, t, t4 = tile(-5)
                            pool.wait_ge(s_pb[u % 4], 16 * t4 + 16)
                            if past(t, 2):
                                pool.wait_ge(s_gsum, t - 1)
                            nc.gpsimd.tensor_tensor(wm[:, u % 2, :], wr[:, u % 4, :], k.c("late"), ALU.mult).then_inc(s_wm, 1)
                    sweep(pool, body, LEAD, BL)

            @block.vector
            def _(dve):
                def body(tile):
                    if tile(-TL):
                        u, n, m, t, t4 = tile(-TL)
                        dve.wait_ge(s_tr, t + 1)
                        e, w = act_blocks(u % KB) * P, width(u % KB)
                        if w > e:
                            nc.vector.tensor_copy(probT[:, u % 2, e:w], ps[:, 5, 0:w - e]).then_inc(s_evD, 1)
                        else:
                            dve.sem_inc(s_evD, 1)
                    if rel and tile(-TL):
                        u, n, m, t, t4 = tile(-TL)
                        dve.wait_ge(s_wm, t + 1)
                        nc.vector.tensor_reduce(gsum[:, u:u + 1], wm[:, u % 2, :], AX.X, ALU.add).then_inc(s_gsum, 1)
                    if tile(-BL) and tile(-BL)[0] % KB == KB - 1:
                        u, n, m, t, t4 = tile(-BL)
                        j = u // KB
                        dve.wait_ge(s_bt, n + 1)
                        dve.wait_ge(s_inv, t + 1)
                        heads = out[:, :, bass.ds(n, 1), :].rearrange("p k a d -> p k (a d)")
                        sums = ps[:, OB[1], 0:KB * HD].rearrange("p (k d) -> p k d", d=HD)
                        inverse = rinv[:, j * KB:(j + 1) * KB].unsqueeze(2).to_broadcast([P, KB, HD])
                        if rel:
                            dve.wait_ge(s_gsum, t + 1)
                            nc.vector.tensor_tensor(ge[:, :, :], gsum[:, j * KB:(j + 1) * KB].unsqueeze(2).to_broadcast([P, KB, HD]),
                                                    relv[:, 1, :].unsqueeze(1).to_broadcast([P, KB, HD]), ALU.mult).then_inc(s_ge, 1)
                            dve.wait_ge(s_ge, 2 * n + 1)
                            nc.vector.tensor_tensor(ge[:, :, :], ge[:, :, :], sums, ALU.add).then_inc(s_ge, 1)
                            dve.wait_ge(s_ge, 2 * n + 2)
                            sums = ge[:, :, :]
                        nc.vector.tensor_tensor(heads, sums, inverse, ALU.mult).then_inc(s_out, 1)
                    if tile(0):
                        u, n, m, t, t4 = tile(0)
                        bank = 2 * (u % 2)
                        dve.wait_ge(s_score, t + 1)
                        if rel:
                            lo, hi, o = band_keys(u % KB)
                            dve.wait_ge(s_bb[u % 4], 16 * t4 + 16)
                            nc.vector.tensor_tensor(wide(bank, lo, hi), wide(bank, lo, hi), dev[:, u % 4, o:o + hi - lo],
                                                    ALU.add).then_inc(s_add, 1)
                            dve.wait_ge(s_add, t + 1)
                        nc.vector.tensor_reduce(nmax[:, u % 2:u % 2 + 1], wide(bank, 0, width(u % KB)), AX.X, ALU.max,
                                                negate=True).then_inc(s_max, 1)
                    if tile(-2):
                        u, n, m, t, t4 = tile(-2)
                        dve.wait_ge(s_exp, t + 1)
                        nc.vector.reciprocal(rinv[:, u:u + 1], rsum[:, u % 4:u % 4 + 1]).then_inc(s_inv, 1)
                    if rel and tile(LEAD):
                        u, n, m, t, t4 = tile(LEAD)
                        dve.wait_ge(s_sideE, t + 1)
                        if past(t, 4):
                            dve.wait_ge(s_bo[u % 4], 16 * t4)
                        nc.vector.scalar_tensor_tensor(band[:, u % 4, :], k.c("late"), side[:, u % 4, P:P + 1], side[:, u % 4, 0:P],
                                                       ALU.mult, ALU.add).then_inc(s_band, 1)
                if not rel:
                    nc.vector.memset(zero[:, :], 0.0).then_inc(s_zero, 1)
                sweep(dve, body, LEAD, BL)
        k.end_stage()
        if rel:
            project_out(k, tag, out, "L1_attn_W_out", "L1_attn_b_out")
        else:
            project_out(k, tag, out, "L0_attn_w_o", None)


def project_out(k, tag, heads, w_name, b_name):
    nc, ps, xT = k.nc, k.ps, k.xT
    with ExitStack() as ctx:
        wo = k.sb("wo" + tag, [P, DC, D], ctx=ctx)
        bo = k.sb("bo" + tag, [1, D], ctx=ctx)
        s_w, s_mm, s_add, s_t, s_te = (k.sem("s_o" + tag + n) for n in ("w", "mm", "add", "t", "te"))
        with nc.Block() as block:
            @block.sync
            def _(sp):
                sp.dma_start(wo[:, :, :], k.d[w_name].rearrange("(c p) n -> p c n", p=P)).then_inc(s_w, 16)
                if b_name:
                    sp.dma_start(bo[:, :], k.d[b_name].rearrange("(a n) -> a n", a=1)).then_inc(s_w, 16)

            @block.tensor
            def _(pe):
                for step in range(NT + 2):
                    if step < NT:
                        t = step
                        if t >= 4:
                            pe.wait_ge(s_te, t - 3)
                        for c in range(DC):
                            n = (t // KB) * H + c * HG
                            last = nc.tensor.transpose(ps[:, 4 + t % 4, c * P:(c + 1) * P],
                                                       heads[:, t % KB, n:n + HG, :].rearrange("p n d -> p (n d)"), k.c("ident"))
                        last.then_inc(s_t, 1)
                    if step >= 2:
                        t = step - 2
                        if t == 0:
                            pe.wait_ge(s_w, 32 if b_name else 16)
                        pe.wait_ge(s_te, t + 1)
                        if t >= 4:
                            pe.wait_ge(s_add, t - 3)
                        for c in range(DC):
                            last = nc.tensor.matmul(ps[:, t % 4, 0:D], xT[:, c, t * P:(t + 1) * P], wo[:, c, :],
                                                    start=(c == 0), stop=(c == DC - 1 and not b_name))
                        if b_name:
                            last = nc.tensor.matmul(ps[:, t % 4, 0:D], k.c("ones", 1), bo[:, :], start=False, stop=True)
                        last.then_inc(s_mm, 1)

            @block.scalar
            def _(act):
                for t in range(NT):
                    act.wait_ge(s_t, t + 1)
                    nc.scalar.activation(xT[:, :, t * P:(t + 1) * P], ps[:, 4 + t % 4, 0:D].rearrange("p (c q) -> p c q", c=DC),
                                         ACT.Copy).then_inc(s_te, 1)

            @block.vector
            def _(dve):
                for t in range(NT):
                    dve.wait_ge(s_mm, t + 1)
                    nc.vector.tensor_tensor(k.x[:, t, :], k.x[:, t, :], ps[:, t % 4, 0:D], ALU.add).then_inc(s_add, 1)


def context_prep(k):
    nc, ps = k.nc, k.ps
    with ExitStack() as ctx:
        wa = k.sb("wa", [P, DC, D], ctx=ctx)
        waT = k.sb("waT", [P, DC, D], ctx=ctx)
        wp = k.sb("wp", [PH, D], ctx=ctx)
        s_cst, s_x, s_ld, s_t1, s_e1, s_g, s_ge = (k.sem("s_ctx" + n) for n in ("cst", "x", "ld", "t1", "e1", "g", "ge"))
        with nc.Block() as block:
            @block.sync
            def _(sp):
                sp.dma_start(k.cst[:, :], k.d["consts"]).then_inc(s_cst, 16)
                sp.dma_start(wa[:, :, :], k.d["L0_xattn_W_a"].rearrange("(c p) q -> p c q", p=P)).then_inc(s_ld, 16)
                sp.dma_start(k.ctxn[:, :, :], k.d["ctx_1024"].rearrange("b j q -> j b q")).then_inc(s_ld, 16)
                sp.dma_start(wp[:, :], k.d["L0_xattn_W_p"]).then_inc(s_ld, 16)
                sp.dma_start(k.vp[:, :], k.d["L0_xattn_V_p"].rearrange("a p -> p a"),
                             allow_slow_non_contiguous=True).then_inc(s_ld, 16)
                sp.dma_start(k.x[:, :, :], k.d["x"].rearrange("b (t p) d -> p (b t) d", p=P)).then_inc(s_x, 16)
                sp.wait_ge(s_x, 16)

            @block.tensor
            def _(pe):
                pe.wait_ge(s_cst, 16)
                pe.wait_ge(s_ld, 64)
                for q in range(DC):
                    for c in range(DC):
                        nc.tensor.transpose(ps[:, 0, (q * DC + c) * P:(q * DC + c + 1) * P], wa[:, c, q * P:(q + 1) * P], k.c("ident"))
                for b in range(B):
                    for c in range(DC):
                        nc.tensor.transpose(ps[:, 1, (b * DC + c) * P:(b * DC + c) * P + SC],
                                            k.ctxn[:, b, c * P:(c + 1) * P], k.c("ident", SC)[:, 0:SC])
                for c in range(DC):
                    last = nc.tensor.transpose(ps[:, 2, c * P:c * P + PH], wp[:, c * P:(c + 1) * P], k.c("ident", PH)[:, 0:PH])
                last.then_inc(s_t1, 1)
                pe.wait_ge(s_e1, 1)
                for b in range(B):
                    for c in range(DC):
                        for q in range(DC):
                            last = nc.tensor.matmul(ps[:, 3, (b * DC + c) * P:(b * DC + c) * P + SC],
                                                    waT[:, q, c * P:(c + 1) * P], k.ctxT[:, b, q, :],
                                                    start=(q == 0), stop=(q == DC - 1))
                last.then_inc(s_g, 1)

            @block.vector
            def _(dve):
                dve.wait_ge(s_t1, 1)
                nc.vector.tensor_copy(waT[:, :, :], ps[:, 0, :].rearrange("p (q c) -> p q c", q=DC))
                nc.vector.tensor_copy(k.wpT[:, :, :], ps[:, 2, 0:DC * P].rearrange("p (c n) -> p c n", c=DC)[:, :, 0:PH])
                nc.vector.tensor_copy(k.ctxT[:, :, :, :].rearrange("p b c j -> p (b c) j"),
                                      ps[:, 1, :].rearrange("p (bc n) -> p bc n", n=P)[:, :, 0:SC]).then_inc(s_e1, 1)
                dve.wait_ge(s_g, 1)
                nc.vector.tensor_copy(k.gT[:, :, :, :].rearrange("p b c j -> p (b c) j"),
                                      ps[:, 3, :].rearrange("p (bc n) -> p bc n", n=P)[:, :, 0:SC]).then_inc(s_ge, 1)


def cross_attention0(k):
    nc, ps, xT = k.nc, k.ps, k.xT
    with ExitStack() as ctx:
        hidT = k.sb("hidT", [PH, N], ctx=ctx)
        pt = k.sb("pt", [P, NT], ctx=ctx)
        lo = k.sb("lo", [P, NT], ctx=ctx)
        loi = k.sb("loi", [P, NT], I32, ctx=ctx)
        fl = k.sb("fl", [P, NT], ctx=ctx)
        mx = k.sb("mx", [P, NT], ctx=ctx)
        sc = k.sb("sc", [P, NT, SC], ctx=ctx)
        cnt = k.sb("cnt", [P, NT, SC], ctx=ctx)
        tmp = k.sb("tmp", [P, NT, SC], ctx=ctx)
        gs = k.sb("gs", [P, NT, SC], ctx=ctx)
        aT = k.sb("aT", [SC, NT, P], ctx=ctx)
        s_hid, s_th, s_z, s_tz, s_sc, s_ch, s_gin, s_g, s_ein, s_e, s_a, s_at, s_ate, s_o, s_x = (
            k.sem("s_x0_" + n) for n in ("hid", "th", "z", "tz", "sc", "ch", "gin", "g", "ein", "e", "a", "at", "ate", "o", "x"))

        def rows(v):
            return v.unsqueeze(2).to_broadcast([P, NT, SC])

        with nc.Block() as block:
            @block.tensor
            def _(pe):
                for n in range(4):
                    for c in range(DC):
                        last = nc.tensor.matmul(ps[0:PH, n, :], k.wpT[:, c, :], xT[:, c, n * 512:(n + 1) * 512],
                                                start=(c == 0), stop=(c == DC - 1))
                    last.then_inc(s_hid, 1)
                for t in range(NT):
                    for c in range(DC):
                        last = nc.tensor.matmul(ps[:, 4 + t // 4, (t % 4) * P:(t % 4) * P + SC], xT[:, c, t * P:(t + 1) * P],
                                                k.gT[:, t // KB, c, :], start=(c == 0), stop=(c == DC - 1))
                    if t % 4 == 3:
                        last.then_inc(s_sc, 1)
                pe.wait_ge(s_th, 4)
                for t in range(NT):
                    last = nc.tensor.matmul(ps[:, 0, t:t + 1], hidT[:, t * P:(t + 1) * P], k.vp[:, :], start=True, stop=True)
                last.then_inc(s_z, 1)
                pe.wait_ge(s_a, 1)
                for g in range(4):
                    for t in range(4 * g, 4 * g + 4):
                        last = nc.tensor.transpose(ps[0:SC, 1 + g, (t % 4) * P:(t % 4 + 1) * P], sc[:, t, :], k.c("ident"))
                    last.then_inc(s_at, 1)
                for t in range(NT):
                    if t % 4 == 0:
                        pe.wait_ge(s_ate, t // 4 + 1)
                    if t >= 2:
                        pe.wait_ge(s_x, t - 1)
                    nc.tensor.matmul(ps[:, 5 + t % 2, 0:D], aT[:, t, :], k.ctxn[:, t // KB, :], start=True, stop=True).then_inc(s_o, 1)

            @block.scalar
            def _(act):
                for n in range(4):
                    act.wait_ge(s_hid, n + 1)
                    nc.scalar.activation(hidT[:, n * 512:(n + 1) * 512], ps[0:PH, n, :], ACT.Tanh).then_inc(s_th, 1)
                act.wait_ge(s_z, 1)
                nc.scalar.activation(pt[:, :], ps[:, 0, 0:NT], ACT.Tanh, scale=0.5).then_inc(s_tz, 1)
                act.wait_ge(s_gin, 1)
                nc.scalar.activation(gs[:, :, :], gs[:, :, :], ACT.Exp, scale=-0.5).then_inc(s_g, 1)
                act.wait_ge(s_ein, 1)
                nc.scalar.activation(sc[:, :, :], sc[:, :, :], ACT.Exp).then_inc(s_e, 1)
                for g in range(4):
                    act.wait_ge(s_at, g + 1)
                    nc.scalar.activation(aT[:, 4 * g:4 * g + 4, :], ps[0:SC, 1 + g, :].rearrange("p (t n) -> p t n", t=4),
                                         ACT.Copy).then_inc(s_ate, 1)

            @block.vector
            def _(dve):
                link = Chain(dve, s_ch)
                for g in range(4):
                    dve.wait_ge(s_sc, g + 1)
                    link(nc.vector.tensor_copy(sc[:, 4 * g:4 * g + 4, :],
                                               ps[:, 4 + g, :].rearrange("p (t n) -> p t n", t=4)[:, :, 0:SC]))
                dve.wait_ge(s_tz, 1)
                link(nc.vector.tensor_scalar(pt[:, :], pt[:, :], 1.0, SC / 2.0, ALU.add, ALU.mult))
                iota = k.c("iota77").unsqueeze(1).to_broadcast([P, NT, SC])
                link(nc.vector.tensor_tensor(gs[:, :, :], iota, rows(pt[:, :]), ALU.subtract))
                nc.vector.tensor_tensor(gs[:, :, :], gs[:, :, :], gs[:, :, :], ALU.mult).then_inc(s_gin, 1)
                link(nc.vector.tensor_copy(loi[:, :], pt[:, :]))
                link(nc.vector.tensor_copy(lo[:, :], loi[:, :]))
                link(nc.vector.tensor_tensor(fl[:, :], lo[:, :], pt[:, :], ALU.is_gt))
                link(nc.vector.tensor_tensor(lo[:, :], lo[:, :], fl[:, :], ALU.subtract))
                link(nc.vector.tensor_scalar(lo[:, :], lo[:, :], float(WIN), None, ALU.subtract))
                link(nc.vector.tensor_tensor(tmp[:, :, :], iota, rows(lo[:, :]), ALU.subtract))
                link(nc.vector.tensor_scalar(cnt[:, :, :], tmp[:, :, :], 2.0 * WIN - 1, None, ALU.is_le))
                link(nc.vector.scalar_tensor_tensor(cnt[:, :, :], tmp[:, :, :], 0.0, cnt[:, :, :], ALU.is_ge, ALU.mult))
                link(nc.vector.tensor_scalar(fl[:, :], lo[:, :], -1.0, 1.0, ALU.mult, ALU.add))
                link(nc.vector.tensor_scalar(cnt[:, :, 0], fl[:, :], 0.0, 2.0 * WIN, ALU.max, ALU.min))
                link(nc.vector.tensor_scalar(fl[:, :], lo[:, :], float(SC - 1 - 2 * WIN), None, ALU.subtract))
                link(nc.vector.tensor_scalar(cnt[:, :, SC - 1], fl[:, :], 0.0, 2.0 * WIN, ALU.max, ALU.min))
                link(nc.vector.scalar_tensor_tensor(sc[:, :, :], cnt[:, :, :], 0.0, sc[:, :, :], ALU.is_gt, ALU.mult))
                link(nc.vector.tensor_scalar(tmp[:, :, :], cnt[:, :, :], 0.0, NEG, ALU.is_le, ALU.mult))
                link(nc.vector.tensor_tensor(sc[:, :, :], sc[:, :, :], tmp[:, :, :], ALU.add))
                link(nc.vector.tensor_reduce(mx[:, :], sc[:, :, :], AX.X, ALU.max))
                nc.vector.tensor_tensor(sc[:, :, :], sc[:, :, :], rows(mx[:, :]), ALU.subtract).then_inc(s_ein, 1)
                dve.wait_ge(s_e, 1)
                link(nc.vector.tensor_tensor(sc[:, :, :], sc[:, :, :], cnt[:, :, :], ALU.mult))
                link(nc.vector.tensor_reduce(mx[:, :], sc[:, :, :], AX.X, ALU.add))
                link(nc.vector.reciprocal(mx[:, :], mx[:, :]))
                dve.wait_ge(s_g, 1)
                nc.vector.tensor_tensor(sc[:, :, :], sc[:, :, :], gs[:, :, :], ALU.mult).then_inc(s_a, 1)
                for t in range(NT):
                    dve.wait_ge(s_o, t + 1)
                    nc.vector.scalar_tensor_tensor(k.x[:, t, :], ps[:, 5 + t % 2, 0:D], mx[:, t:t + 1], k.x[:, t, :],
                                                   ALU.mult, ALU.add).then_inc(s_x, 1)


def moe0(k):
    nc, ps, xT = k.nc, k.ps, k.xT
    ROWS = 2 * CAP
    ST = ROWS // P
    G8 = [P, NT, E]
    disp = k.disp
    ybuf = nc.dram_tensor("ybuf", (E * ROWS, D), F32, kind="Internal").ap()
    with ExitStack() as ctx:
        wgt = k.sb("wgt", [P, 2, NT], ctx=ctx)
        idx_s = k.sb("idx_s", [P, 2, NT], U32, ctx=ctx)
        idx_g = k.sb("idx_g", [P, 2, NT], U32, ctx=ctx)
        w1 = k.sb("w1", [P, 2, DC, F0], ctx=ctx)
        w3 = k.sb("w3", [P, 2, DC, F0], ctx=ctx)
        w2 = k.sb("w2", [P, 2, FC0, D], ctx=ctx)
        s_w13 = [k.sem(f"s_w13_{j}") for j in range(2)]
        s_w2 = [k.sem(f"s_w2_{j}") for j in range(2)]
        with ExitStack() as rctx:
            xn = k.sb("xn_nat", [P, NT, D], ctx=rctx)
            gw = k.sb("gate", [E, D], ctx=rctx)
            gT = k.sb("gateT", [P, DC, E], ctx=rctx)
            lg, ex, oh1, oh2, cand, pos, base, keep, cw = (k.sb("r_" + n, G8, ctx=rctx) for n in (
                "lg", "ex", "oh1", "oh2", "cand", "pos", "base", "keep", "cw"))
            m1, m2, sl, va = (k.sb("r_" + n, [P, NT], ctx=rctx) for n in ("m1", "m2", "sl", "va"))
            dump = k.sb("r_dump", [P, 1], ctx=rctx)
            s_g, s_gt, s_gte, s_lg, s_ch, s_ei, s_ex, s_sel, s_cum, s_idx, s_sc = (
                k.sem("s_r_" + n) for n in ("g", "gt", "gte", "lg", "ch", "ei", "ex", "sel", "cum", "idx", "sc"))
            def load_weights(sp):
                sp.dma_start(gw[:, :], k.d["L0_ffn_gate_w"]).then_inc(s_g, 16)
                for e in range(2):
                    for w, name in ((w1, "w1"), (w3, "w3")):
                        sp.dma_start(w[:, e, :, :], k.d["L0_ffn_" + name][e].rearrange("(c p) f -> p c f", p=P)).then_inc(s_w13[e], 16)
                    sp.dma_start(w2[:, e, :, :], k.d["L0_ffn_w2"][e].rearrange("(c p) d -> p c d", p=P)).then_inc(s_w2[e], 16)

            norm_transpose(k, "0c", natural=xn, loads=load_weights)
            with nc.Block() as block:
                @block.tensor
                def _(pe):
                    pe.wait_ge(s_g, 16)
                    for c in range(DC):
                        last = nc.tensor.transpose(ps[:, 2, c * E:(c + 1) * E], gw[:, c * P:(c + 1) * P], k.c("ident", E)[:, 0:E])
                    last.then_inc(s_gt, 1)
                    pe.wait_ge(s_gte, 1)
                    for t in range(NT):
                        for c in range(DC):
                            last = nc.tensor.matmul(ps[:, 0, t * E:(t + 1) * E], xT[:, c, t * P:(t + 1) * P], gT[:, c, :],
                                                    start=(c == 0), stop=(c == DC - 1))
                    last.then_inc(s_lg, 1)
                    pe.wait_ge(s_sel, 1)
                    nc.tensor.matmul(ps[:, 1, 0:NT * E], k.c("tri"), cand[:, :, :].rearrange("p t e -> p (t e)"),
                                     start=True, stop=True, skip_group_check=True)
                    for b in range(B):
                        for s in range(1, KB):
                            o = (b * KB + s) * E
                            w = (KB - s) * E
                            last = nc.tensor.matmul(ps[:, 1, o:o + w], k.c("ones"),
                                                    cand[:, b * KB:b * KB + KB - s, :].rearrange("p t e -> p (t e)"),
                                                    start=False, stop=True, skip_group_check=True)
                    last.then_inc(s_cum, 1)

                @block.scalar
                def _(act):
                    act.wait_ge(s_ei, 1)
                    nc.scalar.activation(ex[:, :, :], ex[:, :, :], ACT.Exp).then_inc(s_ex, 1)

                @block.vector
                def _(dve):
                    link = Chain(dve, s_ch)
                    iota = k.c("iota8").unsqueeze(1).to_broadcast(G8)

                    def row(v):
                        return v.unsqueeze(2).to_broadcast(G8)

                    def first_best(oh, m):
                        link(nc.vector.tensor_reduce(m[:, :], lg[:, :, :], AX.X, ALU.max))
                        link(nc.vector.tensor_tensor(cand[:, :, :], lg[:, :, :], row(m[:, :]), ALU.is_lt))
                        link(nc.vector.tensor_scalar(cand[:, :, :], cand[:, :, :], 100.0, None, ALU.mult))
                        link(nc.vector.tensor_tensor(cand[:, :, :], cand[:, :, :], iota, ALU.add))
                        link(nc.vector.tensor_reduce(m2[:, :], cand[:, :, :], AX.X, ALU.min))
                        link(nc.vector.tensor_tensor(oh[:, :, :], iota, row(m2[:, :]), ALU.is_equal))

                    dve.wait_ge(s_gt, 1)
                    nc.vector.tensor_copy(gT[:, :, :], ps[:, 2, 0:DC * E].rearrange("p (c e) -> p c e", c=DC)).then_inc(s_gte, 1)
                    dve.wait_ge(s_lg, 1)
                    link(nc.vector.tensor_copy(lg[:, :, :], ps[:, 0, 0:NT * E].rearrange("p (t e) -> p t e", e=E)))
                    first_best(oh1, m1)
                    nc.vector.tensor_tensor(ex[:, :, :], lg[:, :, :], row(m1[:, :]), ALU.subtract).then_inc(s_ei, 1)
                    link(nc.vector.tensor_scalar(cand[:, :, :], oh1[:, :, :], NEG, None, ALU.mult))
                    dve.wait_ge(s_ei, 1)
                    link(nc.vector.tensor_tensor(lg[:, :, :], lg[:, :, :], cand[:, :, :], ALU.add))
                    first_best(oh2, m1)
                    nc.vector.tensor_tensor(cand[:, :, :], oh1[:, :, :], oh2[:, :, :], ALU.add).then_inc(s_sel, 1)
                    dve.wait_ge(s_ex, 1)
                    link(nc.vector.tensor_reduce(m1[:, :], ex[:, :, :], AX.X, ALU.add))
                    link(nc.vector.reciprocal(m1[:, :], m1[:, :]))
                    link(nc.vector.tensor_tensor(ex[:, :, :], ex[:, :, :], row(m1[:, :]), ALU.mult))
                    for b in range(B):
                        link(nc.vector.tensor_scalar(base[:, b * KB:(b + 1) * KB, :],
                                                     k.c("cap0").unsqueeze(1).to_broadcast([P, KB, E]),
                                                     float(b * CAP - 1), None, ALU.add))
                    dve.wait_ge(s_cum, 1)
                    link(nc.vector.tensor_copy(pos[:, :, :], ps[:, 1, 0:NT * E].rearrange("p (t e) -> p t e", e=E)))
                    link(nc.vector.tensor_scalar(keep[:, :, :], pos[:, :, :], float(CAP), None, ALU.is_le))
                    link(nc.vector.tensor_tensor(base[:, :, :], base[:, :, :], pos[:, :, :], ALU.add))
                    for c, oh in enumerate((oh1, oh2)):
                        link(nc.vector.tensor_tensor(oh[:, :, :], oh[:, :, :], keep[:, :, :], ALU.mult))
                        link(nc.vector.tensor_tensor(cw[:, :, :], oh[:, :, :], ex[:, :, :], ALU.mult))
                        link(nc.vector.tensor_reduce(wgt[:, c, :], cw[:, :, :], AX.X, ALU.add))
                        link(nc.vector.tensor_tensor(cw[:, :, :], oh[:, :, :], base[:, :, :], ALU.mult))
                        link(nc.vector.tensor_reduce(sl[:, :], cw[:, :, :], AX.X, ALU.add))
                        link(nc.vector.tensor_reduce(va[:, :], oh[:, :, :], AX.X, ALU.add))
                        link(nc.vector.tensor_copy(idx_g[:, c, :], sl[:, :]))
                        link(nc.vector.tensor_scalar(va[:, :], va[:, :], -1.0, 1.0, ALU.mult, ALU.add))
                        link(nc.vector.tensor_tensor(va[:, :], va[:, :], k.c("spare").to_broadcast([P, NT]), ALU.mult))
                        link(nc.vector.tensor_tensor(sl[:, :], sl[:, :], va[:, :], ALU.add))
                        link(nc.vector.tensor_copy(idx_s[:, c, :], sl[:, :]))
            def dispatch(pool):
                for t in range(NT):
                    for c in range(2):
                        nc.gpsimd.indirect_dma_start(
                            out=disp, out_offset=bass.IndirectOffsetOnAxis(ap=idx_s[:, c, t:t + 1], axis=0),
                            in_=xn[:, t, :], in_offset=None).then_inc(s_sc, 16)
                pool.wait_ge(s_sc, 16 * 2 * NT)
            relative_tables(k, dispatch)

        UPE = FC0 + 2
        HR = ROWS // 2
        with ExitStack() as ectx:
            xe = k.sb("xe", [P, 2, ST, D], ctx=ectx)
            xeT = k.sb("xeT", [P, 2, DC, ROWS], ctx=ectx)
            sg = k.sb("sg", [P, 2, ROWS], ctx=ectx)
            hT = k.sb("hT", [P, 2, FC0, ROWS], ctx=ectx)
            ye = k.sb("ye", [P, 2, ST, D], ctx=ectx)
            s_xe = [k.sem(f"s_xe_{j}") for j in range(2)]
            s_use, s_hT, s_xet, s_silu, s_ye, s_yst, s_yfree = (
                k.sem("s_m_" + n) for n in ("use", "hT", "xet", "silu", "ye", "yst", "yfree"))
            with nc.Block() as block:
                @block.sync
                def _(sp):
                    for e in range(E + 1):
                        j = e % 2
                        if e >= 2:
                            sp.wait_ge(s_use, UPE * (e - 3) + FC0 + 2 if e >= 3 else 1)
                        sp.dma_start(xe[:, j, :, :], disp[e * ROWS:(e + 1) * ROWS, :].rearrange("(t p) d -> p t d", p=P)).then_inc(s_xe[j], 16)
                        if e == E:
                            break
                        if e < 2:
                            continue
                        sp.wait_ge(s_use, UPE * (e - 2) + FC0 + 1)
                        sp.dma_start(w1[:, j, :, :], k.d["L0_ffn_w1"][e].rearrange("(c p) f -> p c f", p=P)).then_inc(s_w13[j], 16)
                        sp.dma_start(w3[:, j, :, :], k.d["L0_ffn_w3"][e].rearrange("(c p) f -> p c f", p=P)).then_inc(s_w13[j], 16)
                        sp.wait_ge(s_use, UPE * (e - 1) + 1)
                        sp.dma_start(w2[:, j, :, :], k.d["L0_ffn_w2"][e].rearrange("(c p) d -> p c d", p=P)).then_inc(s_w2[j], 16)

                def banks(n):
                    return 4 * (n % 2)

                @block.tensor
                def _(pe):
                    def transposes(j, n):
                        for tt in range(ST):
                            for c in range(DC):
                                q = tt * DC + c
                                last = nc.tensor.transpose(ps[:, banks(n) + q // 4, (q % 4) * P:(q % 4 + 1) * P],
                                                           xe[:, j, tt, c * P:(c + 1) * P], k.c("ident"))
                        last.then_inc(s_use, 1)

                    pe.wait_ge(s_xe[0], 16)
                    transposes(0, 0)
                    with pe.Fori(0, E // 2) as i:
                        for j in range(2):
                            n0 = UPE * j + 1
                            pe.wait_ge(s_xet, 2 * i + j + 1)
                            pe.wait_ge(s_w13[j], 32 * i + 32)
                            for f in range(FC0):
                                n = n0 + f
                                if f == 1:
                                    pe.wait_ge(s_ye, 2 * i + j + 1)
                                elif f >= 2:
                                    pe.wait_ge(s_hT, 2 * FC0 * i + FC0 * j + f - 1)
                                for w, o in ((w1, 0), (w3, 2)):
                                    for h in range(2):
                                        for c in range(DC):
                                            last = nc.tensor.matmul(ps[:, banks(n) + o + h, 0:HR], w[:, j, c, f * P:(f + 1) * P],
                                                                    xeT[:, j, c, h * HR:(h + 1) * HR],
                                                                    start=(c == 0), stop=(c == DC - 1))
                                last.then_inc(s_use, 1)
                            n = n0 + FC0
                            pe.wait_ge(s_xe[1 - j], 16 * i + 16 * (j + 1))
                            pe.wait_ge(s_hT, 2 * FC0 * i + FC0 * j + FC0 - 1)
                            transposes(1 - j, n)
                            n = n0 + FC0 + 1
                            pe.wait_ge(s_hT, 2 * FC0 * i + FC0 * j + FC0)
                            pe.wait_ge(s_w2[j], 16 * i + 16)
                            for tt in range(ST):
                                for f in range(FC0):
                                    last = nc.tensor.matmul(ps[:, banks(n) + tt // 2, (tt % 2) * D:(tt % 2 + 1) * D],
                                                            hT[:, j, f, tt * P:(tt + 1) * P], w2[:, j, f, :],
                                                            start=(f == 0), stop=(f == FC0 - 1))
                            last.then_inc(s_use, 1)

                @block.scalar
                def _(act):
                    def copy_rows(j, n, use):
                        act.wait_ge(s_use, use)
                        for q in range(3):
                            w = min(2, ST - 2 * q)
                            last = nc.scalar.activation(
                                xeT[:, j, :, 2 * q * P:(2 * q + w) * P].rearrange("p c (t n) -> p t c n", n=P),
                                ps[:, banks(n) + q, 0:w * DC * P].rearrange("p (t c n) -> p t c n", t=w, c=DC), ACT.Copy)
                        last.then_inc(s_xet, 1)

                    copy_rows(0, 0, 1)
                    with act.Fori(0, E // 2) as i:
                        for j in range(2):
                            for f in range(FC0):
                                n = UPE * j + 1 + f
                                act.wait_ge(s_use, 2 * UPE * i + n + 1)
                                nc.scalar.activation(sg[:, n % 2, :].rearrange("p (h m) -> p h m", h=2),
                                                     ps[:, banks(n):banks(n) + 2, 0:HR], ACT.Silu).then_inc(s_silu, 1)
                            n = UPE * j + 1 + FC0
                            copy_rows(1 - j, n, 2 * UPE * i + n + 1)

                @block.vector
                def _(dve):
                    dve.sem_inc(s_ye, 1)
                    with dve.Fori(0, E // 2) as i:
                        for j in range(2):
                            for f in range(FC0):
                                n = UPE * j + 1 + f
                                dve.wait_ge(s_silu, 2 * FC0 * i + FC0 * j + f + 1)
                                nc.vector.tensor_tensor(hT[:, j, f, :].rearrange("p (h m) -> p h m", h=2),
                                                        ps[:, banks(n) + 2:banks(n) + 4, 0:HR],
                                                        sg[:, n % 2, :].rearrange("p (h m) -> p h m", h=2),
                                                        ALU.mult).then_inc(s_hT, 1)
                            n = UPE * j + 2 + FC0
                            dve.wait_ge(s_use, 2 * UPE * i + n + 1)
                            dve.wait_ge(s_yfree, 2 * i + j + 1)
                            nc.vector.tensor_copy(ye[:, j, :, :], ps[:, banks(n):banks(n) + 3, :].rearrange(
                                "p a n -> p (a n)")[:, 0:ST * D].rearrange("p (t d) -> p t d", d=D)).then_inc(s_ye, 1)

                @block.gpsimd
                def _(pool):
                    pool.sem_inc(s_yfree, 2)
                    for e in range(E):
                        pool.wait_ge(s_ye, e + 2)
                        pool.dma_start(ybuf[e * ROWS:(e + 1) * ROWS, :].rearrange("(t p) d -> p t d", p=P),
                                       ye[:, e % 2, :, :]).then_inc(s_yst, 16)
                        pool.wait_ge(s_yst, 16 * (e + 1))
                        pool.sem_inc(s_yfree, 1)

        with ExitStack() as cctx:
            NB = 8
            yg = k.sb("yg", [P, NB, D], ctx=cctx)
            s_yg = [k.sem(f"s_yg{n}") for n in range(NB)]
            s_add = k.sem("s_yadd")
            with nc.Block() as block:
                @block.gpsimd
                def _(pool):
                    for n in range(2 * NT):
                        if n >= NB:
                            pool.wait_ge(s_add, n - NB + 1)
                        nc.gpsimd.indirect_dma_start(
                            out=yg[:, n % NB, :], out_offset=None, in_=ybuf,
                            in_offset=bass.IndirectOffsetOnAxis(ap=idx_g[:, n % 2, n // 2:n // 2 + 1], axis=0)).then_inc(s_yg[n % NB], 16)

                @block.vector
                def _(dve):
                    for n in range(2 * NT):
                        t = n // 2
                        dve.wait_ge(s_yg[n % NB], 16 * (n // NB + 1))
                        if n:
                            dve.wait_ge(s_add, n)
                        nc.vector.scalar_tensor_tensor(k.x[:, t, :], yg[:, n % NB, :], wgt[:, n % 2, t:t + 1], k.x[:, t, :],
                                                       ALU.mult, ALU.add).then_inc(s_add, 1)


def cross_attention1(k):
    nc, ps, xT = k.nc, k.ps, k.xT
    with ExitStack() as ctx:
        wq = k.sb("xwq", [P, DC, D], ctx=ctx)
        wkv = k.sb("xwkv", [P, DC, 2 * D], ctx=ctx)
        wqT = k.sb("xwqT", [P, DC, D], ctx=ctx)
        kT = k.sb("xkT", [P, B, DC, SC], ctx=ctx)
        aT1 = k.sb("xaT1", [P, B, DC, SC], ctx=ctx)
        v = k.sb("xv", [SC, B, D], ctx=ctx)
        mx = k.sb("xmx", [P, NT], ctx=ctx)
        sc = k.sb("xsc", [P, NT, SC], ctx=ctx)
        pT = k.sb("xpT", [SC, NT, P], ctx=ctx)
        s_w, s_t, s_te, s_k, s_ke, s_a, s_ae, s_sc, s_ch, s_ein, s_e, s_at, s_ate, s_o, s_x = (
            k.sem("s_x1_" + n) for n in ("w", "t", "te", "k", "ke", "a", "ae", "sc", "ch", "ein", "e", "at", "ate", "o", "x"))

        def rows(r):
            return r.unsqueeze(2).to_broadcast([P, NT, SC])

        def load_weights(sp):
            sp.dma_start(wq[:, :, :], k.d["L1_xattn_Wq"].rearrange("(c p) n -> p c n", p=P)).then_inc(s_w, 16)
            sp.dma_start(wkv[:, :, :], k.d["L1_xattn_Wkv"].rearrange("(c p) n -> p c n", p=P)).then_inc(s_w, 16)

        norm_transpose(k, "1b", loads=load_weights)
        with nc.Block() as block:
            @block.tensor
            def _(pe):
                pe.wait_ge(s_w, 32)
                for q in range(DC):
                    for c in range(DC):
                        last = nc.tensor.transpose(ps[:, 0, (q * DC + c) * P:(q * DC + c + 1) * P], wq[:, c, q * P:(q + 1) * P], k.c("ident"))
                last.then_inc(s_t, 1)
                for b in range(B):
                    for e in range(DC):
                        for c in range(DC):
                            nc.tensor.matmul(ps[:, 1, (b * DC + e) * P:(b * DC + e) * P + SC], wkv[:, c, e * P:(e + 1) * P],
                                             k.ctxT[:, b, c, :], start=(c == 0), stop=(c == DC - 1))
                    for c in range(DC):
                        last = nc.tensor.matmul(ps[0:SC, 2, b * D:(b + 1) * D], k.ctxT[:, b, c, :], wkv[:, c, D:2 * D],
                                                start=(c == 0), stop=(c == DC - 1))
                last.then_inc(s_k, 1)
                pe.wait_ge(s_ke, 1)
                for b in range(B):
                    for c in range(DC):
                        for e in range(DC):
                            last = nc.tensor.matmul(ps[:, 3, (b * DC + c) * P:(b * DC + c) * P + SC], wqT[:, e, c * P:(c + 1) * P],
                                                    kT[:, b, e, :], start=(e == 0), stop=(e == DC - 1))
                last.then_inc(s_a, 1)
                pe.wait_ge(s_ae, 1)
                for t in range(NT):
                    for c in range(DC):
                        last = nc.tensor.matmul(ps[:, 4 + t // 4, (t % 4) * P:(t % 4) * P + SC], xT[:, c, t * P:(t + 1) * P],
                                                aT1[:, t // KB, c, :], start=(c == 0), stop=(c == DC - 1))
                    if t % 4 == 3:
                        last.then_inc(s_sc, 1)
                pe.wait_ge(s_e, 1)
                for g in range(4):
                    for t in range(4 * g, 4 * g + 4):
                        last = nc.tensor.transpose(ps[0:SC, g, (t % 4) * P:(t % 4 + 1) * P], sc[:, t, :], k.c("ident"))
                    last.then_inc(s_at, 1)
                for t in range(NT):
                    if t % 4 == 0:
                        pe.wait_ge(s_ate, t // 4 + 1)
                    if t >= 2:
                        pe.wait_ge(s_x, t - 1)
                    nc.tensor.matmul(ps[:, 4 + t % 2, 0:D], pT[:, t, :], v[:, t // KB, :], start=True, stop=True).then_inc(s_o, 1)

            @block.scalar
            def _(act):
                act.wait_ge(s_ein, 1)
                nc.scalar.activation(sc[:, :, :], sc[:, :, :], ACT.Exp).then_inc(s_e, 1)
                for g in range(4):
                    act.wait_ge(s_at, g + 1)
                    nc.scalar.activation(pT[:, 4 * g:4 * g + 4, :], ps[0:SC, g, :].rearrange("p (t n) -> p t n", t=4),
                                         ACT.Copy).then_inc(s_ate, 1)

            @block.vector
            def _(dve):
                link = Chain(dve, s_ch)
                dve.wait_ge(s_t, 1)
                nc.vector.tensor_copy(wqT[:, :, :], ps[:, 0, :].rearrange("p (q c) -> p q c", q=DC))
                dve.wait_ge(s_k, 1)
                nc.vector.tensor_copy(v[:, :, :], ps[0:SC, 2, :].rearrange("p (b d) -> p b d", b=B))
                nc.vector.tensor_copy(kT[:, :, :, :].rearrange("p b c j -> p (b c) j"),
                                      ps[:, 1, :].rearrange("p (bc n) -> p bc n", n=P)[:, :, 0:SC]).then_inc(s_ke, 1)
                dve.wait_ge(s_a, 1)
                nc.vector.tensor_scalar(aT1[:, :, :, :].rearrange("p b c j -> p (b c) j"),
                                        ps[:, 3, :].rearrange("p (bc n) -> p bc n", n=P)[:, :, 0:SC],
                                        float(D) ** -0.5, None, ALU.mult).then_inc(s_ae, 1)
                for g in range(4):
                    dve.wait_ge(s_sc, g + 1)
                    link(nc.vector.tensor_copy(sc[:, 4 * g:4 * g + 4, :],
                                               ps[:, 4 + g, :].rearrange("p (t n) -> p t n", t=4)[:, :, 0:SC]))
                link(nc.vector.tensor_reduce(mx[:, :], sc[:, :, :], AX.X, ALU.max))
                nc.vector.tensor_tensor(sc[:, :, :], sc[:, :, :], rows(mx[:, :]), ALU.subtract).then_inc(s_ein, 1)
                dve.wait_ge(s_e, 1)
                link(nc.vector.tensor_reduce(mx[:, :], sc[:, :, :], AX.X, ALU.add))
                link(nc.vector.reciprocal(mx[:, :], mx[:, :]))
                for t in range(NT):
                    dve.wait_ge(s_o, t + 1)
                    nc.vector.scalar_tensor_tensor(k.x[:, t, :], ps[:, 4 + t % 2, 0:D], mx[:, t:t + 1], k.x[:, t, :],
                                                   ALU.mult, ALU.add).then_inc(s_x, 1)


def moe1(k):
    nc, ps, xT = k.nc, k.ps, k.xT
    T1 = NF1 // P
    FC1 = F1 // P
    LIMIT, ALPHA = 7.0, 1.702
    with ExitStack() as ctx:
        gu = k.sb("gu", [P, 2, DC, 2 * F1], ctx=ctx)
        dn = k.sb("dn", [P, 2, FC1, D], ctx=ctx)
        gub = k.sb("gub", [E, 2 * F1], ctx=ctx)
        gubT = k.sb("gubT", [P, FC1, 2, E], ctx=ctx)
        dnb = k.sb("dnb", [1, E, D], ctx=ctx)
        idx = k.sb("ridx", [P, T1, 2], I32, ctx=ctx)
        idf = k.sb("ridf", [P, T1, 2], ctx=ctx)
        rw = k.sb("rw", [P, T1, E], ctx=ctx)
        cw = k.sb("rcw", [P, T1, E], ctx=ctx)
        oh = k.sb("roh", [P, T1, E], ctx=ctx)
        g1 = k.sb("g1", [P, NF1], ctx=ctx)
        sg = k.sb("sg1", [P, NF1], ctx=ctx)
        u1 = k.sb("u1", [P, NF1], ctx=ctx)
        hT = k.sb("hT1", [P, 2, FC1, NF1], ctx=ctx)
        s_in, s_bt, s_bte, s_ch, s_gu, s_g1, s_sg, s_hT, s_dn, s_acc = (
            k.sem("s_m1_" + n) for n in ("in", "bt", "bte", "ch", "gu", "g1", "sg", "hT", "dn", "acc"))
        s_rest = k.sem("s_rest")
        s_wgu = [k.sem(f"s_wgu{j}") for j in range(2)]
        s_wdn = [k.sem(f"s_wdn{j}") for j in range(2)]
        def load_gate_up(sp, e):
            sp.dma_start(gu[:, e % 2, :, :], k.d["L1_ffn_gate_up_proj"][e].rearrange("(c p) f -> p c f", p=P)).then_inc(s_wgu[e % 2], 16)

        def load_down(sp, e):
            sp.dma_start(dn[:, e % 2, :, :], k.d["L1_ffn_down_proj"][e].rearrange("(c p) d -> p c d", p=P)).then_inc(s_wdn[e % 2], 16)

        def load_first(sp):
            sp.dma_start(gub[:, :], k.d["L1_ffn_gate_up_proj_bias"]).then_inc(s_in, 16)
            sp.dma_start(dnb[:, :, :], k.d["L1_ffn_down_proj_bias"].rearrange("(a e) d -> a e d", a=1)).then_inc(s_in, 16)
            sp.dma_start(idx[:, :, :], k.d["L1_ffn_router_indices"].rearrange("(t p) k -> p t k", p=P)).then_inc(s_in, 16)
            sp.dma_start(rw[:, :, :], k.d["L1_ffn_routing_weights"].rearrange("(t p) e -> p t e", p=P)).then_inc(s_in, 16)
            for e in range(2):
                load_gate_up(sp, e)
                load_down(sp, e)

        norm_transpose(k, "1c", tiles=T1, loads=load_first)
        with nc.Block() as block:
            @block.sync
            def _(sp):
                for e in range(2, E):
                    sp.wait_ge(s_gu, FC1 * (e - 1))
                    load_gate_up(sp, e)
                    sp.wait_ge(s_dn, e - 1)
                    load_down(sp, e)
                sp.dma_start(k.d["out"].rearrange("b (t p) d -> p (b t) d", p=P)[:, T1:NT, :], k.x[:, T1:NT, :]).then_inc(s_rest, 16)
                sp.wait_ge(s_rest, 16)

            @block.tensor
            def _(pe):
                pe.wait_ge(s_in, 64)
                for c in range(FC1):
                    for z in range(2):
                        o = c * 2 * P + z
                        last = nc.tensor.transpose(ps[:, 7, (2 * c + z) * E:(2 * c + z + 1) * E], gub[:, o:o + 2 * P - 1:2],
                                                   k.c("ident", E)[:, 0:E])
                last.then_inc(s_bt, 1)

                def gate_up(j, e, i):
                    pe.wait_ge(s_wgu[j], 16 * i + 16)
                    for c in range(FC1):
                        pe.wait_ge(s_hT, FC1 * e + c + 1)
                        for z in range(2):
                            o = c * 2 * P + z
                            for q in range(DC):
                                last = nc.tensor.matmul(ps[:, 2 * c + z, :], gu[:, j, q, o:o + 2 * P - 1:2], xT[:, q, 0:NF1],
                                                        start=(q == 0), stop=(q == DC - 1))
                        last.then_inc(s_gu, 1)

                def down(j, e, i, bias):
                    pe.wait_ge(s_wdn[j], 16 * i + 16)
                    pe.wait_ge(s_hT, FC1 * e + 4)
                    pe.wait_ge(s_acc, T1 * e + 4)
                    for t in range(T1):
                        for c in range(FC1):
                            nc.tensor.matmul(ps[:, 4 + t // 2, (t % 2) * D:(t % 2 + 1) * D], hT[:, j, c, t * P:(t + 1) * P],
                                             dn[:, j, c, :], start=(c == 0), stop=False)
                        last = nc.tensor.matmul(ps[:, 4 + t // 2, (t % 2) * D:(t % 2 + 1) * D], k.c("ones", 1), bias,
                                                start=False, stop=True)
                    last.then_inc(s_dn, 1)

                gate_up(0, 0, 0)
                with pe.Fori(0, E // 2 - 1) as i:
                    for j in range(2):
                        e = 2 * i + j
                        gate_up(1 - j, e + 1, i + j)
                        down(j, e, i, dnb[:, bass.ds(e, 1), :].rearrange("p a d -> p (a d)"))
                gate_up(1, E - 1, E // 2 - 1)
                down(0, E - 2, E // 2 - 1, dnb[:, E - 2, :])
                down(1, E - 1, E // 2 - 1, dnb[:, E - 1, :])

            @block.scalar
            def _(act):
                with act.Fori(0, FC1 * E) as n:
                    act.wait_ge(s_g1, n + 1)
                    nc.scalar.activation(sg[:, :], g1[:, :], ACT.Sigmoid, scale=ALPHA).then_inc(s_sg, 1)

            @block.vector
            def _(dve):
                link = Chain(dve, s_ch)
                dve.sem_inc(s_hT, 2)
                dve.sem_inc(s_acc, 4)
                dve.wait_ge(s_in, 64)
                iota = k.c("iota8").unsqueeze(1).to_broadcast([P, T1, E])
                link(nc.vector.tensor_copy(idf[:, :, :], idx[:, :, :]))
                link(nc.vector.tensor_tensor(cw[:, :, :], iota, idf[:, :, 0:1].to_broadcast([P, T1, E]), ALU.is_equal))
                link(nc.vector.tensor_tensor(oh[:, :, :], iota, idf[:, :, 1:2].to_broadcast([P, T1, E]), ALU.is_equal))
                link(nc.vector.tensor_tensor(cw[:, :, :], cw[:, :, :], oh[:, :, :], ALU.add))
                link(nc.vector.tensor_tensor(cw[:, :, :], cw[:, :, :], rw[:, :, :], ALU.mult))
                dve.wait_ge(s_bt, 1)
                link(nc.vector.tensor_copy(gubT[:, :, :, :].rearrange("p c z e -> p (c z e)"), ps[:, 7, 0:2 * FC1 * E]))

                for e in range(E + 1):
                    if e < E:
                        for c in range(FC1):
                            dve.wait_ge(s_gu, FC1 * e + c + 1)
                            nc.vector.tensor_scalar(g1[:, :], ps[:, 2 * c, :], gubT[:, c, 0, e:e + 1], LIMIT,
                                                    ALU.add, ALU.min).then_inc(s_g1, 1)
                            link(nc.vector.tensor_scalar(u1[:, :], ps[:, 2 * c + 1, :], gubT[:, c, 1, e:e + 1], LIMIT,
                                                         ALU.add, ALU.min))
                            link(nc.vector.tensor_scalar(u1[:, :], u1[:, :], -LIMIT, 1.0, ALU.max, ALU.add))
                            dve.wait_ge(s_sg, FC1 * e + c + 1)
                            link(nc.vector.tensor_tensor(sg[:, :], g1[:, :], sg[:, :], ALU.mult))
                            nc.vector.tensor_tensor(hT[:, e % 2, c, :], u1[:, :], sg[:, :], ALU.mult).then_inc(s_hT, 1)
                            dve.wait_ge(s_hT, FC1 * e + c + 3)
                    if e:
                        dve.wait_ge(s_dn, e)
                        for t in range(T1):
                            nc.vector.scalar_tensor_tensor(k.x[:, t, :], ps[:, 4 + t // 2, (t % 2) * D:(t % 2 + 1) * D],
                                                           cw[:, t, e - 1:e], k.x[:, t, :], ALU.mult, ALU.add).then_inc(s_acc, 1)


def store(k):
    nc = k.nc
    s_out = k.sem("s_out")
    with nc.Block() as block:
        @block.sync
        def _(sp):
            sp.dma_start(k.d["out"].rearrange("b (t p) d -> p (b t) d", p=P)[:, 0:NF1 // P, :], k.x[:, 0:NF1 // P, :]).then_inc(s_out, 16)
            sp.wait_ge(s_out, 16)


def decoder(nc, dram):
    with ExitStack() as ctx:
        k = Prog(nc, ctx, dram)
        context_prep(k)
        norm_rms_transpose(k, "0a")
        attention(k, "0", rel=False)
        k.end_stage()
        norm_transpose(k, "0b")
        cross_attention0(k)
        k.end_stage()
        moe0(k)
        k.end_stage()
        attention(k, "1", rel=True)
        k.end_stage()
        cross_attention1(k)
        k.end_stage()
        moe1(k)
        store(k)


_INS = ['x', 'ctx_1024', 'L0_attn_w_q', 'L0_attn_w_k', 'L0_attn_w_v', 'L0_attn_w_o', 'L0_attn_norm_w',
        'L0_xattn_W_a', 'L0_xattn_W_p', 'L0_xattn_V_p', 'L0_ffn_gate_w', 'L0_ffn_w1', 'L0_ffn_w2', 'L0_ffn_w3',
        'L1_attn_W_qkv', 'L1_attn_b_qkv', 'L1_attn_W_out', 'L1_attn_b_out', 'L1_attn_rel_emb_k',
        'L1_attn_rel_emb_v', 'L1_xattn_Wq', 'L1_xattn_Wkv', 'L1_ffn_router_indices', 'L1_ffn_routing_weights',
        'L1_ffn_gate_up_proj', 'L1_ffn_gate_up_proj_bias', 'L1_ffn_down_proj', 'L1_ffn_down_proj_bias']


def shape_constants():
    import numpy as np
    c = np.zeros((P, CW), np.float32)

    def put(name, a):
        lo, hi = Consts.at(name)
        c[:a.shape[0], lo:hi] = a
    p = np.arange(P)[:, None]
    put("ident", np.eye(P))
    put("causal", np.where(np.arange(P)[None, :] <= p, 0.0, NEG))
    put("late", (p + np.arange(P)[None, :] >= P))
    put("tri", (p <= np.arange(P)[None, :]))
    put("ones", np.ones((P, P)))
    put("iota8", np.arange(E)[None, :] + 0 * p)
    put("iota77", np.arange(SC)[None, :] + 0 * p)
    put("cap0", np.arange(E)[None, :] * 2 * CAP + 0 * p)
    put("spare", E * 2 * CAP + p)
    f = np.float32
    d = np.arange(HD)
    theta = np.power(f(10000.0), f(-2.0) * (d // 2).astype(f) / f(HD)).astype(f)
    pos = np.arange(S, dtype=f)
    ang = (pos[:, None] * theta[None, :]).astype(f)
    rf = np.cos(ang) + np.sin(ang) * np.where(np.arange(S) % 2 == 0, f(-1.0), f(1.0))[:, None]
    put("rope", np.tile(rf.T.astype(f), (8, 1)))
    return c


def kernel(**inputs):
    import numpy as np
    import concourse.bacc as bacc
    from concourse.bass_utils import run_bass_kernel_spmd

    nc = bacc.Bacc("TRN2", target_bir_lowering=False, num_devices=1)
    arrays, dram = {}, {}
    for name in _INS:
        a = np.ascontiguousarray(inputs[name])
        arrays[f"in_{name}"] = a
        dram[name] = nc.dram_tensor(f"in_{name}", a.shape, mybir.dt.from_np(a.dtype), kind="ExternalInput").ap()
    arrays["in_consts"] = shape_constants()
    dram["consts"] = nc.dram_tensor("in_consts", (P, CW), F32, kind="ExternalInput").ap()
    dram["out"] = nc.dram_tensor("out_0", (B, S, D), F32, kind="ExternalOutput").ap()
    decoder(nc, dram)
    r = run_bass_kernel_spmd(nc, [arrays], core_ids=[0])
    return r.results[0]["out_0"]
```
